# Optimizing a Trainium2 kernel written in Bass

```python
import numpy as np
import jax
import jax.numpy as jnp

def _softmax(x, axis=-1):
    return jax.nn.softmax(x, axis=axis)

def _gelu(x):
    return jax.nn.gelu(x, approximate=True)

def _silu(x):
    return jax.nn.silu(x)

def _sigmoid(x):
    return jax.nn.sigmoid(x)

def _layernorm(x, axis=-1, eps=1e-05):
    m = jnp.mean(x, axis=axis, keepdims=True)
    v = jnp.var(x, axis=axis, keepdims=True)
    return (x - m) / jnp.sqrt(v + eps)

def _scatter_add(tgt, idx, src, axis=0):
    return tgt.at[idx].add(src)

def _segment_sum(src, seg, n):
    return jax.ops.segment_sum(src, seg, n)
kernel_name = 'mk_decoder_postln_d1_seqx_r8_ff77a2'

def setup_inputs(seed: int=0):
    np.random.seed(seed)
    _w = jnp.asarray

    def _rec_inputs():
        import jax
        import jax.numpy as jnp
        _rk = jax.random.key(seed)
        x = -0.0005146 + 1 * jax.random.normal(jax.random.fold_in(_rk, 1), (128, 64, 128), jnp.float32)
        _lenS = 64 - jax.random.randint(jax.random.fold_in(_rk, 7), (128,), 0, max(1, 64 // 4) + 1, jnp.int32)
        _lenS2 = 64 - jax.random.randint(jax.random.fold_in(_rk, 8), (128,), 0, max(1, 64 // 4) + 1, jnp.int32)
        _ctx_1024P = jax.random.normal(jax.random.fold_in(_rk, 11), (128, 16, 128), jnp.float32)
        _ctx_1024c = jax.random.dirichlet(jax.random.fold_in(_rk, 511), 0.3 * jnp.ones((16,), jnp.float32), (128, 64))
        _ctx_1024t = jnp.einsum('bsk,bkd->bsd', _ctx_1024c, _ctx_1024P)
        _ctx_1024t = _ctx_1024t * jax.lax.rsqrt(jnp.mean(jnp.square(_ctx_1024t)) + 1e-12) * 0.953939
        ctx_1024 = -0.000392918 + 0.999932 * (_ctx_1024t + 0.3 * jax.random.normal(jax.random.fold_in(_rk, 611), (128, 64, 128), jnp.float32))
        return (x, ctx_1024)
    x, ctx_1024 = _rec_inputs()

    def _L0_attn_setup():
        import jax, jax.numpy as jnp
        import numpy as np
        D = 128
        ROT = D // 2
        B, S = (4, 1024)

        def _l2norm(x, eps=1e-06):
            return x * jax.lax.rsqrt(jnp.sum(x * x, axis=-1, keepdims=True) + eps)

        def _rotary(x, rot_dim):
            seq = x.shape[-2]
            half = rot_dim // 2
            inv_freq = 1.0 / 10000.0 ** (jnp.arange(0, rot_dim, 2, dtype=jnp.float32) / rot_dim)
            freqs = jnp.arange(seq, dtype=jnp.float32)[:, None] * inv_freq[None, :]
            freqs = jnp.repeat(freqs, 2, axis=-1)
            cos, sin = (jnp.cos(freqs), jnp.sin(freqs))
            xr, xp = (x[..., :rot_dim], x[..., rot_dim:])
            x2 = xr.reshape(*xr.shape[:-1], half, 2)
            rh = jnp.stack([-x2[..., 1], x2[..., 0]], axis=-1).reshape(xr.shape)
            return jnp.concatenate([xr * cos + rh * sin, xp], axis=-1)

        def _layernorm(x, g, b, eps=1e-05):
            mu = jnp.mean(x, axis=-1, keepdims=True)
            var = jnp.mean(jnp.square(x - mu), axis=-1, keepdims=True)
            return (x - mu) * jax.lax.rsqrt(var + eps) * g + b
        key = jax.random.key(seed)
        k1, k2, k3 = jax.random.split(key, 3)
        X = jax.random.normal(k1, (B, S, D), jnp.float32)
        W_in = jax.random.normal(k2, (3 * D, D), jnp.float32) / np.float32(np.sqrt(D))
        W_out = jax.random.normal(k3, (D, D), jnp.float32) / np.float32(np.sqrt(D))
        ln_g = jnp.ones((D,), jnp.float32)
        ln_b = jnp.zeros((D,), jnp.float32)
        return {'X': X, 'W_in': W_in, 'W_out': W_out, 'ln_g': ln_g, 'ln_b': ln_b}
    _L0_attn_all = _L0_attn_setup()
    _L0_attn_in = {k: v for k, v in _L0_attn_all.items() if k in ('W_in', 'W_out', 'ln_g', 'ln_b')}
    del _L0_attn_all

    def _L0_xattn_setup():
        import jax, jax.numpy as jnp
        import numpy as np
        DIM = 128
        DIM_HEAD = 64
        HEADS = 16
        INNER = DIM_HEAD * HEADS
        EPS = 1e-05

        def layer_norm(x, g, b):
            m = jnp.mean(x, axis=-1, keepdims=True)
            v = jnp.mean(jnp.square(x - m), axis=-1, keepdims=True)
            return (x - m) * jax.lax.rsqrt(v + EPS) * g + b
        key = jax.random.key(seed)
        ks = jax.random.split(key, 8)
        B, N_IMG, N_LAT = (4, 512, 64)
        std = 1.0 / np.sqrt(DIM)
        return {'image_embeds': jax.random.normal(ks[0], (B, N_IMG, DIM), dtype=jnp.float32), 'latents': jax.random.normal(ks[1], (B, N_LAT, DIM), dtype=jnp.float32), 'ln1_g': jnp.ones((DIM,), jnp.float32), 'ln1_b': jnp.zeros((DIM,), jnp.float32), 'ln2_g': jnp.ones((DIM,), jnp.float32), 'ln2_b': jnp.zeros((DIM,), jnp.float32), 'Wq': jax.random.normal(ks[2], (DIM, INNER), dtype=jnp.float32) * std, 'Wkv': jax.random.normal(ks[3], (DIM, 2 * INNER), dtype=jnp.float32) * std, 'Wo': jax.random.normal(ks[4], (INNER, DIM), dtype=jnp.float32) * std}
    _L0_xattn_all = _L0_xattn_setup()
    _L0_xattn_in = {k: v for k, v in _L0_xattn_all.items() if k in ('ln1_g', 'ln1_b', 'ln2_g', 'ln2_b', 'Wq', 'Wkv', 'Wo')}
    del _L0_xattn_all

    def _L0_ffn_setup():
        import jax, jax.numpy as jnp
        import numpy as np
        D_MODEL = 128
        D_FF = 512
        N_EXPERTS = 8
        TOP_K = 2
        key = jax.random.key(seed)
        ks = jax.random.split(key, 8)
        s = 1.0 / np.sqrt(D_MODEL)
        sf = 1.0 / np.sqrt(D_FF)
        return {'x': jax.random.normal(ks[0], (4, 128, D_MODEL), dtype=jnp.float32), 'W1': jax.random.uniform(ks[1], (N_EXPERTS, D_MODEL, D_FF), jnp.float32, -s, s), 'b1': jax.random.uniform(ks[2], (N_EXPERTS, D_FF), jnp.float32, -s, s), 'W2': jax.random.uniform(ks[3], (N_EXPERTS, D_FF, D_MODEL), jnp.float32, -sf, sf), 'b2': jax.random.uniform(ks[4], (N_EXPERTS, D_MODEL), jnp.float32, -sf, sf), 'Wg': jax.random.uniform(ks[5], (D_MODEL, N_EXPERTS), jnp.float32, -s, s), 'bg': jax.random.uniform(ks[6], (N_EXPERTS,), jnp.float32, -s, s)}
    _L0_ffn_all = _L0_ffn_setup()
    _L0_ffn_in = {k: v for k, v in _L0_ffn_all.items() if k in ('W1', 'b1', 'W2', 'b2', 'Wg', 'bg')}
    del _L0_ffn_all
    return {'x': x, 'ctx_1024': ctx_1024, 'L0_attn_W_in': _L0_attn_in['W_in'], 'L0_attn_W_out': _L0_attn_in['W_out'], 'L0_attn_ln_g': _L0_attn_in['ln_g'], 'L0_attn_ln_b': _L0_attn_in['ln_b'], 'L0_xattn_ln1_g': _L0_xattn_in['ln1_g'], 'L0_xattn_ln1_b': _L0_xattn_in['ln1_b'], 'L0_xattn_ln2_g': _L0_xattn_in['ln2_g'], 'L0_xattn_ln2_b': _L0_xattn_in['ln2_b'], 'L0_xattn_Wq': _L0_xattn_in['Wq'], 'L0_xattn_Wkv': _L0_xattn_in['Wkv'], 'L0_xattn_Wo': _L0_xattn_in['Wo'], 'L0_ffn_W1': _L0_ffn_in['W1'], 'L0_ffn_b1': _L0_ffn_in['b1'], 'L0_ffn_W2': _L0_ffn_in['W2'], 'L0_ffn_b2': _L0_ffn_in['b2'], 'L0_ffn_Wg': _L0_ffn_in['Wg'], 'L0_ffn_bg': _L0_ffn_in['bg']}

def reference(x, ctx_1024, L0_attn_W_in, L0_attn_W_out, L0_attn_ln_g, L0_attn_ln_b, L0_xattn_ln1_g, L0_xattn_ln1_b, L0_xattn_ln2_g, L0_xattn_ln2_b, L0_xattn_Wq, L0_xattn_Wkv, L0_xattn_Wo, L0_ffn_W1, L0_ffn_b1, L0_ffn_W2, L0_ffn_b2, L0_ffn_Wg, L0_ffn_bg):
    import jax
    import jax.numpy as jnp

    def _L0_attn_ref(X, W_in, W_out, ln_g, ln_b):
        import jax, jax.numpy as jnp
        import numpy as np
        D = 128
        ROT = D // 2
        B, S = (4, 1024)

        def _l2norm(x, eps=1e-06):
            return x * jax.lax.rsqrt(jnp.sum(x * x, axis=-1, keepdims=True) + eps)

        def _rotary(x, rot_dim):
            seq = x.shape[-2]
            half = rot_dim // 2
            inv_freq = 1.0 / 10000.0 ** (jnp.arange(0, rot_dim, 2, dtype=jnp.float32) / rot_dim)
            freqs = jnp.arange(seq, dtype=jnp.float32)[:, None] * inv_freq[None, :]
            freqs = jnp.repeat(freqs, 2, axis=-1)
            cos, sin = (jnp.cos(freqs), jnp.sin(freqs))
            xr, xp = (x[..., :rot_dim], x[..., rot_dim:])
            x2 = xr.reshape(*xr.shape[:-1], half, 2)
            rh = jnp.stack([-x2[..., 1], x2[..., 0]], axis=-1).reshape(xr.shape)
            return jnp.concatenate([xr * cos + rh * sin, xp], axis=-1)

        def _layernorm(x, g, b, eps=1e-05):
            mu = jnp.mean(x, axis=-1, keepdims=True)
            var = jnp.mean(jnp.square(x - mu), axis=-1, keepdims=True)
            return (x - mu) * jax.lax.rsqrt(var + eps) * g + b
        Xn = _layernorm(X, ln_g, ln_b)
        QKV = jnp.einsum('bsd,ed->bse', Xn, W_in)
        Q, K, V = jnp.split(QKV, 3, axis=-1)
        Q = _rotary(Q, ROT)
        K = _rotary(K, ROT)
        A = jnp.sum(_l2norm(K) * V, axis=-2)
        Y = A[:, None, :] * _l2norm(Q)
        Y = jnp.einsum('bsd,ed->bse', Y, W_out)
        return Y + X

    def _L0_xattn_ref(image_embeds, latents, ln1_g, ln1_b, ln2_g, ln2_b, Wq, Wkv, Wo):
        import jax, jax.numpy as jnp
        import numpy as np
        DIM = 128
        DIM_HEAD = 64
        HEADS = 16
        INNER = DIM_HEAD * HEADS
        EPS = 1e-05

        def layer_norm(x, g, b):
            m = jnp.mean(x, axis=-1, keepdims=True)
            v = jnp.mean(jnp.square(x - m), axis=-1, keepdims=True)
            return (x - m) * jax.lax.rsqrt(v + EPS) * g + b
        B, S_lat, _ = latents.shape
        x = layer_norm(image_embeds, ln1_g, ln1_b)
        l = layer_norm(latents, ln2_g, ln2_b)
        q = l @ Wq
        kv_in = jnp.concatenate([x, l], axis=1)
        kv = kv_in @ Wkv
        k, v = jnp.split(kv, 2, axis=-1)

        def to_heads(t):
            return t.reshape(t.shape[0], t.shape[1], HEADS, DIM_HEAD).transpose(0, 2, 1, 3)
        q, k, v = (to_heads(q), to_heads(k), to_heads(v))
        scale = 1.0 / np.sqrt(np.sqrt(DIM_HEAD))
        w = jnp.einsum('bhqd,bhkd->bhqk', q * scale, k * scale)
        w = jax.nn.softmax(w.astype(jnp.float32), axis=-1).astype(q.dtype)
        out = jnp.einsum('bhqk,bhkd->bhqd', w, v)
        out = out.transpose(0, 2, 1, 3).reshape(B, S_lat, INNER)
        return out @ Wo

    def _L0_ffn_ref(x, W1, b1, W2, b2, Wg, bg):
        import jax, jax.numpy as jnp
        import numpy as np
        D_MODEL = 128
        D_FF = 512
        N_EXPERTS = 8
        TOP_K = 2
        logits = jnp.einsum('bsd,de->bse', x, Wg) + bg
        probs = jax.nn.softmax(logits, axis=-1)
        topk_vals, topk_idx = jax.lax.top_k(probs, TOP_K)
        mask = jax.nn.one_hot(topk_idx, N_EXPERTS, dtype=probs.dtype).sum(axis=-2)
        probs = probs * mask
        denom = probs.sum(axis=-1, keepdims=True)
        denom = denom + (denom == 0).astype(probs.dtype)
        probs = probs / denom
        h = jnp.einsum('bsd,edf->besf', x, W1) + b1[None, :, None, :]
        h = jax.nn.gelu(h, approximate=False)
        y = jnp.einsum('besf,efd->besd', h, W2) + b2[None, :, None, :]
        out = jnp.einsum('bse,besd->bsd', probs, y)
        return out
    x = _layernorm(x + _L0_attn_ref(x, L0_attn_W_in, L0_attn_W_out, L0_attn_ln_g, L0_attn_ln_b), axis=-1)
    x = _layernorm(x + _L0_xattn_ref(ctx_1024, x, L0_xattn_ln1_g, L0_xattn_ln1_b, L0_xattn_ln2_g, L0_xattn_ln2_b, L0_xattn_Wq, L0_xattn_Wkv, L0_xattn_Wo), axis=-1)
    x = _layernorm(x + _L0_ffn_ref(x, L0_ffn_W1, L0_ffn_b1, L0_ffn_W2, L0_ffn_b2, L0_ffn_Wg, L0_ffn_bg), axis=-1)
    return x

_drawn_inputs = setup_inputs


def setup_inputs(seed=0):
    import zlib

    import numpy as np

    out = dict(_drawn_inputs(seed))
    spreads = {'L0_attn_ln_g': (1.0, 0.6),
     'L0_attn_ln_b': (0.0, 0.603),
     'L0_xattn_ln1_g': (1.0, 0.2),
     'L0_xattn_ln1_b': (0.0, 0.1),
     'L0_xattn_ln2_g': (1.0, 0.2),
     'L0_xattn_ln2_b': (0.0, 0.1)}
    factors = {'L0_ffn_b1': 4.262, 'L0_ffn_b2': 3.173}
    for name, (base, spread) in spreads.items():
        noise = np.random.default_rng([zlib.crc32(name.encode()), seed]).standard_normal(out[name].shape)
        drawn = base * np.exp(spread * noise) if base else spread * noise
        out[name] = jnp.asarray(drawn.astype(out[name].dtype))
    for name, factor in factors.items():
        out[name] = (out[name] * factor).astype(out[name].dtype)
    return out
```

```python
import concourse.bass as bass
from concourse import mybir
from contextlib import ExitStack


FFN_ROWS = 256


def ffn_tiles(tokens, experts):
    most = (2 * tokens + experts * (FFN_ROWS - 1)) // FFN_ROWS
    return most + most % 2


def decoder_layer(nc, x, ctx_in, w_in, w_out, ln_g, ln_b, ln1_g, ln1_b, ln2_g, ln2_b,
                  w_q, w_kv, w_o, w1, b1, w2, b2, w_g, b_g, rot_cos, rot_sin, batch_of, eye,
                  before, expert_ids, region_base, row_ids, tile_ids, x_rows, y_rows, out):
    F32 = mybir.dt.float32
    I32 = mybir.dt.int32
    U32 = mybir.dt.uint32
    ALU = mybir.AluOpType
    ACT = mybir.ActivationFunctionType
    AX = mybir.AxisListType

    B, S, D = x.shape
    P = 128
    BT = P // S
    NT = B // BT
    HD = 64
    H = w_q.shape[1] // HD
    HH = H // 2
    UP = HH // BT
    UNITS = 4
    ROT = D // 2
    EPS_LN, EPS_L2 = 1e-5, 1e-6
    N = B * S
    E, F = w1.shape[0], w1.shape[2]
    FC = F // P
    T = FFN_ROWS
    TB = T // P
    CAP = N + T
    NF = ffn_tiles(N, E)
    ROW = D + 2
    ZT = 4
    NZ = NT // ZT
    QS_SCALE = 1.0 / HD ** 0.5

    x_t = x.rearrange("(t b) s d -> t (b s) d", b=BT)
    ctx_t = ctx_in.rearrange("(t b) s d -> t b s d", b=BT)
    out_z = out.rearrange("(t b) s d -> t (b s) d", b=BT)

    ctx = ExitStack()
    with ctx:
        def sb(name, shape, dt=F32):
            return ctx.enter_context(nc.sbuf_tensor(name, shape, dt))

        def pb(name):
            return ctx.enter_context(nc.psum_tensor(name, [P, 512], F32))

        def sem(name):
            return ctx.enter_context(nc.semaphore(name))

        ident = sb("ident", [P, P])
        cosb = sb("cosb", [P, ROT])
        sinb = sb("sinb", [P, ROT])
        member = sb("member", [P, BT])
        m_half = sb("m_half", [P, ZT])
        gcol = sb("gcol", [P, 1])
        bcol = sb("bcol", [P, 1])
        g_ctx = sb("g_ctx", [P, D])
        b_ctx = sb("b_ctx", [P, D])
        g_lat = sb("g_lat", [P, D])
        b_lat = sb("b_lat", [P, D])
        winT = sb("winT", [P, 3 * D])
        woutT = sb("woutT", [P, D])
        score_w = sb("score_w", [P, H, D])
        value_w = sb("value_w", [P, H, D])
        win_raw = sb("win_raw", [P, 3, D])
        wout_raw = sb("wout_raw", [P, D])
        wq_raw = sb("wq_raw", [P, H * HD])
        wkv_raw = sb("wkv_raw", [P, 2 * H * HD])
        wo_raw = sb("wo_raw", [P, H // 2, D])
        wqT = sb("wqT", [P, H // 2, D])
        wkT = sb("wkT", [P, H // 2, D])
        wvT = sb("wvT", [P, H // 2, D])

        x_raw = sb("x_raw", [P, 2, D])
        c_raw = sb("c_raw", [P, 2, D])
        st_in = sb("st_in", [P, 2, 2, 6])
        mv_in = sb("mv_in", [P, 2, 2, 2])
        ve_in = sb("ve_in", [P, 2, 2])
        rs_in = sb("rs_in", [P, 2, 2])
        x_hat = sb("x_hat", [P, 2, D])
        c_hat = sb("c_hat", [P, 2, D])
        xnT = sb("xnT", [P, 2, D])
        qkv = sb("qkv", [P, 2, 3 * D])
        sq_junk = sb("sq_junk", [P, 2, D])
        ss_qk = sb("ss_qk", [P, 2, 2])
        se_qk = sb("se_qk", [P, 2, 2])
        rs_qk = sb("rs_qk", [P, 2, 2])
        turned = sb("turned", [P, 2, 2, ROT])
        kv_prod = sb("kv_prod", [P, 2, D])
        k_pick = sb("k_pick", [P, 2, BT])
        yT = sb("yT", [P, 2, P])
        attn_o = sb("attn_o", [P, 2, D])
        z1 = sb("z1", [P, 2, D])
        st_z1 = sb("st_z1", [P, 2, 6])
        mv_z1 = sb("mv_z1", [P, 2, 2])
        ve_z1 = sb("ve_z1", [P, 2, 1])
        rs_z1 = sb("rs_z1", [P, 2, 1])
        st_x1 = sb("st_x1", [P, 2, 6])
        mv_x1 = sb("mv_x1", [P, 2, 2])
        ve_x1 = sb("ve_x1", [P, 2, 1])
        rs_x1 = sb("rs_x1", [P, 2, 1])
        l_hat = sb("l_hat", [P, 2, D])
        l_scaled = sb("l_scaled", [P, 2, D])
        c_scaled = sb("c_scaled", [P, 2, D])
        l_rows = sb("l_rows", [P, 2, D])
        c_rows = sb("c_rows", [P, 2, D])
        kv_rows = sb("kv_rows", [P, 2, BT, D])
        kvT = sb("kvT", [P, 2, 4, S])
        u_sb = sb("u_sb", [P, 2, BT, H, S])
        tT = sb("tT", [P, 2, H, P])
        z2 = sb("z2", [P, 2, D])
        st_z2 = sb("st_z2", [P, 2, 6])
        mv_z2 = sb("mv_z2", [P, 2, 2])
        ve_z2 = sb("ve_z2", [P, 2, 1])
        rs_z2 = sb("rs_z2", [P, 2, 1])
        neg_max = sb("neg_max", [P, 2, UP])
        probs = sb("probs", [P, 2, UP, P])
        sums = sb("sums", [P, 2, UP])
        inv_sum = sb("inv_sum", [P, 2, UP])
        probs_n = sb("probs_n", [P, 2, UP, P])
        pT = sb("pT", [P, 2, UP * P])
        x2s = sb("x2s", [P, 2, D])
        x2T = sb("x2T", [P, 2, P])
        wg_sb = sb("wg_sb", [P, E])
        bg_sb = sb("bg_sb", [P, E])
        tri = sb("tri", [P, P])
        ones = sb("ones", [P, P])
        eids = sb("eids", [P, E])
        rbase = sb("rbase", [P, E])
        rids = sb("rids", [P, NT, 2], I32)
        tids = sb("tids", [1, NF])
        logits = sb("logits", [P, 2, E])
        lmax = sb("lmax", [P, 2, 1])
        gexp = sb("gexp", [P, 2, E])
        gsum = sb("gsum", [P, 2, 1])
        ginv = sb("ginv", [P, 2, 1])
        gprob = sb("gprob", [P, 2, E])
        top = sb("top", [P, 2, 8])
        top_at = sb("top_at", [P, 2, 8], U32)
        top_atf = sb("top_atf", [P, 2, 2])
        den = sb("den", [P, 2, 1])
        den_g = sb("den_g", [P, 2, 1])
        den_i = sb("den_i", [P, 2, 1])
        picked = sb("picked", [P, 2, 2, E])
        mask = sb("mask", [P, 2, E])
        seen = sb("seen", [P, 2, E])
        pos_all = sb("pos_all", [P, 2, E])
        pos_sel = sb("pos_sel", [P, 2, 2, E])
        pos_f = sb("pos_f", [P, 2, 2])
        pos_i = sb("pos_i", [P, 2, 2], I32)
        routed = sb("routed", [P, 2, 2, ROW])
        pad_row = sb("pad_row", [P, ROW])
        b1_raw = sb("b1_raw", [E * FC, P])
        b1_all = sb("b1_all", [P, E * FC])
        rows = sb("rows", [P, NT, D])

        cnt_up = sb("cnt_up", [1, E])
        cnt_i = sb("cnt_i", [1, E], I32)
        nt_i = sb("nt_i", [1, E], I32)
        nt_f = sb("nt_f", [1, E])
        cum_nt = sb("cum_nt", [1, E])
        pad_f = sb("pad_f", [1, E])
        pad_i = sb("pad_i", [1, E], I32)
        past = sb("past", [1, NF, E])
        past_nt = sb("past_nt", [1, NF, E])
        ex_f = sb("ex_f", [1, NF])
        start_f = sb("start_f", [1, NF])
        valid_f = sb("valid_f", [1, NF])
        blk_f = sb("blk_f", [1, NF])
        blk_v = sb("blk_v", [1, NF])
        base_f = sb("base_f", [1, NF])
        exw_f = sb("exw_f", [1, NF])
        base_i = sb("base_i", [1, NF], I32)
        exw_i = sb("exw_i", [1, NF], I32)
        f_x = sb("f_x", [P, 2, TB, ROW])
        f_w1 = wq_raw[:].rearrange("p (q f) -> p q f", q=2)
        f_w2 = wo_raw[:].rearrange("p (q c) d -> p q c d", q=2)
        f_b1 = sb("f_b1", [P, 2, FC])
        f_b2 = sb("f_b2", [P, 2, D])
        f_xT = sb("f_xT", [P, 2, T])
        f_h = wkv_raw[:].rearrange("p (q c t) -> p q c t", q=2, t=T)
        f_yb = sb("f_yb", [P, 2, TB, D])
        f_y = sb("f_y", [P, 2, TB, D])
        u_flat = u_sb[:].rearrange("p q b h s -> p (q b h s)").rearrange("p (n d) -> p n d", d=D)
        e_y = tT[:, 0].rearrange("p (q s c) d -> p q s c d", q=2, s=2)
        e_sum = u_flat[:, 0:8].rearrange("p (q c) d -> p q c d", q=2)
        e_z = u_flat[:, 8:16].rearrange("p (q c) d -> p q c d", q=2)
        e_st = sb("e_st", [P, 2, ZT, 6])
        e_mv = sb("e_mv", [P, 2, ZT, 2])
        e_ve = sb("e_ve", [P, 2, ZT])
        e_rs = sb("e_rs", [P, 2, ZT])
        e_nm = sb("e_nm", [P, 2, ZT])
        e_out = u_flat[:, 16:24].rearrange("p (q c) d -> p q c d", q=2)
        eps_ln = sb("eps_ln", [P, ZT])
        eps_l2 = sb("eps_l2", [P, ZT])

        ps_s = [pb("ps_s0"), pb("ps_s1")]
        ps_pT = pb("ps_pT")
        ps_t = pb("ps_t")
        ps_u = pb("ps_u")
        ps_o = pb("ps_o")
        ps_a = pb("ps_a")
        ps_b = pb("ps_b")
        A_QKV = ps_a[:, 0:3 * D]
        A_XT = ps_a[:, 384:512]
        A_QT = ps_a[:, 0:P]
        A_AT = ps_a[:, P:P + BT]
        A_O = ps_a[:, 256:384]
        B_XT = ps_b[:, 0:P]
        B_RANK = ps_b[:, 128:128 + E]
        B_GATE = ps_b[:, 144:144 + E]
        F_XT = [ps_o[:, 0:T], ps_a[:, 0:T]]
        F_H = [ps_s, [ps_pT, ps_b]]
        F_Y = [ps_t[:, 0:TB * D], ps_u[:, 0:TB * D]]
        KVT = ps_u[:, 0:BT * P]

        s_const = sem("s_const")
        s_weights = sem("s_weights")
        half_set = sem("half_set")
        prep_ps = sem("prep_ps")
        prep_sb = sem("prep_sb")
        x_in = [sem("x_in0"), sem("x_in1")]
        c_in = [sem("c_in0"), sem("c_in1")]
        names = """in_stats in_moments in_eps in_rstd x_hat_done c_hat_done xT_ps xnT_done qkv_ps qkv_done sq_done
        qk_eps qk_rstd rot_turned rot_cosed rot_done kvp_done pick_done at_ps yT_done wo_ps attn_done
        z1_done z1_stats z1_moments z1_eps z1_rstd x1_done x1_stats x1_moments x1_eps x1_rstd l_hat_done
        l_scaled_done c_scaled_done kv_done kv_kept kvT_ps kvT_done u_ps u_done s_ps max_done exp_done inv_done p_done pT_ps pT_done
        t_ps t_done o_ps z2_done z2_stats z2_moments z2_eps z2_rstd x2_done
        x2s_done x2T_ps x2T_done gate_ps logits_done lmax_done gexp_done ginv_done gprob_done top_done top_at_done den_done den_g_done den_i_done
        weight_done atf_done picked_done mask_done seen_done rows_kept rids_kept rank_ps pos_all_done pos_sel_done pos_f_done
        pos_done pad_set pad_ready cnt_ps tab tab_base tab_ready f_xT_ps f_xT_done f_h_ps f_h_done f_y_ps f_yb_done f_y_done
        e_sum_done e_z_done e_stats e_moments e_eps e_rstd e_nm_done e_out_done""".split()
        (in_stats, in_moments, in_eps, in_rstd, x_hat_done, c_hat_done, xT_ps, xnT_done, qkv_ps, qkv_done, sq_done,
         qk_eps, qk_rstd, rot_turned, rot_cosed, rot_done, kvp_done, pick_done, at_ps, yT_done, wo_ps, attn_done,
         z1_done, z1_stats, z1_moments, z1_eps, z1_rstd, x1_done, x1_stats, x1_moments, x1_eps, x1_rstd, l_hat_done,
         l_scaled_done, c_scaled_done, kv_done, kv_kept, kvT_ps, kvT_done, u_ps, u_done, s_ps, max_done, exp_done, inv_done,
         p_done, pT_ps, pT_done, t_ps, t_done, o_ps, z2_done, z2_stats, z2_moments, z2_eps, z2_rstd,
         x2_done, x2s_done, x2T_ps, x2T_done, gate_ps, logits_done, lmax_done, gexp_done, ginv_done, gprob_done,
         top_done, top_at_done, den_done, den_g_done, den_i_done, weight_done, atf_done, picked_done, mask_done, seen_done, rows_kept,
         rids_kept, rank_ps, pos_all_done, pos_sel_done, pos_f_done, pos_done, pad_set, pad_ready, cnt_ps, tab, tab_base,
         tab_ready, f_xT_ps, f_xT_done, f_h_ps, f_h_done, f_y_ps, f_yb_done, f_y_done, e_sum_done, e_z_done, e_stats,
         e_moments, e_eps, e_rstd, e_nm_done, e_out_done) = [sem(n) for n in names]
        s_out = [sem("s_out0"), sem("s_out1")]
        x_routed = [sem("x_routed0"), sem("x_routed1")]
        pad_filled = sem("pad_filled")
        f_in = [sem("f_in0"), sem("f_in1")]
        y_routed = [sem("y_routed0"), sem("y_routed1")]
        e_in = [sem("e_in0"), sem("e_in1")]

        def wait(eng, s, n):
            if not isinstance(n, int) or n > 0:
                eng.wait_ge(s, n)

        def settle(eng):
            eng.nop(nofuse=True)

        FIRST, LAST = -3, NT + 3

        def periods(eng, period):
            lo = 4
            pairs = (NT - 4 - lo) // 2
            hi = lo + 2 * pairs
            for t in range(FIRST, lo):
                period(t, t % 2)
            with eng.Fori(0, pairs) as i:
                for half in range(2):
                    period(i * 2 + (lo + half), (lo + half) % 2)
            for t in range(hi, LAST + 1):
                period(t, t % 2)

        def pairwise(eng, n, step, tail=0):
            for i in range(2):
                step(i, i)
            if n - tail > 2:
                with eng.Fori(1, (n - tail) // 2) as i:
                    for q in range(2):
                        step(i * 2 + q, q)
            for i in range(n - tail, n):
                step(i, i % 2)

        def on(t, lag):
            return not isinstance(t, int) or 0 <= t + lag < NT

        def unit_on(t, k):
            return not isinstance(t, int) or 0 <= 4 * t + k < UNITS * NT

        def one(t):
            return bass.ds(t, 1)

        prep_list = []
        n = 0
        banks = [ps_s[0], ps_s[1], ps_pT, ps_b, ps_t, ps_u, ps_o]
        jobs = [("t", [win_raw[:, c] for c in range(3)] + [wout_raw[:]], None, 1.0)]
        for raw, lo, dst in ((wq_raw, 0, wqT), (wkv_raw, 0, wkT), (wkv_raw, H * HD, wvT)):
            for g in range(2):
                jobs.append(("t", [raw[:, lo + (4 * g + c) * P:lo + (4 * g + c + 1) * P] for c in range(4)],
                             dst[:, 4 * g:4 * g + 4].rearrange("p c d -> p (c d)"), 1.0))
        for kind, dst, scale in (("m", score_w, QS_SCALE), ("v", value_w, 1.0)):
            for g in range(4):
                jobs.append((kind, g, dst[:].rearrange("p (c r) d -> p c r d", r=2)[:, 4 * (g // 2):4 * (g // 2) + 4, g % 2],
                             scale))
        jobs.append(("b", None, b1_all[:], 1.0))
        for at, (kind, what, dst, scale) in enumerate(jobs):
            bank = banks[at % len(banks)]
            if kind == "b":
                prep_list.append((at + 1, dst, bank[:, 0:E * FC], scale))
            elif dst is None:
                prep_list.append((at + 1, winT[:], bank[:, 0:3 * D], 1.0))
                prep_list.append((at + 1, woutT[:], bank[:, 3 * D:4 * D], 1.0))
            else:
                prep_list.append((at + 1, dst, bank[:] if kind == "t" else bank[:].rearrange("p (c d) -> p c d", c=4), scale))

        block = ctx.enter_context(nc.Block())

        N_CONST, N_WEIGHTS = 18, 5

        @block.sync
        def _(sp):
            sp.dma_start(ident[:], eye).then_inc(s_const, 16)
            sp.dma_start(win_raw[:], w_in.rearrange("(c p) d -> p c d", p=P)).then_inc(s_weights, 16)
            sp.dma_start(wout_raw[:], w_out).then_inc(s_weights, 16)
            sp.dma_start(wq_raw[:], w_q).then_inc(s_weights, 16)
            sp.dma_start(wkv_raw[:], w_kv).then_inc(s_weights, 16)
            sp.dma_start(wo_raw[:], w_o.rearrange("(c p) n -> p c n", p=P)).then_inc(s_weights, 16)
            sp.dma_start(cosb[:], rot_cos).then_inc(s_const, 16)
            sp.dma_start(sinb[:], rot_sin).then_inc(s_const, 16)
            sp.dma_start(member[:], batch_of).then_inc(s_const, 16)
            sp.dma_start(gcol[:], ln_g.rearrange("(p o) -> p o", o=1)).then_inc(s_const, 16)
            sp.dma_start(bcol[:], ln_b.rearrange("(p o) -> p o", o=1)).then_inc(s_const, 16)
            for dst, src in ((g_ctx, ln1_g), (b_ctx, ln1_b), (g_lat, ln2_g), (b_lat, ln2_b)):
                sp.dma_start(dst[:], src.rearrange("(o d) -> o d", o=1).to_broadcast([P, D])).then_inc(s_const, 16)

            sp.dma_start(wg_sb[:], w_g).then_inc(s_const, 16)
            sp.dma_start(bg_sb[:], b_g.rearrange("(o d) -> o d", o=1).to_broadcast([P, E])).then_inc(s_const, 16)
            sp.dma_start(tri[:], before).then_inc(s_const, 16)
            sp.dma_start(eids[:], expert_ids).then_inc(s_const, 16)
            sp.dma_start(rbase[:], region_base).then_inc(s_const, 16)
            sp.dma_start(rids[:], row_ids).then_inc(s_const, 16)
            sp.dma_start(tids[:], tile_ids).then_inc(s_const, 16)
            sp.dma_start(b1_raw[:], b1.rearrange("e (c f) -> (e c) f", f=P)).then_inc(s_const, 16)

            def period(t, p):
                q = (p + 4) % 2
                if on(t, 4):
                    j = t + 4
                    m = (j - q) // 2 if isinstance(t, int) else None
                    load(j, q)

            def load(j, q):
                wait(sp, z1_done, j - 1)
                wait(sp, c_hat_done, j - 1)
                sp.dma_start(x_raw[:, q:q + 1, :], x_t[one(j), :, :].rearrange("t p d -> p t d")).then_inc(x_in[q], 16)
                sp.dma_start(c_raw[S:P, q:q + 1, :],
                             ctx_t[one(j), 0, :, :].rearrange("t s d -> s t d")).then_inc(c_in[q], 16)
                sp.dma_start(c_raw[0:S, q:q + 1, :],
                             ctx_t[one(j), 1, :, :].rearrange("t s d -> s t d")).then_inc(c_in[q], 16)

            load(0, 0)
            periods(sp, period)

            sp.wait_ge(pad_ready, 3)
            for b in range(TB):
                sp.dma_start(x_rows[E * CAP + b * P:E * CAP + (b + 1) * P, :], pad_row[:]).then_inc(pad_filled, 16)
            sp.wait_ge(tab_ready, 2)
            for e in range(E):
                at = sp.value_load(pad_i[0:1, e:e + 1], min_val=0, max_val=E * CAP - T)
                for b in range(TB):
                    sp.dma_start(x_rows[bass.ds(at + b * P, P), :], pad_row[:]).then_inc(pad_filled, 16)
            for s in x_routed:
                sp.wait_ge(s, 16 * NT)
            sp.wait_ge(pad_filled, 16 * TB * (E + 1))

            def ffn(i, q):
                e = sp.value_load(exw_i[0:1, bass.ds(i, 1)], min_val=0, max_val=E - 1)
                base = sp.value_load(base_i[0:1, bass.ds(i, 1)], min_val=0, max_val=E * CAP)
                if not isinstance(i, int) or i >= 2:
                    wait(sp, y_routed[q], (i - q) * (8 * TB))
                settle(sp)
                sp.dma_start(f_x[:, q], x_rows[bass.ds(base, T), :].rearrange("(b p) d -> p b d", p=P)).then_inc(f_in[q], 16)
                sp.dma_start(f_w1[:, q:q + 1], w1[bass.ds(e, 1), :, :].rearrange("e d f -> d e f")).then_inc(f_in[q], 16)
                sp.dma_start(f_w2[:, q], w2[bass.ds(e, 1), :, :].rearrange("e (c f) d -> f (e c) d", f=P)).then_inc(f_in[q], 16)
                sp.dma_start(f_b1[:, q], b1_all[:, bass.ds(e * FC, FC)]).then_inc(f_in[q], 16)
                sp.dma_start(f_b2[:, q], b2[bass.ds(e, 1), :].to_broadcast([P, D])).then_inc(f_in[q], 16)

            pairwise(sp, NF, ffn)
            for s in y_routed:
                sp.wait_ge(s, 16 * TB * (NF // 2))

            def last_in(g, q):
                wait(sp, e_sum_done, g - 1)
                for sl in range(2):
                    sp.dma_start(e_y[:, q, sl],
                                 y_rows[bass.ds(g * (ZT * P) + sl * N, ZT * P), :].rearrange("(c p) d -> p c d", p=P)
                                 ).then_inc(e_in[q], 16)

            def last_out(g, q):
                wait(sp, e_out_done, ZT * (g + 1))
                sp.dma_start(out_z[bass.ds(g * ZT, ZT), :, :].rearrange("t p d -> p t d"), e_out[:, q]).then_inc(s_out[q], 16)

            def last(g, q):
                if not isinstance(g, int) or g + 1 < NZ:
                    last_in(g + 1, (q + 1) % 2)
                last_out(g, q)

            last_in(0, 0)
            pairwise(sp, NZ, last, 2)
            for q in range(2):
                sp.wait_ge(s_out[q], 16 * (NZ // 2))

        def half_count(t, p, lag, per):
            if isinstance(t, int):
                return per * ((t + lag) // 2 + 1)
            return (t + (lag - (p + lag) % 2 + 2)) * (per // 2)

        @block.gpsimd
        def _(pool):
            nc.gpsimd.memset(m_half[:], -0.5).then_inc(half_set, 1)
            nc.gpsimd.memset(eps_ln[:], EPS_LN).then_inc(half_set, 1)
            nc.gpsimd.memset(eps_l2[:], EPS_L2).then_inc(half_set, 1)

            def rstd(var, ve, rs, eps, moments, n_moments, eps_done, rstd_done, j):
                wait(pool, moments, n_moments)
                nc.gpsimd.tensor_tensor(ve, var, eps[:, 0:var.shape[-1]], ALU.add).then_inc(eps_done, 1)
                wait(pool, eps_done, j + 1)
                nc.gpsimd.tensor_tensor(rs, ve, m_half[:, 0:rs.shape[-1]], ALU.pow).then_inc(rstd_done, 1)

            def scale(t, k):
                n, sl = t * 4 + k, k % 2
                wait(pool, inv_done, n + 1)
                wait(pool, pT_ps, n - 1)
                nc.gpsimd.tensor_tensor(
                    probs_n[:, sl], probs[:, sl],
                    inv_sum[:, sl, :].rearrange("p (u o) -> p u o", o=1).to_broadcast([P, UP, P]),
                    ALU.mult).then_inc(p_done, 1)

            def period(t, p):
                p3, p2 = (p + 3) % 2, p
                for k in range(UNITS):
                    if k == 1 and on(t, -4):
                        wait(pool, rows_kept, t - 3)
                        wait(pool, rids_kept, t - 3)
                        wait(pool, weight_done, t - 3)
                        wait(pool, pos_done, t - 3)
                        for sl in range(2):
                            settle(pool)
                            pool.indirect_dma_start(
                                out=x_rows, out_offset=bass.IndirectOffsetOnAxis(ap=pos_i[:, p, sl:sl + 1].bitcast(U32), axis=0),
                                in_=routed[:, p, sl], in_offset=None, bounds_check=E * CAP - 1,
                                oob_is_err=False).then_inc(x_routed[p], 16)
                    if k == 0 and on(t, -2):
                        rstd(mv_z2[:, p, 1:2], ve_z2[:, p], rs_z2[:, p], eps_ln, z2_moments, t - 1, z2_eps, z2_rstd, t - 2)
                    if k == 0 and on(t, 3):
                        rstd(mv_in[:, p3, :, 1], ve_in[:, p3], rs_in[:, p3], eps_ln, in_moments, 2 * t + 8, in_eps, in_rstd, t + 3)
                    if k == 0 and on(t, 2):
                        rstd(mv_z1[:, p2, 1:2], ve_z1[:, p2], rs_z1[:, p2], eps_ln, z1_moments, t + 3, z1_eps, z1_rstd, t + 2)
                    if k == 1 and on(t, 2):
                        rstd(mv_x1[:, p2, 1:2], ve_x1[:, p2], rs_x1[:, p2], eps_ln, x1_moments, t + 3, x1_eps, x1_rstd, t + 2)
                    if k == 2 and on(t, 2):
                        wait(pool, l_hat_done, t + 3)
                        nc.gpsimd.tensor_tensor(l_scaled[:, p2], l_hat[:, p2], g_lat[:], ALU.mult).then_inc(l_scaled_done, 1)
                        wait(pool, c_hat_done, t + 3)
                        nc.gpsimd.tensor_tensor(c_scaled[:, p2], c_hat[:, p2], g_ctx[:], ALU.mult).then_inc(c_scaled_done, 1)
                        wait(pool, kv_kept, 4 * t + 4)
                        wait(pool, l_scaled_done, t + 3)
                        nc.gpsimd.tensor_tensor(l_rows[:, p2], l_scaled[:, p2], b_lat[:], ALU.add).then_inc(kv_done, 1)
                        wait(pool, c_scaled_done, t + 3)
                        nc.gpsimd.tensor_tensor(c_rows[:, p2], c_scaled[:, p2], b_ctx[:], ALU.add).then_inc(kv_done, 1)
                    if on(t, 0):
                        scale(t, k)
                    if k == 2 and on(t, 3):
                        rstd(ss_qk[:, p3], se_qk[:, p3], rs_qk[:, p3], eps_l2, sq_done, 2 * t + 8, qk_eps, qk_rstd, t + 3)

            pool.wait_ge(half_set, 3)
            pool.wait_ge(s_const, 16 * N_CONST)
            periods(pool, period)

            def ffn(i, q):
                wait(pool, f_y_done, TB * (i + 1))
                for b in range(TB):
                    settle(pool)
                    pool.indirect_dma_start(
                        out=y_rows, out_offset=bass.IndirectOffsetOnAxis(ap=f_x[:, q, b, D + 1:D + 2].bitcast(U32), axis=0),
                        in_=f_y[:, q, b], in_offset=None, bounds_check=2 * N - 1, oob_is_err=False).then_inc(y_routed[q], 16)

            pairwise(pool, NF, ffn)

            def last(g, q):
                if not isinstance(g, int) or g < NZ:
                    wait(pool, e_in[q], (g + (2 - q)) * 16)
                    wait(pool, e_z_done, g - 1)
                    nc.gpsimd.tensor_tensor(e_sum[:, q], e_y[:, q, 0], e_y[:, q, 1], ALU.add).then_inc(e_sum_done, 1)
                if not isinstance(g, int) or g:
                    rstd(e_mv[:, 1 - q, :, 1], e_ve[:, 1 - q], e_rs[:, 1 - q], eps_ln, e_moments, ZT * g, e_eps, e_rstd, g - 1)

            pairwise(pool, NZ, last)
            last(NZ, 0)

        PREP = 7 + 8

        @block.scalar
        def _(act):
            def prep(n, dst, src, scale=1.0):
                act.wait_ge(prep_ps, n)
                nc.scalar.activation(dst, src, ACT.Copy, scale=scale).then_inc(prep_sb, 1)
            for n, dst, src, scale in prep_list:
                prep(n, dst, src, scale)

            act.wait_ge(s_const, 16 * N_CONST)

            def exps(t, k):
                n, sl = t * 4 + k, k % 2
                wait(act, max_done, n + 1)
                wait(act, p_done, n - 1)
                for j in range(UP):
                    last = nc.scalar.activation(probs[:, sl, j], ps_s[sl][:, j * P:(j + 1) * P], ACT.Exp,
                                                bias=neg_max[:, sl, j:j + 1], accum_out=sums[:, sl, j:j + 1])
                last.then_inc(exp_done, 1)

            def period(t, p):
                p3, p2, p1 = (p + 3) % 2, p, (p + 1) % 2
                for k in range(UNITS):
                    if on(t, 0):
                        exps(t, k)
                    if k == 0 and on(t, 2):
                        wait(act, wo_ps, t + 3)
                        wait(act, qk_rstd, t + 3)
                        nc.scalar.activation(attn_o[:, p2], A_O, ACT.Copy, scale=rs_qk[:, p2, 0:1]).then_inc(attn_done, 1)
                    if k == 1 and on(t, 3):
                        wait(act, xT_ps, t + 4)
                        nc.scalar.activation(xnT[:, p3], A_XT, ACT.Identity, scale=gcol[:, 0:1],
                                             bias=bcol[:, 0:1]).then_inc(xnT_done, 1)
                    if k == 2 and on(t, 3):
                        wait(act, qkv_ps, t + 4)
                        nc.scalar.activation(qkv[:, p3], A_QKV, ACT.Copy).then_inc(qkv_done, 1)
                        for j in range(2):
                            nc.scalar.activation(sq_junk[:, j], A_QKV[:, j * D:(j + 1) * D], ACT.Square,
                                                 accum_out=ss_qk[:, p3, j:j + 1]).then_inc(sq_done, 1)
                    if on(t, 1):
                        wait(act, u_ps, 4 * t + (4 + k + 1))
                        nc.scalar.activation(u_sb[:, p1, :, 4 * k:4 * k + 4, :].rearrange("p b h s -> p h b s"),
                                             ps_u[:].rearrange("p (h b s) -> p h b s", b=BT, s=S), ACT.Copy).then_inc(u_done, 1)
                    if k == 0 and on(t, -3):
                        wait(act, lmax_done, t - 2)
                        nc.scalar.activation(gexp[:, p3], logits[:, p3], ACT.Exp, bias=lmax[:, p3, 0:1],
                                             accum_out=gsum[:, p3, 0:1]).then_inc(gexp_done, 1)
                    if k == 2 and on(t, -2):
                        wait(act, x2T_ps, t - 1)
                        nc.scalar.activation(x2T[:, p], B_XT, ACT.Copy).then_inc(x2T_done, 1)
                    if unit_on(t, k - 1):
                        n = t * 4 + (k - 1)
                        kk = (k - 1) % 4
                        pp = p if k else (p + 1) % 2
                        b, hf = kk // 2, kk % 2
                        wait(act, t_ps, n + 1)
                        nc.scalar.activation(tT[:, pp, hf * HH:(hf + 1) * HH, b * S:(b + 1) * S],
                                             ps_t[:].rearrange("p (h q) -> p h q", q=S), ACT.Copy).then_inc(t_done, 1)
                    if k == 3 and on(t, 2):
                        wait(act, kvT_ps, t + 3)
                        nc.scalar.activation(kvT[:, p2, 1:3], KVT[:, 0:P].rearrange("p (b s) -> p b s", b=BT), ACT.Copy).then_inc(kvT_done, 1)
                        nc.scalar.activation(kvT[:, p2, 0:4:3], KVT[:, P:2 * P].rearrange("p (b s) -> p b s", b=BT), ACT.Copy).then_inc(kvT_done, 1)

            periods(act, period)

            def ffn(i, q):
                wait(act, f_in[q], (i + (2 - q)) * 40)
                for c in range(FC):
                    wait(act, f_h_ps, i * (FC // 2) + (c // 2 + 1))
                    if c == 0:
                        wait(act, f_y_ps, i - 1)
                    nc.scalar.activation(f_h[:, q, c], F_H[q][c // 2][:, (c % 2) * T:(c % 2 + 1) * T], ACT.Gelu,
                                         bias=f_b1[:, q, c:c + 1]).then_inc(f_h_done, 1)

            pairwise(act, NF, ffn)

            def last(g, q):
                wait(act, e_nm_done, g + 1)
                if not isinstance(g, int) or g >= 2:
                    wait(act, s_out[q], (g - q) * 8)
                for c in range(ZT):
                    nc.scalar.activation(e_out[:, q, c], e_z[:, q, c], ACT.Identity, scale=e_rs[:, q, c:c + 1],
                                         bias=e_nm[:, q, c:c + 1]).then_inc(e_out_done, 1)

            pairwise(act, NZ, last)

        @block.vector
        def _(dve):
            nc.vector.memset(pad_row[:, 0:D + 1], 0.0).then_inc(pad_ready, 1)
            nc.vector.memset(pad_row[:, D + 1:D + 2].bitcast(I32), 2 * N).then_inc(pad_ready, 1)
            nc.vector.memset(ones[:], 1.0).then_inc(pad_ready, 1)
            nc.vector.memset(seen[:, 0], 0.0).then_inc(seen_done, 1)
            dve.wait_ge(s_const, 16 * N_CONST)

            def period(t, p):
                p3, p2 = (p + 3) % 2, p
                for k in range(UNITS):
                    n, sl = t * 4 + k, k % 2
                    if on(t, 0):
                        wait(dve, s_ps, n + 1)
                        wait(dve, exp_done, n - 1)
                        nc.vector.tensor_reduce(neg_max[:, sl], ps_s[sl][:].rearrange("p (u k) -> p u k", k=P),
                                                axis=AX.X, op=ALU.max, negate=True).then_inc(max_done, 1)
                    if k == 0 and on(t, -2):
                        wait(dve, o_ps, t - 1)
                        nc.vector.tensor_tensor(z2[:, p:p + 1], ps_o[:, 0:D].rearrange("p (o d) -> p o d", o=1),
                                                rows[:, one(t - 2), :], ALU.add).then_inc(z2_done, 1)
                    if k == 0 and on(t, 3):
                        q = p3
                        wait(dve, x_in[q], half_count(t, p, 3, 16))
                        settle(dve)
                        nc.vector.bn_stats(st_in[:, q, 0], x_raw[:, q]).then_inc(in_stats, 1)
                        wait(dve, c_in[q], half_count(t, p, 3, 32))
                        settle(dve)
                        nc.vector.bn_stats(st_in[:, q, 1], c_raw[:, q]).then_inc(in_stats, 1)
                    if k == 0 and on(t, -2):
                        wait(dve, z2_done, t - 1)
                        settle(dve)
                        nc.vector.bn_stats(st_z2[:, p], z2[:, p]).then_inc(z2_stats, 1)
                    if k == 0 and on(t, 3):
                        for j in range(2):
                            wait(dve, in_stats, 2 * t + (7 + j))
                            settle(dve)
                            nc.vector.bn_aggr(mv_in[:, p3, j], st_in[:, p3, j]).then_inc(in_moments, 1)
                    if k == 0 and on(t, -2):
                        wait(dve, z2_stats, t - 1)
                        settle(dve)
                        nc.vector.bn_aggr(mv_z2[:, p], st_z2[:, p]).then_inc(z2_moments, 1)
                    if k == 1 and on(t, 3):
                        wait(dve, in_rstd, t + 4)
                        nc.vector.tensor_scalar(x_hat[:, p3], x_raw[:, p3], mv_in[:, p3, 0, 0:1], rs_in[:, p3, 0:1],
                                                ALU.subtract, ALU.mult).then_inc(x_hat_done, 1)
                        nc.vector.tensor_scalar(c_hat[:, p3], c_raw[:, p3], mv_in[:, p3, 1, 0:1], rs_in[:, p3, 1:2],
                                                ALU.subtract, ALU.mult).then_inc(c_hat_done, 1)
                    if k == 1 and on(t, -2):
                        wait(dve, z2_rstd, t - 1)
                        wait(dve, x2T_ps, t - 3)
                        nc.vector.tensor_scalar(x2s[:, p], z2[:, p], mv_z2[:, p, 0:1], rs_z2[:, p, 0:1],
                                                ALU.subtract, ALU.mult).then_inc(x2s_done, 1)
                        nc.vector.tensor_scalar(rows[:, one(t - 2), :], z2[:, p:p + 1], mv_z2[:, p, 0:1], rs_z2[:, p, 0:1],
                                                ALU.subtract, ALU.mult).then_inc(x2_done, 1)
                    if k == 1 and on(t, 1):
                        wait(dve, kv_done, 2 * t + 4)
                        wait(dve, t_ps, 4 * t)
                        p1 = (p + 1) % 2
                        for b in range(BT):
                            own, other = slice(b * S, (b + 1) * S), slice((1 - b) * S, (2 - b) * S)
                            nc.vector.tensor_copy(kv_rows[own, p1, b], l_rows[own, p1]).then_inc(kv_kept, 1)
                            nc.vector.tensor_copy(kv_rows[other, p1, b], c_rows[other, p1]).then_inc(kv_kept, 1)
                    if k == 2 and on(t, 2):
                        wait(dve, x1_rstd, t + 3)
                        nc.vector.tensor_scalar(l_hat[:, p2:p2 + 1], rows[:, one(t + 2), :], mv_x1[:, p2, 0:1], rs_x1[:, p2, 0:1],
                                                ALU.subtract, ALU.mult).then_inc(l_hat_done, 1)
                    if k == 3 and on(t, 3):
                        qk = qkv[:, p3, 0:2 * D].rearrange("p (w d) -> p w d", w=2)[:, :, 0:ROT]
                        pairs = qk.rearrange("p w (i two) -> p w i two", two=2)
                        trn = turned[:, p3].rearrange("p w (i two) -> p w i two", two=2)
                        sn = sinb[:].rearrange("p (o i two) -> p o i two", o=1, two=2)
                        wait(dve, qkv_done, t + 4)
                        for j in range(2):
                            nc.vector.tensor_tensor(trn[:, :, :, j], pairs[:, :, :, 1 - j],
                                                    sn[:, :, :, j].to_broadcast([P, 2, ROT // 2]), ALU.mult).then_inc(rot_turned, 1)
                        wait(dve, rot_turned, 2 * t + 8)
                        nc.vector.tensor_tensor(qk, qk, cosb[:].rearrange("p (o d) -> p o d", o=1).to_broadcast([P, 2, ROT]),
                                                ALU.mult).then_inc(rot_cosed, 1)
                        wait(dve, rot_cosed, t + 4)
                        nc.vector.tensor_tensor(qk, qk, turned[:, p3], ALU.add).then_inc(rot_done, 1)
                        wait(dve, qk_rstd, t + 4)
                        nc.vector.tensor_scalar(k_pick[:, p3], member[:], rs_qk[:, p3, 1:2], None, ALU.mult).then_inc(pick_done, 1)
                        wait(dve, rot_done, t + 4)
                        nc.vector.tensor_tensor(kv_prod[:, p3], qkv[:, p3, D:2 * D], qkv[:, p3, 2 * D:3 * D],
                                                ALU.mult).then_inc(kvp_done, 1)
                    if k == 0 and on(t, -3):
                        wait(dve, gate_ps, t - 2)
                        nc.vector.tensor_tensor(logits[:, p3], B_GATE, bg_sb[:], ALU.add).then_inc(logits_done, 1)
                        wait(dve, logits_done, t - 2)
                        nc.vector.tensor_reduce(lmax[:, p3], logits[:, p3], axis=AX.X, op=ALU.max, negate=True).then_inc(lmax_done, 1)
                    if k == 0 and on(t, -4):
                        wait(dve, rank_ps, t - 3)
                        nc.vector.tensor_tensor(pos_all[:, p], B_RANK, rbase[:], ALU.add).then_inc(pos_all_done, 1)
                        wait(dve, pos_all_done, t - 3)
                        nc.vector.tensor_tensor(pos_sel[:, p], picked[:, p], pos_all[:, p:p + 1].to_broadcast([P, 2, E]),
                                                ALU.mult).then_inc(pos_sel_done, 1)
                        wait(dve, pos_sel_done, t - 3)
                        nc.vector.tensor_reduce(pos_f[:, p], pos_sel[:, p], axis=AX.X, op=ALU.add).then_inc(pos_f_done, 1)
                        wait(dve, pos_f_done, t - 3)
                        wait(dve, x_routed[p], (t - (p + 4)) * 16)
                        nc.vector.tensor_copy(pos_i[:, p], pos_f[:, p]).then_inc(pos_done, 1)
                    if k == 1 and on(t, -3):
                        wait(dve, gexp_done, t - 2)
                        nc.vector.reciprocal(ginv[:, p3], gsum[:, p3]).then_inc(ginv_done, 1)
                        wait(dve, ginv_done, t - 2)
                        nc.vector.tensor_scalar(gprob[:, p3], gexp[:, p3], ginv[:, p3, 0:1], None, ALU.mult).then_inc(gprob_done, 1)
                        wait(dve, gprob_done, t - 2)
                        settle(dve)
                        nc.vector.max(top[:, p3], gprob[:, p3]).then_inc(top_done, 1)
                    if k == 2 and on(t, -3):
                        wait(dve, top_done, t - 2)
                        settle(dve)
                        nc.vector.max_index(top_at[:, p3], top[:, p3], gprob[:, p3]).then_inc(top_at_done, 1)
                        nc.vector.tensor_tensor(den[:, p3], top[:, p3, 0:1], top[:, p3, 1:2], ALU.add).then_inc(den_done, 1)
                        wait(dve, top_at_done, t - 2)
                        nc.vector.tensor_copy(top_atf[:, p3], top_at[:, p3, 0:2]).then_inc(atf_done, 1)
                        wait(dve, den_done, t - 2)
                        nc.vector.scalar_tensor_tensor(den_g[:, p3], den[:, p3], 0.0, den[:, p3], ALU.is_equal,
                                                       ALU.add).then_inc(den_g_done, 1)
                        wait(dve, atf_done, t - 2)
                        nc.vector.tensor_tensor(picked[:, p3], eids[:].rearrange("p (o e) -> p o e", o=1).to_broadcast([P, 2, E]),
                                                top_atf[:, p3].rearrange("p (s o) -> p s o", o=1).to_broadcast([P, 2, E]),
                                                ALU.is_equal).then_inc(picked_done, 1)
                        wait(dve, den_g_done, t - 2)
                        nc.vector.reciprocal(den_i[:, p3], den_g[:, p3]).then_inc(den_i_done, 1)
                        wait(dve, picked_done, t - 2)
                        nc.vector.tensor_tensor(mask[:, p3], picked[:, p3, 0], picked[:, p3, 1], ALU.add).then_inc(mask_done, 1)
                    if k == 3 and on(t, -3):
                        wait(dve, mask_done, t - 2)
                        nc.vector.tensor_tensor(seen[:, 1 - p3], seen[:, p3], mask[:, p3], ALU.add).then_inc(seen_done, 1)
                        wait(dve, x_routed[p3], (t - (p3 + 3)) * 16)
                        wait(dve, den_i_done, t - 2)
                        nc.vector.tensor_scalar(routed[:, p3, :, D], top[:, p3, 0:2], den_i[:, p3, 0:1], None,
                                                ALU.mult).then_inc(weight_done, 1)
                        nc.vector.tensor_copy(routed[:, p3, :, 0:D],
                                              rows[:, one(t - 3), :].to_broadcast([P, 2, D])).then_inc(rows_kept, 1)
                        nc.vector.tensor_copy(routed[:, p3, :, D + 1:D + 2].bitcast(I32).rearrange("p s o -> p o s"),
                                              rids[:, one(t - 3), :]).then_inc(rids_kept, 1)
                    if unit_on(t, k - 1):
                        m, ss = t * 4 + (k - 1), (k - 1) % 2
                        wait(dve, pT_ps, m + 1)
                        wait(dve, t_ps, m - 1)
                        nc.vector.tensor_copy(pT[:, ss], ps_pT[:]).then_inc(pT_done, 1)
                    if on(t, 0):
                        wait(dve, exp_done, n + 1)
                        nc.vector.reciprocal(inv_sum[:, sl], sums[:, sl]).then_inc(inv_done, 1)
                    if k == 0 and on(t, 2):
                        wait(dve, attn_done, t + 3)
                        nc.vector.scalar_tensor_tensor(z1[:, p2], x_raw[:, p2], 2.0, attn_o[:, p2], ALU.mult, ALU.add).then_inc(z1_done, 1)
                        wait(dve, z1_done, t + 3)
                        settle(dve)
                        nc.vector.bn_stats(st_z1[:, p2], z1[:, p2]).then_inc(z1_stats, 1)
                        wait(dve, z1_stats, t + 3)
                        settle(dve)
                        nc.vector.bn_aggr(mv_z1[:, p2], st_z1[:, p2]).then_inc(z1_moments, 1)
                    if k == 1 and on(t, 2):
                        wait(dve, z1_rstd, t + 3)
                        nc.vector.tensor_scalar(rows[:, one(t + 2), :], z1[:, p2:p2 + 1], mv_z1[:, p2, 0:1], rs_z1[:, p2, 0:1],
                                                ALU.subtract, ALU.mult).then_inc(x1_done, 1)
                        wait(dve, x1_done, t + 3)
                        settle(dve)
                        nc.vector.bn_stats(st_x1[:, p2], rows[:, one(t + 2), :]).then_inc(x1_stats, 1)
                        wait(dve, x1_stats, t + 3)
                        settle(dve)
                        nc.vector.bn_aggr(mv_x1[:, p2], st_x1[:, p2]).then_inc(x1_moments, 1)
                    if k == 3 and on(t, 3):
                        wait(dve, at_ps, t + 4)
                        for b in range(BT):
                            nc.vector.tensor_scalar(yT[:, p3, b * S:(b + 1) * S], A_QT[:, b * S:(b + 1) * S],
                                                    A_AT[:, b:b + 1], None, ALU.mult).then_inc(yT_done, 1)

            periods(dve, period)

            steps = [0]

            def then(ins):
                steps[0] += 1
                ins.then_inc(tab, 1)
                dve.wait_ge(tab, steps[0])

            dve.wait_ge(cnt_ps, 1)
            then(nc.vector.tensor_scalar(cnt_up[:], B_RANK[0:1], float(T - 1), None, ALU.add))
            nc.vector.tensor_tensor(pad_f[:], B_RANK[0:1], rbase[0:1], ALU.add).then_inc(tab_base, 1)
            then(nc.vector.tensor_copy(cnt_i[:], cnt_up[:]))
            dve.wait_ge(tab_base, 1)
            nc.vector.tensor_copy(pad_i[:], pad_f[:]).then_inc(tab_ready, 1)
            then(nc.vector.tensor_scalar(nt_i[:], cnt_i[:], T.bit_length() - 1, None, ALU.arith_shift_right))
            then(nc.vector.tensor_copy(nt_f[:], nt_i[:]))
            then(nc.vector.tensor_tensor_scan(cum_nt[:], ones[0:1, 0:E], nt_f[:], 0.0, ALU.mult, ALU.add))
            over_tiles = lambda ap: ap.rearrange("p (o e) -> p o e", o=1).to_broadcast([1, NF, E])
            then(nc.vector.tensor_tensor(past[:], over_tiles(cum_nt[:]),
                                         tids[:].rearrange("p (i o) -> p i o", o=1).to_broadcast([1, NF, E]), ALU.is_le))
            then(nc.vector.tensor_tensor(past_nt[:], past[:], over_tiles(nt_f[:]), ALU.mult))
            then(nc.vector.tensor_reduce(ex_f[:], past[:], axis=AX.X, op=ALU.add))
            then(nc.vector.tensor_reduce(start_f[:], past_nt[:], axis=AX.X, op=ALU.add))
            then(nc.vector.tensor_scalar(valid_f[:], ex_f[:], E - 0.5, float(T), ALU.is_lt, ALU.mult))
            then(nc.vector.tensor_tensor(blk_f[:], tids[:], start_f[:], ALU.subtract))
            then(nc.vector.tensor_tensor(blk_v[:], blk_f[:], valid_f[:], ALU.mult))
            then(nc.vector.scalar_tensor_tensor(base_f[:], ex_f[:], float(CAP), blk_v[:], ALU.mult, ALU.add))
            then(nc.vector.tensor_scalar(exw_f[:], ex_f[:], float(E - 1), None, ALU.min))
            then(nc.vector.tensor_copy(base_i[:], base_f[:]))
            nc.vector.tensor_copy(exw_i[:], exw_f[:]).then_inc(tab_ready, 1)

            def rowsT(i, q):
                wait(dve, f_xT_ps, i + 1)
                wait(dve, f_h_ps, i * (FC // 2) - FC // 2)
                nc.vector.tensor_copy(f_xT[:, q], F_XT[q]).then_inc(f_xT_done, 1)

            def result(i, q):
                wait(dve, f_y_ps, i + 1)
                wait(dve, f_y_done, TB * i - TB)
                nc.vector.tensor_tensor(f_yb[:, q], F_Y[q].rearrange("p (b d) -> p b d", d=D),
                                        f_b2[:, q:q + 1].to_broadcast([P, TB, D]), ALU.add).then_inc(f_yb_done, 1)
                wait(dve, f_yb_done, i + 1)
                if not isinstance(i, int) or i >= 2:
                    wait(dve, y_routed[q], (i - q) * (8 * TB))
                for b in range(TB):
                    nc.vector.tensor_scalar(f_y[:, q, b], f_yb[:, q, b], f_x[:, q, b, D:D + 1], None,
                                            ALU.mult).then_inc(f_y_done, 1)

            def ffn(i, q):
                if not isinstance(i, int) or i:
                    result(i - 1, 1 - q)
                if not isinstance(i, int) or i + 1 < NF:
                    rowsT(i + 1, 1 - q)

            rowsT(0, 0)
            pairwise(dve, NF, ffn, 2)
            result(NF - 1, 1)

            def last(g, q):
                if not isinstance(g, int) or g < NZ:
                    wait(dve, e_sum_done, g + 1)
                    wait(dve, e_out_done, ZT * g - ZT)
                    nc.vector.tensor_tensor(e_z[:, q], e_sum[:, q], rows[:, bass.ds(g * ZT, ZT), :], ALU.add).then_inc(e_z_done, 1)
                    wait(dve, e_z_done, g + 1)
                    for c in range(ZT):
                        nc.vector.bn_stats(e_st[:, q, c], e_z[:, q, c]).then_inc(e_stats, 1)
                    for c in range(ZT):
                        wait(dve, e_stats, g * ZT + (c + 1))
                        settle(dve)
                        nc.vector.bn_aggr(e_mv[:, q, c], e_st[:, q, c]).then_inc(e_moments, 1)
                if not isinstance(g, int) or g:
                    o = 1 - q
                    wait(dve, e_rstd, g)
                    nc.vector.scalar_tensor_tensor(e_nm[:, o], e_mv[:, o, :, 0], -1.0, e_rs[:, o], ALU.mult, ALU.mult).then_inc(e_nm_done, 1)

            pairwise(dve, NZ, last)
            last(NZ, 0)

        @block.tensor
        def _(pe):
            pe.wait_ge(s_const, 16 * N_CONST)
            pe.wait_ge(s_weights, 16 * N_WEIGHTS)
            for at, (kind, what, dst, scale) in enumerate(jobs):
                bank = banks[at % len(banks)]
                if kind != "t":
                    pe.wait_ge(prep_sb, max(at - len(banks) + 2, 8))
                elif at >= len(banks):
                    pe.wait_ge(prep_sb, at - len(banks) + 2)
                for c in range(4):
                    o = bank[:, c * P:(c + 1) * P]
                    if kind == "t":
                        last = nc.tensor.transpose(o, what[c], ident[:])
                        continue
                    if kind == "b":
                        last = nc.tensor.transpose(bank[:, 0:E * FC], b1_raw[:], ident[0:E * FC, 0:E * FC])
                        break
                    h = 8 * (what // 2) + 2 * c + what % 2
                    e = slice((h % 2) * HD, (h % 2 + 1) * HD)
                    if kind == "m":
                        last = nc.tensor.matmul(o, wqT[e, h // 2], wkT[e, h // 2], start=True, stop=True)
                    else:
                        last = nc.tensor.matmul(o, wvT[e, h // 2], wo_raw[e, h // 2], start=True, stop=True)
                last.then_inc(prep_ps, 1)
            pe.wait_ge(prep_sb, len(prep_list))
            pe.wait_ge(pad_ready, 3)

            def score(t, k, p):
                n, sl, b, hf = t * 4 + k, k % 2, k // 2, k % 2
                if k == 0:
                    wait(pe, u_done, 4 * t + 4)
                    wait(pe, kvT_done, 2 * t + 2)
                wait(pe, exp_done, n - 1)
                for j in range(UP):
                    h = hf * HH + 2 * j
                    last = nc.tensor.matmul(ps_s[sl][:, j * P:(j + 1) * P], u_sb[:, p, b, h:h + 2].rearrange("p h s -> p (h s)"),
                                            kvT[:, p, 1 - b:4 - b:2], start=True, stop=True)
                last.then_inc(s_ps, 1)

            def out_part(t, k, p):
                if k == 1:
                    wait(pe, t_done, 4 * t)
                    wait(pe, z2_done, t - 1)
                lo, hi = ((0, 6), (6, 11), (11, 16))[k - 1]
                for h in range(lo, hi):
                    last = nc.tensor.matmul(ps_o[:, 0:D], tT[:, (p + 1) % 2, h], value_w[:, h],
                                            start=(h == 0), stop=(h == H - 1))
                if k == 3:
                    last.then_inc(o_ps, 1)

            def period(t, p):
                p3, p2, p1 = (p + 3) % 2, p, (p + 1) % 2
                for k in range(UNITS):
                    if on(t, 0):
                        score(t, k, p)
                    if k and on(t, -1):
                        out_part(t, k, p)
                    if unit_on(t, k - 1):
                        m, ss = t * 4 + (k - 1), (k - 1) % 2
                        wait(pe, p_done, m + 1)
                        wait(pe, pT_done, m)
                        for j in range(UP):
                            last = nc.tensor.transpose(ps_pT[:, j * P:(j + 1) * P], probs_n[:, ss, j], ident[:])
                        last.then_inc(pT_ps, 1)
                    if k == 0 and on(t, 2):
                        wait(pe, yT_done, 2 * t + 6)
                        nc.tensor.matmul(A_O, yT[:, p2], woutT[:], start=True, stop=True).then_inc(wo_ps, 1)
                    if k == 0 and on(t, -4):
                        wait(pe, mask_done, t - 3)
                        wait(pe, seen_done, t - 3)
                        wait(pe, logits_done, min(t - 2, NT) if isinstance(t, int) else t - 2)
                        nc.tensor.matmul(B_RANK, ones[:], seen[:, p], start=True, stop=False)
                        nc.tensor.matmul(B_RANK, tri[:], mask[:, p], start=False, stop=True).then_inc(rank_ps, 1)
                    if k == 2 and on(t, -2):
                        wait(pe, x2s_done, t - 1)
                        wait(pe, pos_all_done, t - 3)
                        nc.tensor.transpose(B_XT, x2s[:, p], ident[:]).then_inc(x2T_ps, 1)
                    if k == 1 and on(t, 3):
                        wait(pe, x_hat_done, t + 4)
                        wait(pe, attn_done, t + 3)
                        nc.tensor.transpose(A_XT, x_hat[:, p3], ident[:]).then_inc(xT_ps, 1)
                    if k == 2 and on(t, 3):
                        wait(pe, xnT_done, t + 4)
                        nc.tensor.matmul(A_QKV, xnT[:, p3], winT[:], start=True, stop=True).then_inc(qkv_ps, 1)
                    if on(t, 1):
                        if k == 0:
                            wait(pe, kvT_done, 2 * t + 4)
                        wait(pe, u_done, 4 * t + (4 + k))
                        for c in range(4):
                            last = nc.tensor.matmul(ps_u[:, c * P:(c + 1) * P], score_w[:, 4 * k + c],
                                                    kvT[:, p1, 1:3].rearrange("p b s -> p (b s)"), start=True, stop=True)
                        last.then_inc(u_ps, 1)
                    if k == 3 and on(t, 3):
                        wait(pe, kvp_done, t + 4)
                        wait(pe, pick_done, t + 4)
                        nc.tensor.transpose(A_QT, qkv[:, p3, 0:D], ident[:])
                        nc.tensor.matmul(A_AT, kv_prod[:, p3], k_pick[:, p3], start=True, stop=True).then_inc(at_ps, 1)
                    if k == 3 and on(t, -2):
                        wait(pe, x2T_done, t - 1)
                        nc.tensor.matmul(B_GATE, x2T[:, p], wg_sb[:], start=True, stop=True).then_inc(gate_ps, 1)
                    if unit_on(t, k - 1):
                        m, ss = t * 4 + (k - 1), (k - 1) % 2
                        b = (k - 1) % 4 // 2
                        pp = p if k else (p + 1) % 2
                        wait(pe, pT_done, m + 1)
                        wait(pe, t_done, m)
                        nc.tensor.matmul(ps_t[:], kv_rows[:, pp, b], pT[:, ss], start=True, stop=True).then_inc(t_ps, 1)
                    if k == 3 and on(t, 2):
                        wait(pe, kv_done, 2 * t + 6)
                        wait(pe, u_done, 4 * t + 8)
                        nc.tensor.transpose(KVT[:, 0:P], l_rows[:, p2], ident[:])
                        last = nc.tensor.transpose(KVT[:, P:2 * P], c_rows[:, p2], ident[:])
                        last.then_inc(kvT_ps, 1)

            periods(pe, period)

            pe.wait_ge(pos_all_done, NT)
            pe.wait_ge(seen_done, NT + 1)
            nc.tensor.matmul(B_RANK, ones[:], seen[:, NT % 2], start=True, stop=True).then_inc(cnt_ps, 1)
            pe.wait_ge(tab, 1)

            def rowsT(i, q):
                wait(pe, f_in[q], (i + (2 - q)) * 40)
                wait(pe, f_xT_done, i - 1)
                for b in range(TB):
                    last = nc.tensor.transpose(F_XT[q][:, b * P:(b + 1) * P], f_x[:, q, b, 0:D], ident[:])
                last.then_inc(f_xT_ps, 1)

            def hidden(i, q):
                wait(pe, f_xT_done, i + 1)
                wait(pe, f_h_done, i * FC - FC)
                for c in range(FC):
                    done = nc.tensor.matmul(F_H[q][c // 2][:, (c % 2) * T:(c % 2 + 1) * T], f_w1[:, q, c * P:(c + 1) * P],
                                            f_xT[:, q], start=True, stop=True)
                    if c % 2:
                        done.then_inc(f_h_ps, 1)

            def result(i, q):
                wait(pe, f_h_done, i * FC + FC)
                wait(pe, f_yb_done, i - 1)
                for b in range(TB):
                    for c in range(FC):
                        last = nc.tensor.matmul(F_Y[q][:, b * D:(b + 1) * D], f_h[:, q, c, b * P:(b + 1) * P],
                                                f_w2[:, q, c], start=(c == 0), stop=(c == FC - 1))
                last.then_inc(f_y_ps, 1)

            def ffn(i, q):
                hidden(i, q)
                if not isinstance(i, int) or i:
                    result(i - 1, 1 - q)
                if not isinstance(i, int) or i + 1 < NF:
                    rowsT(i + 1, 1 - q)

            rowsT(0, 0)
            pairwise(pe, NF, ffn, 2)
            result(NF - 1, 1)


_ARGS = {
    "x": "x", "ctx_in": "ctx_1024", "w_in": "L0_attn_W_in", "w_out": "L0_attn_W_out", "ln_g": "L0_attn_ln_g",
    "ln_b": "L0_attn_ln_b", "ln1_g": "L0_xattn_ln1_g", "ln1_b": "L0_xattn_ln1_b", "ln2_g": "L0_xattn_ln2_g",
    "ln2_b": "L0_xattn_ln2_b", "w_q": "L0_xattn_Wq", "w_kv": "L0_xattn_Wkv", "w_o": "L0_xattn_Wo",
    "w1": "L0_ffn_W1", "b1": "L0_ffn_b1", "w2": "L0_ffn_W2", "b2": "L0_ffn_b2", "w_g": "L0_ffn_Wg", "b_g": "L0_ffn_bg",
}


def shape_constants(batches, length, width, experts):
    import numpy as np

    f32 = np.float32
    tokens, p = batches * length, 128
    rot = width // 2
    inv_freq = f32(1.0) / f32(10000.0) ** (np.arange(0, rot, 2, dtype=f32) / f32(rot))
    angle = np.repeat(np.arange(length, dtype=f32)[:, None] * inv_freq[None, :], 2, axis=-1)
    sign = np.tile(np.array([-1.0, 1.0], f32), rot // 2)
    lane = np.arange(p)
    cap = tokens + FFN_ROWS
    return {
        "rot_cos": np.tile(np.cos(angle), (p // length, 1)),
        "rot_sin": np.tile(np.sin(angle) * sign, (p // length, 1)),
        "batch_of": np.repeat(np.eye(p // length, dtype=f32), length, 0),
        "eye": np.eye(p, dtype=f32),
        "before": (lane[:, None] < lane[None, :]).astype(f32),
        "expert_ids": np.tile(np.arange(experts, dtype=f32), (p, 1)),
        "region_base": np.tile(np.arange(experts, dtype=f32) * f32(cap), (p, 1)),
        "row_ids": (lane[:, None, None] + p * np.arange(tokens // p)[None, :, None]
                    + tokens * np.arange(2)[None, None, :]).astype(np.int32),
        "tile_ids": np.arange(ffn_tiles(tokens, experts), dtype=f32)[None],
    }


def kernel(**inputs):
    import numpy as np
    import concourse.bacc as bacc
    from concourse.bass_utils import run_bass_kernel_spmd

    nc = bacc.Bacc("TRN2", target_bir_lowering=False, num_devices=1)
    arrays, args = {}, {}

    def give(name, a):
        a = np.ascontiguousarray(a)
        arrays[f"in_{name}"] = a
        args[name] = nc.dram_tensor(f"in_{name}", a.shape, mybir.dt.from_np(a.dtype), kind="ExternalInput").ap()

    for name, key in _ARGS.items():
        give(name, inputs[key])
    batches, length, width = arrays["in_x"].shape
    experts = arrays["in_w1"].shape[0]
    for name, a in shape_constants(batches, length, width, experts).items():
        give(name, a)
    tokens = batches * length
    f32 = mybir.dt.float32
    args["x_rows"] = nc.dram_tensor("x_rows", [experts * (tokens + FFN_ROWS) + FFN_ROWS, width + 2], f32, kind="Internal").ap()
    args["y_rows"] = nc.dram_tensor("y_rows", [2 * tokens, width], f32, kind="Internal").ap()
    args["out"] = nc.dram_tensor("out", [batches, length, width], f32, kind="ExternalOutput").ap()
    decoder_layer(nc, **args)
    return run_bass_kernel_spmd(nc, [arrays], core_ids=[0]).results[0]["out"]
```

```python
import concourse.bass as bass
from concourse import mybir
from contextlib import ExitStack


FFN_ROWS = 256


def ffn_tiles(tokens, experts):
    most = (2 * tokens + experts * (FFN_ROWS - 1)) // FFN_ROWS
    return -(-most // 4) * 4


def decoder_layer(nc, x, ctx_in, w_in, w_out, ln_g, ln_b, ln1_g, ln1_b, ln2_g, ln2_b,
                  w_q, w_kv, w_o, expert_w, w_g, b_g, rot_cos, rot_sin, batch_of, eye,
                  before, expert_ids, region_base, row_ids, tile_ids, x_rows, y_rows, out):
    F32 = mybir.dt.float32
    BF16 = mybir.dt.bfloat16
    I32 = mybir.dt.int32
    U32 = mybir.dt.uint32
    ALU = mybir.AluOpType
    ACT = mybir.ActivationFunctionType
    AX = mybir.AxisListType

    B, S, D = x.shape
    P = 128
    BT = P // S
    NT = B // BT
    assert NT <= 256
    HD = 64
    H = w_q.shape[1] // HD
    HH = H // 2
    UP = HH // BT
    UNITS = 4
    ROT = D // 2
    EPS_LN, EPS_L2 = 1e-5, 1e-6
    N = B * S
    E = w_g.shape[1]
    FC = (expert_w.shape[2] - D) // (2 * D + 1)
    F = FC * P
    W2_AT, B1_AT, B2_AT, W_ROW = F, F + FC * D, F + FC * (D + 1), F + FC * (D + 1) + D
    T = FFN_ROWS
    TB = T // P
    CAP = N + T
    NF = ffn_tiles(N, E)
    ROW = D + 2
    RING = 4
    ZT = 4
    NZ = NT // ZT
    QS_SCALE = 1.0 / HD ** 0.5

    x_t = x.rearrange("(t b) s d -> t (b s) d", b=BT)
    ctx_t = ctx_in.rearrange("(t b) s d -> t b s d", b=BT)
    out_z = out.rearrange("(t b) s d -> t (b s) d", b=BT)

    ctx = ExitStack()
    with ctx:
        def sb(name, shape, dt=F32):
            return ctx.enter_context(nc.sbuf_tensor(name, shape, dt))

        def pb(name):
            return ctx.enter_context(nc.psum_tensor(name, [P, 512], F32))

        def sem(name):
            return ctx.enter_context(nc.semaphore(name))

        ident = sb("ident", [P, P])
        cosb = sb("cosb", [P, ROT])
        sinb = sb("sinb", [P, ROT])
        member = sb("member", [P, BT])
        m_half = sb("m_half", [P, ZT])
        gcol = sb("gcol", [P, 1])
        bcol = sb("bcol", [P, 1])
        g_ctx = sb("g_ctx", [P, D])
        b_ctx = sb("b_ctx", [P, D])
        g_lat = sb("g_lat", [P, D])
        b_lat = sb("b_lat", [P, D])
        winT = sb("winT", [P, 3 * D])
        woutT = sb("woutT", [P, D])
        score_w = sb("score_w", [P, H, D])
        value_w = sb("value_w", [P, H, D])
        win_raw = sb("win_raw", [P, 3, D])
        wout_raw = sb("wout_raw", [P, D])
        wq_raw = sb("wq_raw", [P, H * HD])
        wkv_raw = sb("wkv_raw", [P, 2 * H * HD])
        wo_raw = sb("wo_raw", [P, H // 2, D])
        wqT = sb("wqT", [P, H // 2, D])
        wkT = sb("wkT", [P, H // 2, D])
        wvT = sb("wvT", [P, H // 2, D])

        x_raw = sb("x_raw", [P, 2, D])
        c_raw = sb("c_raw", [P, 2, D])
        st_in = sb("st_in", [P, 2, 2, 6])
        mv_in = sb("mv_in", [P, 2, 2, 2])
        ve_in = sb("ve_in", [P, 2, 2])
        rs_in = sb("rs_in", [P, 2, 2])
        x_hat = sb("x_hat", [P, 2, D])
        c_hat = sb("c_hat", [P, 2, D])
        xnT = sb("xnT", [P, 2, D])
        qkv = sb("qkv", [P, 2, 3 * D])
        sq_junk = sb("sq_junk", [P, 2, D])
        ss_qk = sb("ss_qk", [P, 2, 2])
        se_qk = sb("se_qk", [P, 2, 2])
        rs_qk = sb("rs_qk", [P, 2, 2])
        turned = sb("turned", [P, 2, 2, ROT])
        kv_prod = sb("kv_prod", [P, 2, D])
        k_pick = sb("k_pick", [P, 2, BT])
        yT = sb("yT", [P, 2, P])
        attn_o = sb("attn_o", [P, 2, D])
        z1 = sb("z1", [P, 2, D])
        x1s = sb("x1s", [P, 2, D])
        st_z1 = sb("st_z1", [P, 2, 6])
        mv_z1 = sb("mv_z1", [P, 2, 2])
        ve_z1 = sb("ve_z1", [P, 2, 1])
        rs_z1 = sb("rs_z1", [P, 2, 1])
        st_x1 = sb("st_x1", [P, 2, 6])
        mv_x1 = sb("mv_x1", [P, 2, 2])
        ve_x1 = sb("ve_x1", [P, 2, 1])
        rs_x1 = sb("rs_x1", [P, 2, 1])
        l_hat = sb("l_hat", [P, 2, D])
        l_scaled = sb("l_scaled", [P, 2, D])
        c_scaled = sb("c_scaled", [P, 2, D])
        l_rows = sb("l_rows", [P, 2, D])
        c_rows = sb("c_rows", [P, 2, D])
        kv_rows = sb("kv_rows", [P, 2, BT, D])
        kvT = sb("kvT", [P, 2, 4, S])
        u_sb = sb("u_sb", [P, 2, BT, H, S])
        tT = sb("tT", [P, 2, H, P])
        z2 = sb("z2", [P, 2, D])
        st_z2 = sb("st_z2", [P, 2, 6])
        mv_z2 = sb("mv_z2", [P, 2, 2])
        ve_z2 = sb("ve_z2", [P, 2, 1])
        rs_z2 = sb("rs_z2", [P, 2, 1])
        neg_max = sb("neg_max", [P, 2, UP])
        probs = sb("probs", [P, 2, UP, P])
        sums = sb("sums", [P, 2, UP])
        inv_sum = sb("inv_sum", [P, 2, UP])
        probs_n = sb("probs_n", [P, 2, UP, P])
        pT = sb("pT", [P, 2, UP * P])
        x2s = sb("x2s", [P, 2, D])
        x2T = sb("x2T", [P, 2, P])
        wg_sb = sb("wg_sb", [P, E])
        bg_sb = sb("bg_sb", [P, E])
        tri = sb("tri", [P, P])
        tri_bf = sb("tri_bf", [P, P], BF16)
        ones = sb("ones", [P, P], BF16)
        ones_row = sb("ones_row", [1, E])
        eids = sb("eids", [P, E])
        rbase = sb("rbase", [P, E])
        rids = sb("rids", [P, NT, 2], I32)
        tids = sb("tids", [1, NF])
        logits = sb("logits", [P, 2, E])
        lmax = sb("lmax", [P, 2, 1])
        gexp = sb("gexp", [P, 2, E])
        gsum = sb("gsum", [P, 2, 1])
        ginv = sb("ginv", [P, 2, 1])
        gprob = sb("gprob", [P, 2, E])
        top = sb("top", [P, 2, 8])
        top_at = sb("top_at", [P, 2, 8], U32)
        top_atf = sb("top_atf", [P, 2, 2])
        den = sb("den", [P, 2, 1])
        den_g = sb("den_g", [P, 2, 1])
        den_i = sb("den_i", [P, 2, 1])
        picked = sb("picked", [P, 2, 2, E])
        mask = sb("mask", [P, 2, E], BF16)
        seen = sb("seen", [P, 2, E], BF16)
        pos_all = sb("pos_all", [P, 2, E])
        pos_sel = sb("pos_sel", [P, 2, 2, E])
        pos_f = sb("pos_f", [P, 2, 2])
        pos_i = sb("pos_i", [P, 2, 2], I32)
        routed = sb("routed", [P, 2, 2, ROW])
        pad_row = sb("pad_row", [P, ROW])
        rows = sb("rows", [P, NT, D])

        cnt_up = sb("cnt_up", [1, E])
        cnt_i = sb("cnt_i", [1, E], I32)
        nt_i = sb("nt_i", [1, E], I32)
        nt_f = sb("nt_f", [1, E])
        cum_nt = sb("cum_nt", [1, E])
        pad_f = sb("pad_f", [1, E])
        pad_i = sb("pad_i", [1, E], I32)
        past = sb("past", [1, NF, E])
        past_nt = sb("past_nt", [1, NF, E])
        ex_f = sb("ex_f", [1, NF])
        start_f = sb("start_f", [1, NF])
        valid_f = sb("valid_f", [1, NF])
        blk_f = sb("blk_f", [1, NF])
        blk_v = sb("blk_v", [1, NF])
        base_f = sb("base_f", [1, NF])
        exw_f = sb("exw_f", [1, NF])
        base_i = sb("base_i", [1, NF], I32)
        exw_i = sb("exw_i", [1, NF], I32)
        u_flat = u_sb[:].rearrange("p q b h s -> p (q b h s)")
        t_flat = tT[:].rearrange("p q h s -> p (q h s)")
        f_w = [t_flat[:, q * W_ROW:(q + 1) * W_ROW] for q in range(RING - 1)] + [u_flat[:, 0:W_ROW]]
        f_x = sb("f_x", [P, RING, TB, ROW])
        f_id = sb("f_id", [P, RING, TB])
        f_xT = sb("f_xT", [P, 2, T])
        f_h = wkv_raw[:].rearrange("p (q c t) -> p q c t", q=2, t=T)
        f_yb = sb("f_yb", [P, 2, TB, D])
        f_y = wvT[:].rearrange("p (q b) d -> p q b d", q=RING)
        e_y = t_flat.rearrange("p (q s c d) -> p q s c d", q=RING, s=2, c=ZT)
        e_parts = u_flat.rearrange("p (q c d) -> p q c d", c=ZT, d=D)
        e_z, e_sum, e_out = e_parts[:, 0:RING], e_parts[:, RING:RING + 2], e_parts[:, RING + 2:RING + 4]
        e_st = sb("e_st", [P, RING, ZT, 6])
        e_mv = sb("e_mv", [P, RING, ZT, 2])
        e_ve = sb("e_ve", [P, RING, ZT])
        e_rs = sb("e_rs", [P, RING, ZT])
        e_nm = sb("e_nm", [P, RING, ZT])
        eps_ln = sb("eps_ln", [P, ZT])
        eps_l2 = sb("eps_l2", [P, ZT])

        ps_s = [pb("ps_s0"), pb("ps_s1")]
        ps_pT = pb("ps_pT")
        ps_t = pb("ps_t")
        ps_u = pb("ps_u")
        ps_o = pb("ps_o")
        ps_a = pb("ps_a")
        ps_b = pb("ps_b")
        A_QKV = ps_a[:, 0:3 * D]
        A_XT = ps_a[:, 384:512]
        A_QT = ps_a[:, 0:P]
        A_AT = ps_a[:, P:P + BT]
        A_O = ps_a[:, 256:384]
        B_XT = ps_b[:, 0:P]
        B_RANK = ps_b[:, 128:128 + E]
        B_GATE = ps_b[:, 144:144 + E]
        F_XT = [ps_o[:, 0:T], ps_a[:, 0:T]]
        F_H = [ps_s, [ps_pT, ps_b]]
        F_Y = [ps_t[:, 0:TB * D], ps_u[:, 0:TB * D]]
        KVT = ps_u[:, 0:BT * P]

        s_const = sem("s_const")
        s_gains = sem("s_gains")
        s_ident = sem("s_ident")
        s_win = sem("s_win")
        s_wq = sem("s_wq")
        s_wkv = sem("s_wkv")
        s_wo = sem("s_wo")
        half_set = sem("half_set")
        win_kept = sem("win_kept")
        prep_ps = sem("prep_ps")
        prep_act = sem("prep_act")
        prep_dve = sem("prep_dve")
        x_in = [sem("x_in0"), sem("x_in1")]
        c_in = [sem("c_in0"), sem("c_in1")]
        names = """in_stats in_moments in_eps in_rstd x_hat_done c_hat_done xT_ps xnT_done qkv_ps qkv_done sq_done
        qk_eps qk_rstd rot_turned rot_cosed rot_done kvp_done pick_done at_ps yT_done wo_ps attn_done
        z1_done z1_stats z1_moments z1_eps z1_rstd x1_done x1_stats x1_moments x1_eps x1_rstd l_hat_done
        l_scaled_done c_scaled_done kv_done kv_kept kvT_ps kvT_done u_ps u_done s_ps max_done exp_done inv_done p_done pT_ps pT_done
        t_ps t_done o_ps z2_done z2_stats z2_moments z2_eps z2_rstd x2_done
        x1_kept x2s_done x2T_ps x2T_done gate_ps logits_done lmax_done gexp_done ginv_done gprob_done top_done top_at_done den_done den_g_done den_i_done
        weight_done atf_done picked_done mask_done seen_done rows_kept rids_kept rank_ps pos_all_done pos_sel_done pos_f_done
        pos_done pad_set pad_ready cnt_ps tab tab_base tab_ready f_xT_ps f_xT_done f_h_ps f_h_done f_y_ps f_yb_done f_id_done f_y_done
        e_sum_done e_z_done e_stats e_moments e_eps e_rstd e_nm_done e_out_done""".split()
        (in_stats, in_moments, in_eps, in_rstd, x_hat_done, c_hat_done, xT_ps, xnT_done, qkv_ps, qkv_done, sq_done,
         qk_eps, qk_rstd, rot_turned, rot_cosed, rot_done, kvp_done, pick_done, at_ps, yT_done, wo_ps, attn_done,
         z1_done, z1_stats, z1_moments, z1_eps, z1_rstd, x1_done, x1_stats, x1_moments, x1_eps, x1_rstd, l_hat_done,
         l_scaled_done, c_scaled_done, kv_done, kv_kept, kvT_ps, kvT_done, u_ps, u_done, s_ps, max_done, exp_done, inv_done,
         p_done, pT_ps, pT_done, t_ps, t_done, o_ps, z2_done, z2_stats, z2_moments, z2_eps, z2_rstd,
         x2_done, x1_kept, x2s_done, x2T_ps, x2T_done, gate_ps, logits_done, lmax_done, gexp_done, ginv_done, gprob_done,
         top_done, top_at_done, den_done, den_g_done, den_i_done, weight_done, atf_done, picked_done, mask_done, seen_done, rows_kept,
         rids_kept, rank_ps, pos_all_done, pos_sel_done, pos_f_done, pos_done, pad_set, pad_ready, cnt_ps, tab, tab_base,
         tab_ready, f_xT_ps, f_xT_done, f_h_ps, f_h_done, f_y_ps, f_yb_done, f_id_done, f_y_done, e_sum_done, e_z_done, e_stats,
         e_moments, e_eps, e_rstd, e_nm_done, e_out_done) = [sem(n) for n in names]
        s_out = [sem("s_out0"), sem("s_out1")]
        x_routed = [sem("x_routed0"), sem("x_routed1")]
        pad_filled = sem("pad_filled")
        f_in = [sem(f"f_in{q}") for q in range(RING)]
        fw_in = [sem(f"fw_in{q}") for q in range(RING)]
        y_routed = [sem(f"y_routed{q}") for q in range(RING)]
        e_in = [sem(f"e_in{q}") for q in range(RING)]

        def count(n):
            return max(n, 0) if isinstance(n, int) else n

        def settle(eng):
            eng.nop(nofuse=True)

        FIRST, LAST = -3, NT + 4

        def periods(eng, period):
            lo = 6
            pairs = (NT - 4 - lo) // 2
            hi = lo + 2 * pairs
            for t in range(FIRST, lo):
                period(t, t % 2)
            with eng.Fori(0, pairs) as i:
                for half in range(2):
                    period(i * 2 + (lo + half), (lo + half) % 2)
            for t in range(hi, LAST + 1):
                period(t, t % 2)

        def turns(eng, n, step, by, tail=0):
            for i in range(by):
                step(i, i)
            if n - tail > by:
                with eng.Fori(1, (n - tail) // by) as i:
                    for q in range(by):
                        step(i * by + q, q)
            for i in range(n - tail, n):
                step(i, i % by)

        def on(t, lag):
            return not isinstance(t, int) or 0 <= t + lag < NT

        def unit_on(t, k):
            return not isinstance(t, int) or 0 <= 4 * t + k < UNITS * NT

        def one(t):
            return bass.ds(t, 1)

        banks = [ps_s[0], ps_s[1], ps_pT, ps_b, ps_t, ps_u, ps_o]
        def turned_jobs(raw, lo, dst):
            return [("t", [raw[:, lo + (4 * g + c) * P:lo + (4 * g + c + 1) * P] for c in range(4)],
                     dst[:, 4 * g:4 * g + 4].rearrange("p c d -> p (c d)")) for g in range(2)]

        def product_jobs(kind, dst):
            return [(kind, g, dst[:].rearrange("p (c r) d -> p c r d", r=2)[:, 4 * (g // 2):4 * (g // 2) + 4, g % 2])
                    for g in range(4)]

        jobs = [("in", [win_raw[:, c] for c in range(3)] + [wout_raw[:]], None)]
        jobs += turned_jobs(wq_raw, 0, wqT) + turned_jobs(wkv_raw, 0, wkT) + turned_jobs(wkv_raw, H * HD, wvT)
        TURNED = len(jobs)
        jobs += product_jobs("m", score_w) + product_jobs("v", value_w)
        BANKS = len(banks)

        def prep_kept(at):
            return (prep_act, prep_dve)[at % 2], at // 2 + 1

        block = ctx.enter_context(nc.Block())

        N_CONST, N_GAINS = 10, 6

        @block.sync
        def _(sp):
            def load(j, q):
                sp.wait_ge(z1_done, count(j - 1))
                sp.wait_ge(c_hat_done, count(j - 1))
                sp.dma_start(x_raw[:, q:q + 1, :], x_t[one(j), :, :].rearrange("t p d -> p t d")).then_inc(x_in[q], 16)
                sp.dma_start(c_raw[S:P, q:q + 1, :],
                             ctx_t[one(j), 0, :, :].rearrange("t s d -> s t d")).then_inc(c_in[q], 16)
                sp.dma_start(c_raw[0:S, q:q + 1, :],
                             ctx_t[one(j), 1, :, :].rearrange("t s d -> s t d")).then_inc(c_in[q], 16)

            sp.dma_start(ident[:], eye).then_inc(s_ident, 16)
            sp.dma_start(wq_raw[:], w_q).then_inc(s_wq, 16)
            sp.dma_start(wkv_raw[:], w_kv).then_inc(s_wkv, 16)
            load(0, 0)
            sp.dma_start(wo_raw[:], w_o.rearrange("(c p) n -> p c n", p=P)).then_inc(s_wo, 16)
            sp.dma_start(tri[:], before).then_inc(s_const, 16)
            sp.dma_start(eids[:], expert_ids).then_inc(s_const, 16)
            sp.dma_start(rbase[:], region_base).then_inc(s_const, 16)
            sp.dma_start(rids[:], row_ids).then_inc(s_const, 16)
            sp.dma_start(tids[:], tile_ids).then_inc(s_const, 16)

            sp.wait_ge(pad_ready, 2)
            pad_rows = pad_row[:].rearrange("p (o d) -> p o d", o=1).to_broadcast([P, TB, ROW])
            sp.dma_start(x_rows[E * CAP:E * CAP + T, :].rearrange("(b p) d -> p b d", p=P), pad_rows).then_inc(pad_filled, 16)

            def period(t, p):
                q = (p + 4) % 2
                if on(t, 4):
                    j = t + 4
                    m = (j - q) // 2 if isinstance(t, int) else None
                    load(j, q)

            periods(sp, period)

            sp.wait_ge(tab_ready, 1)
            for e in range(E):
                at = sp.value_load(pad_i[0:1, e:e + 1], min_val=0, max_val=E * CAP - T)
                sp.dma_start(x_rows[bass.ds(at, T), :].rearrange("(b p) d -> p b d", p=P), pad_rows).then_inc(pad_filled, 16)

            def weights(i, q):
                e = sp.value_load(exw_i[0:1, bass.ds(i, 1)], min_val=0, max_val=E - 1)
                sp.wait_ge(f_y_ps, count(i - (RING - 1)))
                settle(sp)
                sp.wait_ge(f_yb_done, count(i - (RING - 1)))
                settle(sp)
                sp.dma_start(f_w[q].rearrange("p (o f) -> p o f", o=1),
                             expert_w[bass.ds(e, 1), :, :].rearrange("e p f -> p e f")).then_inc(fw_in[q], 16)

            def ffn(i, q):
                if not isinstance(i, int) or i >= RING:
                    weights(i, q)
                base = sp.value_load(base_i[0:1, bass.ds(i, 1)], min_val=0, max_val=E * CAP)
                sp.wait_ge(f_y_done, count(TB * i - TB * (RING - 1)))
                settle(sp)
                sp.wait_ge(f_id_done, count(i - (RING - 1)))
                settle(sp)
                sp.dma_start(f_x[:, q], x_rows[bass.ds(base, T), :].rearrange("(b p) d -> p b d", p=P)).then_inc(f_in[q], 16)

            sp.wait_ge(tab_ready, 2)
            for i in range(RING):
                weights(i, i)
            for s in x_routed:
                sp.wait_ge(s, 16 * NT)
            sp.wait_ge(pad_filled, 16 * (E + 1))
            turns(sp, NF, ffn, RING)
            for s in y_routed:
                sp.wait_ge(s, 16 * TB * (NF // RING))

            def last_in(g, q):
                sp.wait_ge(e_sum_done, count(g - (RING - 1)))
                for sl in range(2):
                    sp.dma_start(e_y[:, q, sl],
                                 y_rows[bass.ds(g * (ZT * P) + sl * N, ZT * P), :].rearrange("(c p) d -> p c d", p=P)
                                 ).then_inc(e_in[q], 16)

            turns(sp, NZ, last_in, RING)
            for q in range(2):
                sp.wait_ge(s_out[q], 16 * (NZ // 2))

        def half_count(t, p, lag, per):
            if isinstance(t, int):
                return per * ((t + lag) // 2 + 1)
            return (t + (lag - (p + lag) % 2 + 2)) * (per // 2)

        @block.gpsimd
        def _(pool):
            nc.gpsimd.memset(m_half[:], -0.5).then_inc(half_set, 1)
            nc.gpsimd.memset(eps_ln[:], EPS_LN).then_inc(half_set, 1)
            nc.gpsimd.memset(eps_l2[:], EPS_L2).then_inc(half_set, 1)
            for dst, src in ((g_ctx, ln1_g), (b_ctx, ln1_b), (g_lat, ln2_g), (b_lat, ln2_b)):
                pool.dma_start(dst[:], src.rearrange("(o d) -> o d", o=1).to_broadcast([P, D])).then_inc(s_gains, 16)
            pool.dma_start(wg_sb[:], w_g).then_inc(s_gains, 16)
            pool.dma_start(bg_sb[:], b_g.rearrange("(o d) -> o d", o=1).to_broadcast([P, E])).then_inc(s_gains, 16)

            def rstd(var, ve, rs, eps, moments, n_moments, eps_done, rstd_done, j):
                pool.wait_ge(moments, n_moments)
                nc.gpsimd.tensor_tensor(ve, var, eps[:, 0:var.shape[-1]], ALU.add).then_inc(eps_done, 1)
                pool.wait_ge(eps_done, j + 1)
                nc.gpsimd.tensor_tensor(rs, ve, m_half[:, 0:rs.shape[-1]], ALU.pow).then_inc(rstd_done, 1)

            def scale(t, k):
                n, sl = t * 4 + k, k % 2
                pool.wait_ge(inv_done, n + 1)
                pool.wait_ge(pT_ps, count(n - 1))
                nc.gpsimd.tensor_tensor(
                    probs_n[:, sl], probs[:, sl],
                    inv_sum[:, sl, :].rearrange("p (u o) -> p u o", o=1).to_broadcast([P, UP, P]),
                    ALU.mult).then_inc(p_done, 1)

            def route(j, q, sl):
                pool.wait_ge(rows_kept, j + 1)
                pool.wait_ge(rids_kept, j + 1)
                pool.wait_ge(weight_done, j + 1)
                pool.wait_ge(pos_done, j + 1)
                settle(pool)
                pool.indirect_dma_start(
                    out=x_rows, out_offset=bass.IndirectOffsetOnAxis(ap=pos_i[:, q, sl:sl + 1].bitcast(U32), axis=0),
                    in_=routed[:, q, sl], in_offset=None, bounds_check=E * CAP - 1,
                    oob_is_err=False).then_inc(x_routed[q], 16)

            def period(t, p):
                p3, p2 = (p + 3) % 2, p
                for k in range(UNITS):
                    if k == 0 and on(t, -2):
                        rstd(mv_z2[:, p, 1:2], ve_z2[:, p], rs_z2[:, p], eps_ln, z2_moments, t - 1, z2_eps, z2_rstd, t - 2)
                    if on(t, 0):
                        scale(t, k)
                    if k == 0 and on(t, 3):
                        rstd(mv_in[:, p3, :, 1], ve_in[:, p3], rs_in[:, p3], eps_ln, in_moments, 2 * t + 8, in_eps, in_rstd, t + 3)
                    if k == 0 and on(t, 2):
                        rstd(mv_z1[:, p2, 1:2], ve_z1[:, p2], rs_z1[:, p2], eps_ln, z1_moments, t + 3, z1_eps, z1_rstd, t + 2)
                    if k == 1 and on(t, 2):
                        rstd(mv_x1[:, p2, 1:2], ve_x1[:, p2], rs_x1[:, p2], eps_ln, x1_moments, t + 3, x1_eps, x1_rstd, t + 2)
                    if k == 2 and on(t, 2):
                        pool.wait_ge(l_hat_done, t + 3)
                        nc.gpsimd.tensor_tensor(l_scaled[:, p2], l_hat[:, p2], g_lat[:], ALU.mult).then_inc(l_scaled_done, 1)
                        pool.wait_ge(c_hat_done, t + 3)
                        nc.gpsimd.tensor_tensor(c_scaled[:, p2], c_hat[:, p2], g_ctx[:], ALU.mult).then_inc(c_scaled_done, 1)
                        pool.wait_ge(kv_kept, count(4 * t + 4))
                        pool.wait_ge(l_scaled_done, t + 3)
                        nc.gpsimd.tensor_tensor(l_rows[:, p2], l_scaled[:, p2], b_lat[:], ALU.add).then_inc(kv_done, 1)
                        pool.wait_ge(c_scaled_done, t + 3)
                        nc.gpsimd.tensor_tensor(c_rows[:, p2], c_scaled[:, p2], b_ctx[:], ALU.add).then_inc(kv_done, 1)
                    if k == 2 and on(t, 3):
                        rstd(ss_qk[:, p3], se_qk[:, p3], rs_qk[:, p3], eps_l2, sq_done, 2 * t + 8, qk_eps, qk_rstd, t + 3)
                    if k == 3 and on(t, -4):
                        route(t - 4, p, 0)
                    if k == 1 and on(t, -5):
                        route(t - 5, 1 - p, 1)

            pool.wait_ge(half_set, 3)
            pool.wait_ge(s_const, 16 * N_CONST)
            pool.wait_ge(s_gains, 16 * N_GAINS)
            periods(pool, period)

            def ffn(i, q):
                pool.wait_ge(f_y_done, TB * (i + 1))
                settle(pool)
                pool.wait_ge(f_id_done, i + 1)
                for b in range(TB):
                    settle(pool)
                    pool.indirect_dma_start(
                        out=y_rows, out_offset=bass.IndirectOffsetOnAxis(ap=f_id[:, q, b:b + 1].bitcast(U32), axis=0),
                        in_=f_y[:, q, b], in_offset=None, bounds_check=2 * N - 1, oob_is_err=False).then_inc(y_routed[q], 16)

            turns(pool, NF, ffn, RING)

            def last(g, q):
                if not isinstance(g, int) or g < NZ:
                    pool.wait_ge(e_in[q], (g + (RING - q)) * (32 // RING))
                    pool.wait_ge(e_z_done, count(g - 1))
                    nc.gpsimd.tensor_tensor(e_sum[:, q % 2], e_y[:, q, 0], e_y[:, q, 1], ALU.add).then_inc(e_sum_done, 1)
                if not isinstance(g, int) or g:
                    o = (q - 1) % RING
                    rstd(e_mv[:, o, :, 1], e_ve[:, o], e_rs[:, o], eps_ln, e_moments, ZT * g, e_eps, e_rstd, g - 1)

            turns(pool, NZ, last, RING)
            last(NZ, 0)

        @block.scalar
        def _(act):
            act.dma_start(win_raw[:], w_in.rearrange("(c p) d -> p c d", p=P)).then_inc(s_win, 16)
            act.dma_start(wout_raw[:], w_out).then_inc(s_win, 16)
            act.dma_start(gcol[:], ln_g.rearrange("(p o) -> p o", o=1)).then_inc(s_const, 16)
            act.dma_start(bcol[:], ln_b.rearrange("(p o) -> p o", o=1)).then_inc(s_const, 16)
            act.dma_start(cosb[:], rot_cos).then_inc(s_const, 16)
            act.dma_start(sinb[:], rot_sin).then_inc(s_const, 16)
            act.dma_start(member[:], batch_of).then_inc(s_const, 16)

            for at in range(0, len(jobs), 2):
                kind, _, dst = jobs[at]
                bank = banks[at % BANKS]
                act.wait_ge(prep_ps, at + 1)
                if kind == "in":
                    nc.scalar.activation(winT[:], bank[:, 0:3 * D], ACT.Copy).then_inc(win_kept, 1)
                    nc.scalar.activation(woutT[:], bank[:, 3 * D:4 * D], ACT.Copy).then_inc(prep_act, 1)
                elif kind == "t":
                    nc.scalar.activation(dst, bank[:], ACT.Copy).then_inc(prep_act, 1)
                else:
                    nc.scalar.activation(dst, bank[:].rearrange("p (c d) -> p c d", c=4), ACT.Copy,
                                         scale=QS_SCALE if kind == "m" else 1.0).then_inc(prep_act, 1)

            act.wait_ge(s_const, 16 * N_CONST)
            act.wait_ge(s_gains, 16 * N_GAINS)

            def exps(t, k):
                n, sl = t * 4 + k, k % 2
                act.wait_ge(max_done, n + 1)
                act.wait_ge(p_done, count(n - 1))
                for j in range(UP):
                    last = nc.scalar.activation(probs[:, sl, j], ps_s[sl][:, j * P:(j + 1) * P], ACT.Exp,
                                                bias=neg_max[:, sl, j:j + 1], accum_out=sums[:, sl, j:j + 1])
                last.then_inc(exp_done, 1)

            def keep_t(t, k, p):
                n = t * 4 + (k - 2)
                kk = (k - 2) % 4
                pp = p if k > 1 else (p + 1) % 2
                b, hf = kk // 2, kk % 2
                act.wait_ge(t_ps, n + 1)
                nc.scalar.activation(tT[:, pp, hf * HH:(hf + 1) * HH, b * S:(b + 1) * S],
                                     ps_t[:].rearrange("p (h q) -> p h q", q=S), ACT.Copy).then_inc(t_done, 1)

            def period(t, p):
                p3, p2, p1 = (p + 3) % 2, p, (p + 1) % 2
                for k in range(UNITS):
                    if on(t, 0):
                        exps(t, k)
                    if k == 0 and unit_on(t, -2):
                        keep_t(t, 0, p)
                    if k == 0 and on(t, 2):
                        act.wait_ge(wo_ps, t + 3)
                        act.wait_ge(qk_rstd, t + 3)
                        nc.scalar.activation(attn_o[:, p2], A_O, ACT.Copy, scale=rs_qk[:, p2, 0:1]).then_inc(attn_done, 1)
                    if k == 2 and on(t, 3):
                        act.wait_ge(qkv_ps, t + 4)
                        nc.scalar.activation(qkv[:, p3], A_QKV, ACT.Copy).then_inc(qkv_done, 1)
                        for j in range(2):
                            nc.scalar.activation(sq_junk[:, j], A_QKV[:, j * D:(j + 1) * D], ACT.Square,
                                                 accum_out=ss_qk[:, p3, j:j + 1]).then_inc(sq_done, 1)
                    if on(t, 1):
                        act.wait_ge(u_ps, 4 * t + (4 + k + 1))
                        nc.scalar.activation(u_sb[:, p1, :, 4 * k:4 * k + 4, :].rearrange("p b h s -> p h b s"),
                                             ps_u[:].rearrange("p (h b s) -> p h b s", b=BT, s=S), ACT.Copy).then_inc(u_done, 1)
                    if k == 1 and on(t, -3):
                        act.wait_ge(lmax_done, t - 2)
                        nc.scalar.activation(gexp[:, p3], logits[:, p3], ACT.Exp, bias=lmax[:, p3, 0:1],
                                             accum_out=gsum[:, p3, 0:1]).then_inc(gexp_done, 1)
                    if k == 3 and on(t, -2):
                        act.wait_ge(x2T_ps, t - 1)
                        nc.scalar.activation(x2T[:, p], B_XT, ACT.Copy).then_inc(x2T_done, 1)
                    if k and unit_on(t, k - 2):
                        keep_t(t, k, p)
                    if k == 1 and on(t, 3):
                        act.wait_ge(xT_ps, t + 4)
                        nc.scalar.activation(xnT[:, p3], A_XT, ACT.Identity, scale=gcol[:, 0:1],
                                             bias=bcol[:, 0:1]).then_inc(xnT_done, 1)
                    if k == 3 and on(t, 2):
                        act.wait_ge(kvT_ps, t + 3)
                        nc.scalar.activation(kvT[:, p2, 1:3], KVT[:, 0:P].rearrange("p (b s) -> p b s", b=BT), ACT.Copy).then_inc(kvT_done, 1)
                        nc.scalar.activation(kvT[:, p2, 0:4:3], KVT[:, P:2 * P].rearrange("p (b s) -> p b s", b=BT), ACT.Copy).then_inc(kvT_done, 1)

            periods(act, period)

            def ffn(i, q):
                act.wait_ge(fw_in[q], (i + (RING - q)) * (16 // RING))
                for c in range(FC):
                    act.wait_ge(f_h_ps, i * (FC // 2) + (c // 2 + 1))
                    if c == 0:
                        act.wait_ge(f_y_ps, count(i - 1))
                    nc.scalar.activation(f_h[:, q % 2, c], F_H[q % 2][c // 2][:, (c % 2) * T:(c % 2 + 1) * T], ACT.Gelu,
                                         bias=f_w[q][:, B1_AT + c:B1_AT + c + 1]).then_inc(f_h_done, 1)

            turns(act, NF, ffn, RING)

            def last(g, q):
                act.wait_ge(e_nm_done, g + 1)
                act.wait_ge(s_out[q % 2], (g - q % 2) * 8)
                for c in range(ZT):
                    nc.scalar.activation(e_out[:, q % 2, c], e_z[:, q, c], ACT.Identity, scale=e_rs[:, q, c:c + 1],
                                         bias=e_nm[:, q, c:c + 1]).then_inc(e_out_done, 1)
                act.wait_ge(e_out_done, ZT * g + ZT)
                settle(act)
                act.dma_start(out_z[bass.ds(g * ZT, ZT), :, :].rearrange("t p d -> p t d"),
                              e_out[:, q % 2]).then_inc(s_out[q % 2], 16)

            turns(act, NZ, last, RING)

        @block.vector
        def _(dve):
            nc.vector.memset(pad_row[:, 0:D + 1], 0.0).then_inc(pad_ready, 1)
            nc.vector.memset(pad_row[:, D + 1:D + 2].bitcast(I32), 2 * N).then_inc(pad_ready, 1)
            nc.vector.memset(ones[:], 1.0).then_inc(pad_ready, 1)
            nc.vector.memset(ones_row[:], 1.0).then_inc(pad_ready, 1)
            nc.vector.memset(seen[:, 0], 0.0).then_inc(seen_done, 1)
            for at in range(1, len(jobs), 2):
                kind, _, dst = jobs[at]
                bank = banks[at % BANKS]
                dve.wait_ge(prep_ps, at + 1)
                if kind == "t":
                    nc.vector.tensor_copy(dst, bank[:]).then_inc(prep_dve, 1)
                else:
                    nc.vector.tensor_scalar(dst, bank[:].rearrange("p (c d) -> p c d", c=4),
                                            QS_SCALE if kind == "m" else 1.0, None, ALU.mult).then_inc(prep_dve, 1)

            dve.wait_ge(s_const, 16 * N_CONST)
            dve.wait_ge(s_gains, 16 * N_GAINS)
            nc.vector.tensor_copy(tri_bf[:], tri[:]).then_inc(pad_ready, 1)

            def period(t, p):
                p3, p2, p1 = (p + 3) % 2, p, (p + 1) % 2

                def row_max(k):
                    n, sl = t * 4 + k, k % 2
                    dve.wait_ge(s_ps, n + 1)
                    dve.wait_ge(exp_done, count(n - 1))
                    nc.vector.tensor_reduce(neg_max[:, sl], ps_s[sl][:].rearrange("p (u k) -> p u k", k=P),
                                            axis=AX.X, op=ALU.max, negate=True).then_inc(max_done, 1)

                def inverse_sum(k):
                    n, sl = t * 4 + k, k % 2
                    dve.wait_ge(exp_done, n + 1)
                    nc.vector.reciprocal(inv_sum[:, sl], sums[:, sl]).then_inc(inv_done, 1)

                def keep_pT(k):
                    m, ss = t * 4 + (k - 1), (k - 1) % 2
                    dve.wait_ge(pT_ps, m + 1)
                    dve.wait_ge(t_ps, count(m - 1))
                    nc.vector.tensor_copy(pT[:, ss], ps_pT[:]).then_inc(pT_done, 1)

                def in_sums():
                    dve.wait_ge(x_in[p3], half_count(t, p, 3, 16))
                    settle(dve)
                    nc.vector.bn_stats(st_in[:, p3, 0], x_raw[:, p3]).then_inc(in_stats, 1)
                    dve.wait_ge(c_in[p3], half_count(t, p, 3, 32))
                    settle(dve)
                    nc.vector.bn_stats(st_in[:, p3, 1], c_raw[:, p3]).then_inc(in_stats, 1)

                def in_mean(j):
                    dve.wait_ge(in_stats, 2 * t + (7 + j))
                    settle(dve)
                    nc.vector.bn_aggr(mv_in[:, p3, j], st_in[:, p3, j]).then_inc(in_moments, 1)

                def in_hats():
                    dve.wait_ge(in_rstd, t + 4)
                    nc.vector.tensor_scalar(x_hat[:, p3], x_raw[:, p3], mv_in[:, p3, 0, 0:1], rs_in[:, p3, 0:1],
                                            ALU.subtract, ALU.mult).then_inc(x_hat_done, 1)
                    nc.vector.tensor_scalar(c_hat[:, p3], c_raw[:, p3], mv_in[:, p3, 1, 0:1], rs_in[:, p3, 1:2],
                                            ALU.subtract, ALU.mult).then_inc(c_hat_done, 1)

                qk = qkv[:, p3, 0:2 * D].rearrange("p (w d) -> p w d", w=2)[:, :, 0:ROT]

                def rot_turn():
                    pairs = qk.rearrange("p w (i two) -> p w i two", two=2)
                    trn = turned[:, p3].rearrange("p w (i two) -> p w i two", two=2)
                    sn = sinb[:].rearrange("p (o i two) -> p o i two", o=1, two=2)
                    dve.wait_ge(qkv_done, t + 4)
                    for j in range(2):
                        nc.vector.tensor_tensor(trn[:, :, :, j], pairs[:, :, :, 1 - j],
                                                sn[:, :, :, j].to_broadcast([P, 2, ROT // 2]), ALU.mult).then_inc(rot_turned, 1)

                def rot_cos_part():
                    dve.wait_ge(rot_turned, 2 * t + 8)
                    nc.vector.tensor_tensor(qk, qk, cosb[:].rearrange("p (o d) -> p o d", o=1).to_broadcast([P, 2, ROT]),
                                            ALU.mult).then_inc(rot_cosed, 1)

                def rot_add():
                    dve.wait_ge(rot_cosed, t + 4)
                    nc.vector.tensor_tensor(qk, qk, turned[:, p3], ALU.add).then_inc(rot_done, 1)

                def pick_keys():
                    dve.wait_ge(qk_rstd, t + 4)
                    nc.vector.tensor_scalar(k_pick[:, p3], member[:], rs_qk[:, p3, 1:2], None, ALU.mult).then_inc(pick_done, 1)

                def kv_product():
                    dve.wait_ge(rot_done, t + 4)
                    nc.vector.tensor_tensor(kv_prod[:, p3], qkv[:, p3, D:2 * D], qkv[:, p3, 2 * D:3 * D],
                                            ALU.mult).then_inc(kvp_done, 1)

                def scale_queries():
                    dve.wait_ge(at_ps, t + 4)
                    for b in range(BT):
                        nc.vector.tensor_scalar(yT[:, p3, b * S:(b + 1) * S], A_QT[:, b * S:(b + 1) * S],
                                                A_AT[:, b:b + 1], None, ALU.mult).then_inc(yT_done, 1)

                def z1_sum():
                    dve.wait_ge(attn_done, t + 3)
                    nc.vector.scalar_tensor_tensor(z1[:, p2], x_raw[:, p2], 2.0, attn_o[:, p2], ALU.mult, ALU.add).then_inc(z1_done, 1)

                def z1_sums():
                    dve.wait_ge(z1_done, t + 3)
                    settle(dve)
                    nc.vector.bn_stats(st_z1[:, p2], z1[:, p2]).then_inc(z1_stats, 1)

                def z1_mean():
                    dve.wait_ge(z1_stats, t + 3)
                    settle(dve)
                    nc.vector.bn_aggr(mv_z1[:, p2], st_z1[:, p2]).then_inc(z1_moments, 1)

                def x1_norm():
                    dve.wait_ge(z1_rstd, t + 3)
                    nc.vector.tensor_scalar(x1s[:, p2], z1[:, p2], mv_z1[:, p2, 0:1], rs_z1[:, p2, 0:1],
                                            ALU.subtract, ALU.mult).then_inc(x1_done, 1)
                    nc.vector.tensor_scalar(rows[:, one(t + 2), :], z1[:, p2:p2 + 1], mv_z1[:, p2, 0:1], rs_z1[:, p2, 0:1],
                                            ALU.subtract, ALU.mult).then_inc(x1_kept, 1)

                def x1_sums():
                    dve.wait_ge(x1_done, t + 3)
                    settle(dve)
                    nc.vector.bn_stats(st_x1[:, p2], x1s[:, p2]).then_inc(x1_stats, 1)

                def x1_mean():
                    dve.wait_ge(x1_stats, t + 3)
                    settle(dve)
                    nc.vector.bn_aggr(mv_x1[:, p2], st_x1[:, p2]).then_inc(x1_moments, 1)

                def latent_norm():
                    dve.wait_ge(x1_rstd, t + 3)
                    nc.vector.tensor_scalar(l_hat[:, p2], x1s[:, p2], mv_x1[:, p2, 0:1], rs_x1[:, p2, 0:1],
                                            ALU.subtract, ALU.mult).then_inc(l_hat_done, 1)

                def keep_rows():
                    dve.wait_ge(kv_done, 2 * t + 4)
                    dve.wait_ge(t_ps, count(4 * t))
                    for b in range(BT):
                        own, other = slice(b * S, (b + 1) * S), slice((1 - b) * S, (2 - b) * S)
                        nc.vector.tensor_copy(kv_rows[own, p1, b], l_rows[own, p1]).then_inc(kv_kept, 1)
                        nc.vector.tensor_copy(kv_rows[other, p1, b], c_rows[other, p1]).then_inc(kv_kept, 1)

                def z2_sum():
                    dve.wait_ge(o_ps, t - 1)
                    dve.wait_ge(x1_kept, t - 1)
                    nc.vector.tensor_tensor(z2[:, p:p + 1], ps_o[:, 0:D].rearrange("p (o d) -> p o d", o=1),
                                            rows[:, one(t - 2), :], ALU.add).then_inc(z2_done, 1)

                def z2_sums():
                    dve.wait_ge(z2_done, t - 1)
                    settle(dve)
                    nc.vector.bn_stats(st_z2[:, p], z2[:, p]).then_inc(z2_stats, 1)

                def z2_mean():
                    dve.wait_ge(z2_stats, t - 1)
                    settle(dve)
                    nc.vector.bn_aggr(mv_z2[:, p], st_z2[:, p]).then_inc(z2_moments, 1)

                def x2_norm():
                    dve.wait_ge(z2_rstd, t - 1)
                    dve.wait_ge(x2T_ps, count(t - 3))
                    nc.vector.tensor_scalar(x2s[:, p], z2[:, p], mv_z2[:, p, 0:1], rs_z2[:, p, 0:1],
                                            ALU.subtract, ALU.mult).then_inc(x2s_done, 1)
                    nc.vector.tensor_scalar(rows[:, one(t - 2), :], z2[:, p:p + 1], mv_z2[:, p, 0:1], rs_z2[:, p, 0:1],
                                            ALU.subtract, ALU.mult).then_inc(x2_done, 1)

                def gate_logits():
                    dve.wait_ge(gate_ps, t - 2)
                    nc.vector.tensor_tensor(logits[:, p3], B_GATE, bg_sb[:], ALU.add).then_inc(logits_done, 1)

                def gate_max():
                    dve.wait_ge(logits_done, t - 2)
                    nc.vector.tensor_reduce(lmax[:, p3], logits[:, p3], axis=AX.X, op=ALU.max, negate=True).then_inc(lmax_done, 1)

                def gate_inverse():
                    dve.wait_ge(gexp_done, t - 2)
                    nc.vector.reciprocal(ginv[:, p3], gsum[:, p3]).then_inc(ginv_done, 1)

                def gate_probs():
                    dve.wait_ge(ginv_done, t - 2)
                    nc.vector.tensor_scalar(gprob[:, p3], gexp[:, p3], ginv[:, p3, 0:1], None, ALU.mult).then_inc(gprob_done, 1)

                def gate_top():
                    dve.wait_ge(gprob_done, t - 2)
                    settle(dve)
                    nc.vector.max(top[:, p3], gprob[:, p3]).then_inc(top_done, 1)

                def gate_top_at():
                    dve.wait_ge(top_done, t - 2)
                    settle(dve)
                    nc.vector.max_index(top_at[:, p3], top[:, p3], gprob[:, p3]).then_inc(top_at_done, 1)
                    nc.vector.tensor_tensor(den[:, p3], top[:, p3, 0:1], top[:, p3, 1:2], ALU.add).then_inc(den_done, 1)

                def gate_ids():
                    dve.wait_ge(top_at_done, t - 2)
                    nc.vector.tensor_copy(top_atf[:, p3], top_at[:, p3, 0:2]).then_inc(atf_done, 1)
                    dve.wait_ge(den_done, t - 2)
                    nc.vector.scalar_tensor_tensor(den_g[:, p3], den[:, p3], 0.0, den[:, p3], ALU.is_equal,
                                                   ALU.add).then_inc(den_g_done, 1)

                def gate_picked():
                    dve.wait_ge(atf_done, t - 2)
                    nc.vector.tensor_tensor(picked[:, p3], eids[:].rearrange("p (o e) -> p o e", o=1).to_broadcast([P, 2, E]),
                                            top_atf[:, p3].rearrange("p (s o) -> p s o", o=1).to_broadcast([P, 2, E]),
                                            ALU.is_equal).then_inc(picked_done, 1)
                    dve.wait_ge(den_g_done, t - 2)
                    nc.vector.reciprocal(den_i[:, p3], den_g[:, p3]).then_inc(den_i_done, 1)

                def gate_mask():
                    dve.wait_ge(picked_done, t - 2)
                    nc.vector.tensor_tensor(mask[:, p3], picked[:, p3, 0], picked[:, p3, 1], ALU.add).then_inc(mask_done, 1)

                def seen_add():
                    dve.wait_ge(mask_done, t - 3)
                    dve.wait_ge(rank_ps, t - 4)
                    nc.vector.tensor_tensor(seen[:, 1 - p], seen[:, p], mask[:, p], ALU.add).then_inc(seen_done, 1)

                def route_rows():
                    dve.wait_ge(x_routed[p], (t - (p + 4)) * 16)
                    dve.wait_ge(den_i_done, t - 3)
                    nc.vector.tensor_scalar(routed[:, p, :, D], top[:, p, 0:2], den_i[:, p, 0:1], None,
                                            ALU.mult).then_inc(weight_done, 1)
                    dve.wait_ge(x2_done, t - 3)
                    nc.vector.tensor_copy(routed[:, p, :, 0:D],
                                          rows[:, one(t - 4), :].to_broadcast([P, 2, D])).then_inc(rows_kept, 1)
                    nc.vector.tensor_copy(routed[:, p, :, D + 1:D + 2].bitcast(I32).rearrange("p s o -> p o s"),
                                          rids[:, one(t - 4), :]).then_inc(rids_kept, 1)

                def place_all():
                    dve.wait_ge(rank_ps, t - 3)
                    nc.vector.tensor_tensor(pos_all[:, p], B_RANK, rbase[:], ALU.add).then_inc(pos_all_done, 1)

                def place_picked():
                    dve.wait_ge(pos_all_done, t - 3)
                    nc.vector.tensor_tensor(pos_sel[:, p], picked[:, p], pos_all[:, p:p + 1].to_broadcast([P, 2, E]),
                                            ALU.mult).then_inc(pos_sel_done, 1)

                def place_sum():
                    dve.wait_ge(pos_sel_done, t - 3)
                    nc.vector.tensor_reduce(pos_f[:, p], pos_sel[:, p], axis=AX.X, op=ALU.add).then_inc(pos_f_done, 1)

                def place_int():
                    dve.wait_ge(pos_f_done, t - 3)
                    nc.vector.tensor_copy(pos_i[:, p], pos_f[:, p]).then_inc(pos_done, 1)

                if on(t, 0):
                    row_max(0)
                if on(t, -2):
                    z2_sum()
                if on(t, 3):
                    in_sums()
                if on(t, -2):
                    z2_sums()
                if on(t, 3):
                    in_mean(0)
                    in_mean(1)
                if on(t, -2):
                    z2_mean()
                if on(t, 0):
                    inverse_sum(0)
                if unit_on(t, -1):
                    keep_pT(0)
                if on(t, -4):
                    route_rows()
                if on(t, 2):
                    z1_sum()
                if on(t, -4):
                    seen_add()
                if on(t, 2):
                    z1_sums()
                if on(t, 2):
                    z1_mean()
                if on(t, 0):
                    row_max(1)
                if on(t, -3):
                    gate_logits()
                if on(t, -2):
                    x2_norm()
                if on(t, -3):
                    gate_max()
                if on(t, 3):
                    in_hats()
                if on(t, 0):
                    inverse_sum(1)
                if unit_on(t, 0):
                    keep_pT(1)
                if on(t, 2):
                    x1_norm()
                    x1_sums()
                    x1_mean()
                if on(t, 0):
                    row_max(2)
                if on(t, -3):
                    gate_inverse()
                if on(t, 1):
                    keep_rows()
                if on(t, -3):
                    gate_probs()
                if on(t, 0):
                    inverse_sum(2)
                if unit_on(t, 1):
                    keep_pT(2)
                if on(t, 2):
                    latent_norm()
                if on(t, -4):
                    place_all()
                if on(t, -3):
                    gate_top()
                if on(t, 0):
                    row_max(3)
                if on(t, -3):
                    gate_top_at()
                if on(t, 3):
                    rot_turn()
                if on(t, -3):
                    gate_ids()
                if on(t, 3):
                    rot_cos_part()
                if on(t, -3):
                    gate_picked()
                if on(t, 3):
                    rot_add()
                if on(t, 0):
                    inverse_sum(3)
                if unit_on(t, 2):
                    keep_pT(3)
                if on(t, -4):
                    place_picked()
                if on(t, 3):
                    pick_keys()
                    kv_product()
                if on(t, -4):
                    place_sum()
                if on(t, -3):
                    gate_mask()
                if on(t, -4):
                    place_int()
                if on(t, 3):
                    scale_queries()

            periods(dve, period)

            steps = [0]

            def then(ins):
                steps[0] += 1
                ins.then_inc(tab, 1)
                dve.wait_ge(tab, steps[0])

            dve.wait_ge(cnt_ps, 1)
            dve.wait_ge(pad_ready, 5)
            then(nc.vector.tensor_scalar(cnt_up[:], B_RANK[0:1], float(T - 1), None, ALU.add))
            nc.vector.tensor_tensor(pad_f[:], B_RANK[0:1], rbase[0:1], ALU.add).then_inc(tab_base, 1)
            then(nc.vector.tensor_copy(cnt_i[:], cnt_up[:]))
            dve.wait_ge(tab_base, 1)
            nc.vector.tensor_copy(pad_i[:], pad_f[:]).then_inc(tab_ready, 1)
            then(nc.vector.tensor_scalar(nt_i[:], cnt_i[:], T.bit_length() - 1, None, ALU.arith_shift_right))
            then(nc.vector.tensor_copy(nt_f[:], nt_i[:]))
            then(nc.vector.tensor_tensor_scan(cum_nt[:], ones_row[:], nt_f[:], 0.0, ALU.mult, ALU.add))
            over_tiles = lambda ap: ap.rearrange("p (o e) -> p o e", o=1).to_broadcast([1, NF, E])
            then(nc.vector.tensor_tensor(past[:], over_tiles(cum_nt[:]),
                                         tids[:].rearrange("p (i o) -> p i o", o=1).to_broadcast([1, NF, E]), ALU.is_le))
            then(nc.vector.tensor_tensor(past_nt[:], past[:], over_tiles(nt_f[:]), ALU.mult))
            then(nc.vector.tensor_reduce(ex_f[:], past[:], axis=AX.X, op=ALU.add))
            then(nc.vector.tensor_reduce(start_f[:], past_nt[:], axis=AX.X, op=ALU.add))
            then(nc.vector.tensor_scalar(valid_f[:], ex_f[:], E - 0.5, float(T), ALU.is_lt, ALU.mult))
            then(nc.vector.tensor_tensor(blk_f[:], tids[:], start_f[:], ALU.subtract))
            then(nc.vector.tensor_tensor(blk_v[:], blk_f[:], valid_f[:], ALU.mult))
            then(nc.vector.scalar_tensor_tensor(base_f[:], ex_f[:], float(CAP), blk_v[:], ALU.mult, ALU.add))
            then(nc.vector.tensor_scalar(exw_f[:], ex_f[:], float(E - 1), None, ALU.min))
            then(nc.vector.tensor_copy(base_i[:], base_f[:]))
            nc.vector.tensor_copy(exw_i[:], exw_f[:]).then_inc(tab_ready, 1)

            def rowsT(i, q):
                dve.wait_ge(f_xT_ps, i + 1)
                dve.wait_ge(f_h_ps, count(i * (FC // 2) - FC // 2))
                nc.vector.tensor_copy(f_xT[:, q % 2], F_XT[q % 2]).then_inc(f_xT_done, 1)

            def result(i, q):
                dve.wait_ge(f_y_ps, i + 1)
                dve.wait_ge(f_y_done, count(TB * i - TB))
                nc.vector.tensor_tensor(f_yb[:, q % 2], F_Y[q % 2].rearrange("p (b d) -> p b d", d=D),
                                        f_w[q][:, B2_AT:B2_AT + D].rearrange("p (o d) -> p o d", o=1).to_broadcast([P, TB, D]),
                                        ALU.add).then_inc(f_yb_done, 1)
                dve.wait_ge(y_routed[q], (i - q) * (16 * TB // RING))
                nc.vector.tensor_copy(f_id[:, q], f_x[:, q, :, D + 1]).then_inc(f_id_done, 1)
                dve.wait_ge(f_yb_done, i + 1)
                for b in range(TB):
                    nc.vector.tensor_scalar(f_y[:, q, b], f_yb[:, q % 2, b], f_x[:, q, b, D:D + 1], None,
                                            ALU.mult).then_inc(f_y_done, 1)

            def ffn(i, q):
                if not isinstance(i, int) or i + 1 < NF:
                    rowsT(i + 1, (q + 1) % RING)
                if not isinstance(i, int) or i:
                    result(i - 1, (q - 1) % RING)

            rowsT(0, 0)
            turns(dve, NF, ffn, RING, RING)
            result(NF - 1, RING - 1)

            def last(g, q):
                if not isinstance(g, int) or g < NZ:
                    dve.wait_ge(e_sum_done, g + 1)
                    dve.wait_ge(e_out_done, count(ZT * g - ZT * (RING - 1)))
                    nc.vector.tensor_tensor(e_z[:, q], e_sum[:, q % 2], rows[:, bass.ds(g * ZT, ZT), :], ALU.add).then_inc(e_z_done, 1)
                    dve.wait_ge(e_z_done, g + 1)
                    for c in range(ZT):
                        nc.vector.bn_stats(e_st[:, q, c], e_z[:, q, c]).then_inc(e_stats, 1)
                    for c in range(ZT):
                        dve.wait_ge(e_stats, g * ZT + (c + 1))
                        settle(dve)
                        nc.vector.bn_aggr(e_mv[:, q, c], e_st[:, q, c]).then_inc(e_moments, 1)
                if not isinstance(g, int) or g:
                    o = (q - 1) % RING
                    dve.wait_ge(e_rstd, g)
                    nc.vector.scalar_tensor_tensor(e_nm[:, o], e_mv[:, o, :, 0], -1.0, e_rs[:, o], ALU.mult, ALU.mult).then_inc(e_nm_done, 1)

            turns(dve, NZ, last, RING)
            last(NZ, 0)

        @block.tensor
        def _(pe):
            pe.wait_ge(s_ident, 16)
            pe.wait_ge(s_win, 32)
            for at, (kind, what, _) in enumerate(jobs):
                bank = banks[at % BANKS]
                if at == 1:
                    pe.wait_ge(s_wq, 16)
                if at == 3:
                    pe.wait_ge(s_wkv, 16)
                if at == TURNED:
                    pe.wait_ge(prep_act, (TURNED + 1) // 2)
                    pe.wait_ge(prep_dve, TURNED // 2)
                    pe.wait_ge(s_wo, 16)
                if at >= BANKS:
                    kept, n = prep_kept(at - BANKS)
                    pe.wait_ge(kept, n)
                    pe.wait_ge(win_kept, 1)
                for c in range(4):
                    o = bank[:, c * P:(c + 1) * P]
                    if kind in ("in", "t"):
                        last = nc.tensor.transpose(o, what[c], ident[:])
                        continue
                    h = 8 * (what // 2) + 2 * c + what % 2
                    e = slice((h % 2) * HD, (h % 2 + 1) * HD)
                    if kind == "m":
                        last = nc.tensor.matmul(o, wqT[e, h // 2], wkT[e, h // 2], start=True, stop=True)
                    else:
                        last = nc.tensor.matmul(o, wvT[e, h // 2], wo_raw[e, h // 2], start=True, stop=True)
                last.then_inc(prep_ps, 1)
            pe.wait_ge(prep_act, (len(jobs) + 1) // 2)
            pe.wait_ge(prep_dve, len(jobs) // 2)
            pe.wait_ge(pad_ready, 5)
            pe.wait_ge(s_const, 16 * N_CONST)
            pe.wait_ge(s_gains, 16 * N_GAINS)

            def score(t, k, p):
                n, sl, b, hf = t * 4 + k, k % 2, k // 2, k % 2
                if k == 0:
                    pe.wait_ge(u_done, 4 * t + 4)
                    pe.wait_ge(kvT_done, 2 * t + 2)
                pe.wait_ge(exp_done, count(n - 1))
                for j in range(UP):
                    h = hf * HH + 2 * j
                    last = nc.tensor.matmul(ps_s[sl][:, j * P:(j + 1) * P], u_sb[:, p, b, h:h + 2].rearrange("p h s -> p (h s)"),
                                            kvT[:, p, 1 - b:4 - b:2], start=True, stop=True)
                last.then_inc(s_ps, 1)

            def out_part(t, k, p):
                if k == 1:
                    pe.wait_ge(t_done, 4 * t - 1)
                    pe.wait_ge(z2_done, t - 1)
                if k == 2:
                    pe.wait_ge(t_done, 4 * t)
                lo, hi = ((0, 6), (6, 11), (11, 16))[k - 1]
                for h in range(lo, hi):
                    last = nc.tensor.matmul(ps_o[:, 0:D], tT[:, (p + 1) % 2, h], value_w[:, h],
                                            start=(h == 0), stop=(h == H - 1))
                if k == 3:
                    last.then_inc(o_ps, 1)

            def turn_probs(t, k):
                m, ss = t * 4 + (k - 1), (k - 1) % 2
                pe.wait_ge(p_done, m + 1)
                pe.wait_ge(pT_done, m)
                for j in range(UP):
                    last = nc.tensor.transpose(ps_pT[:, j * P:(j + 1) * P], probs_n[:, ss, j], ident[:])
                last.then_inc(pT_ps, 1)

            def weigh(t, k, p):
                m, ss = t * 4 + (k - 2), (k - 2) % 2
                b = (k - 2) % 4 // 2
                pp = p if k > 1 else (p + 1) % 2
                pe.wait_ge(pT_done, m + 1)
                pe.wait_ge(t_done, m)
                nc.tensor.matmul(ps_t[:], kv_rows[:, pp, b], pT[:, ss], start=True, stop=True).then_inc(t_ps, 1)

            def latents_part(t, k, p1):
                if k == 0:
                    pe.wait_ge(kvT_done, 2 * t + 4)
                pe.wait_ge(u_done, 4 * t + (4 + k))
                for c in range(4):
                    last = nc.tensor.matmul(ps_u[:, c * P:(c + 1) * P], score_w[:, 4 * k + c],
                                            kvT[:, p1, 1:3].rearrange("p b s -> p (b s)"), start=True, stop=True)
                last.then_inc(u_ps, 1)

            def period(t, p):
                p3, p2, p1 = (p + 3) % 2, p, (p + 1) % 2
                for k in range(UNITS):
                    if on(t, 0):
                        score(t, k, p)
                    if k == 0:
                        if unit_on(t, -2):
                            weigh(t, 0, p)
                        if on(t, 1):
                            latents_part(t, 0, p1)
                    if k == 2 and on(t, 1):
                        latents_part(t, 2, p1)
                    if k and on(t, -1):
                        out_part(t, k, p)
                    if unit_on(t, k - 1):
                        turn_probs(t, k)
                    if k == 0 and on(t, 2):
                        pe.wait_ge(yT_done, 2 * t + 6)
                        nc.tensor.matmul(A_O, yT[:, p2], woutT[:], start=True, stop=True).then_inc(wo_ps, 1)
                    if k == 0 and on(t, -3):
                        pe.wait_ge(x2T_done, t - 2)
                        nc.tensor.matmul(B_GATE, x2T[:, p3], wg_sb[:], start=True, stop=True).then_inc(gate_ps, 1)
                    if k == 2 and on(t, -4):
                        pe.wait_ge(mask_done, t - 3)
                        pe.wait_ge(seen_done, t - 3)
                        pe.wait_ge(logits_done, min(t - 2, NT) if isinstance(t, int) else t - 2)
                        nc.tensor.matmul(B_RANK, ones[:], seen[:, p], start=True, stop=False)
                        nc.tensor.matmul(B_RANK, tri_bf[:], mask[:, p], start=False, stop=True).then_inc(rank_ps, 1)
                    if k == 3 and on(t, -2):
                        pe.wait_ge(x2s_done, t - 1)
                        pe.wait_ge(pos_all_done, count(t - 3))
                        nc.tensor.transpose(B_XT, x2s[:, p], ident[:]).then_inc(x2T_ps, 1)
                    if k == 2 and on(t, 3):
                        pe.wait_ge(xnT_done, t + 4)
                        nc.tensor.matmul(A_QKV, xnT[:, p3], winT[:], start=True, stop=True).then_inc(qkv_ps, 1)
                    if k:
                        if k != 2 and on(t, 1):
                            latents_part(t, k, p1)
                        if unit_on(t, k - 2):
                            weigh(t, k, p)
                    if k == 1 and on(t, 3):
                        pe.wait_ge(x_hat_done, t + 4)
                        pe.wait_ge(attn_done, t + 3)
                        nc.tensor.transpose(A_XT, x_hat[:, p3], ident[:]).then_inc(xT_ps, 1)
                    if k == 3 and on(t, 2):
                        pe.wait_ge(kv_done, 2 * t + 6)
                        pe.wait_ge(u_done, 4 * t + 8)
                        nc.tensor.transpose(KVT[:, 0:P], l_rows[:, p2], ident[:])
                        last = nc.tensor.transpose(KVT[:, P:2 * P], c_rows[:, p2], ident[:])
                        last.then_inc(kvT_ps, 1)
                    if k == 3 and on(t, 3):
                        pe.wait_ge(kvp_done, t + 4)
                        pe.wait_ge(pick_done, t + 4)
                        nc.tensor.transpose(A_QT, qkv[:, p3, 0:D], ident[:])
                        nc.tensor.matmul(A_AT, kv_prod[:, p3], k_pick[:, p3], start=True, stop=True).then_inc(at_ps, 1)

            periods(pe, period)

            pe.wait_ge(pos_all_done, NT)
            pe.wait_ge(seen_done, NT + 1)
            nc.tensor.matmul(B_RANK, ones[:], seen[:, NT % 2], start=True, stop=True).then_inc(cnt_ps, 1)
            pe.wait_ge(tab, 1)

            def rowsT(i, q):
                pe.wait_ge(f_in[q], (i + (RING - q)) * (16 // RING))
                pe.wait_ge(f_xT_done, count(i - 1))
                for b in range(TB):
                    last = nc.tensor.transpose(F_XT[q % 2][:, b * P:(b + 1) * P], f_x[:, q, b, 0:D], ident[:])
                last.then_inc(f_xT_ps, 1)

            def hidden(i, q):
                pe.wait_ge(fw_in[q], (i + (RING - q)) * (16 // RING))
                pe.wait_ge(f_xT_done, i + 1)
                pe.wait_ge(f_h_done, count(i * FC - FC))
                for c in range(FC):
                    done = nc.tensor.matmul(F_H[q % 2][c // 2][:, (c % 2) * T:(c % 2 + 1) * T], f_w[q][:, c * P:(c + 1) * P],
                                            f_xT[:, q % 2], start=True, stop=True)
                    if c % 2:
                        done.then_inc(f_h_ps, 1)

            def result(i, q):
                pe.wait_ge(f_h_done, i * FC + FC)
                pe.wait_ge(f_yb_done, count(i - 1))
                for b in range(TB):
                    for c in range(FC):
                        last = nc.tensor.matmul(F_Y[q % 2][:, b * D:(b + 1) * D], f_h[:, q % 2, c, b * P:(b + 1) * P],
                                                f_w[q][:, W2_AT + c * D:W2_AT + (c + 1) * D], start=(c == 0), stop=(c == FC - 1))
                last.then_inc(f_y_ps, 1)

            def ffn(i, q):
                hidden(i, q)
                if not isinstance(i, int) or i + 1 < NF:
                    rowsT(i + 1, (q + 1) % RING)
                if not isinstance(i, int) or i:
                    result(i - 1, (q - 1) % RING)

            rowsT(0, 0)
            turns(pe, NF, ffn, RING, RING)
            result(NF - 1, RING - 1)


_ARGS = {
    "x": "x", "ctx_in": "ctx_1024", "w_in": "L0_attn_W_in", "w_out": "L0_attn_W_out", "ln_g": "L0_attn_ln_g",
    "ln_b": "L0_attn_ln_b", "ln1_g": "L0_xattn_ln1_g", "ln1_b": "L0_xattn_ln1_b", "ln2_g": "L0_xattn_ln2_g",
    "ln2_b": "L0_xattn_ln2_b", "w_q": "L0_xattn_Wq", "w_kv": "L0_xattn_Wkv", "w_o": "L0_xattn_Wo",
    "w_g": "L0_ffn_Wg", "b_g": "L0_ffn_bg",
}


def shape_constants(batches, length, width, experts):
    import numpy as np

    f32 = np.float32
    tokens, p = batches * length, 128
    rot = width // 2
    inv_freq = f32(1.0) / f32(10000.0) ** (np.arange(0, rot, 2, dtype=f32) / f32(rot))
    angle = np.repeat(np.arange(length, dtype=f32)[:, None] * inv_freq[None, :], 2, axis=-1)
    sign = np.tile(np.array([-1.0, 1.0], f32), rot // 2)
    lane = np.arange(p)
    cap = tokens + FFN_ROWS
    return {
        "rot_cos": np.tile(np.cos(angle), (p // length, 1)),
        "rot_sin": np.tile(np.sin(angle) * sign, (p // length, 1)),
        "batch_of": np.repeat(np.eye(p // length, dtype=f32), length, 0),
        "eye": np.eye(p, dtype=f32),
        "before": (lane[:, None] < lane[None, :]).astype(f32),
        "expert_ids": np.tile(np.arange(experts, dtype=f32), (p, 1)),
        "region_base": np.tile(np.arange(experts, dtype=f32) * f32(cap), (p, 1)),
        "row_ids": (lane[:, None, None] + p * np.arange(tokens // p)[None, :, None]
                    + tokens * np.arange(2)[None, None, :]).astype(np.int32),
        "tile_ids": np.arange(ffn_tiles(tokens, experts), dtype=f32)[None],
    }


def expert_rows(w1, b1, w2, b2):
    import numpy as np

    e, d, f = w1.shape
    return np.concatenate([
        w1,
        w2.reshape(e, f // d, d, d).transpose(0, 2, 1, 3).reshape(e, d, f),
        b1.reshape(e, f // d, d).transpose(0, 2, 1),
        np.broadcast_to(b2[:, None, :], (e, d, d)),
    ], axis=2)


def kernel(**inputs):
    import numpy as np
    import concourse.bacc as bacc
    from concourse.bass_utils import run_bass_kernel_spmd

    nc = bacc.Bacc("TRN2", target_bir_lowering=False, num_devices=1)
    arrays, args = {}, {}

    def give(name, a):
        a = np.ascontiguousarray(a)
        arrays[f"in_{name}"] = a
        args[name] = nc.dram_tensor(f"in_{name}", a.shape, mybir.dt.from_np(a.dtype), kind="ExternalInput").ap()

    for name, key in _ARGS.items():
        give(name, inputs[key])
    give("expert_w", expert_rows(*(np.asarray(inputs[f"L0_ffn_{n}"]) for n in ("W1", "b1", "W2", "b2"))))
    batches, length, width = arrays["in_x"].shape
    experts = arrays["in_expert_w"].shape[0]
    for name, a in shape_constants(batches, length, width, experts).items():
        give(name, a)
    tokens = batches * length
    f32 = mybir.dt.float32
    args["x_rows"] = nc.dram_tensor("x_rows", [experts * (tokens + FFN_ROWS) + FFN_ROWS, width + 2], f32, kind="Internal").ap()
    args["y_rows"] = nc.dram_tensor("y_rows", [2 * tokens, width], f32, kind="Internal").ap()
    args["out"] = nc.dram_tensor("out", [batches, length, width], f32, kind="ExternalOutput").ap()
    decoder_layer(nc, **args)
    return run_bass_kernel_spmd(nc, [arrays], core_ids=[0]).results[0]["out"]
```

```python
import concourse.bass as bass
from concourse import mybir
from contextlib import ExitStack


FFN_ROWS = 256


def ffn_tiles(tokens, experts):
    most = (2 * tokens + experts * (FFN_ROWS - 1)) // FFN_ROWS
    return -(-most // 8) * 8


def decoder_layer(nc, x, ctx_in, w_in, w_out, ln_g, ln_b, ln1_g, ln1_b, ln2_g, ln2_b,
                  w_q, w_kv, w_o, expert_w, w_g, b_g, rot_cos, rot_sin, batch_of, eye,
                  before, expert_ids, region_base, row_ids, tile_ids, x_rows, y_rows, out):
    F32 = mybir.dt.float32
    BF16 = mybir.dt.bfloat16
    I32 = mybir.dt.int32
    U32 = mybir.dt.uint32
    ALU = mybir.AluOpType
    ACT = mybir.ActivationFunctionType
    AX = mybir.AxisListType

    B, S, D = x.shape
    P = 128
    BT = P // S
    NT = B // BT
    assert NT <= 256
    HD = 64
    H = w_q.shape[1] // HD
    HH = H // 2
    UP = HH // BT
    UNITS = 4
    ROT = D // 2
    HI_BITS = -(1 << 12)
    F32R = mybir.dt.float32r
    EPS_LN, EPS_L2 = 1e-5, 1e-6
    N = B * S
    E = w_g.shape[1]
    FC = (expert_w.shape[2] - D) // (2 * D + 1)
    F = FC * P
    W2_AT, B1_AT, B2_AT, W_ROW = F, F + FC * D, F + FC * (D + 1), F + FC * (D + 1) + D
    T = FFN_ROWS
    TB = T // P
    CAP = N + T
    NF = ffn_tiles(N, E)
    ROW = D + 2
    RING, W_RING = 4, 8
    ZT = 4
    NZ = NT // ZT
    QS_SCALE = 1.0 / HD ** 0.5

    x_t = x.rearrange("(t b) s d -> t (b s) d", b=BT)
    ctx_t = ctx_in.rearrange("(t b) s d -> t b s d", b=BT)
    out_z = out.rearrange("(t b) s d -> t (b s) d", b=BT)

    ctx = ExitStack()
    with ctx:
        def sb(name, shape, dt=F32):
            return ctx.enter_context(nc.sbuf_tensor(name, shape, dt))

        def pb(name):
            return ctx.enter_context(nc.psum_tensor(name, [P, 512], F32))

        def sem(name):
            return ctx.enter_context(nc.semaphore(name))

        ident = sb("ident", [P, P])
        cosb = sb("cosb", [P, ROT])
        sinb = sb("sinb", [P, ROT])
        member = sb("member", [P, BT])
        m_half = sb("m_half", [P, ZT])
        gcol = sb("gcol", [P, 1])
        bcol = sb("bcol", [P, 1])
        g_ctx = sb("g_ctx", [P, D])
        b_ctx = sb("b_ctx", [P, D])
        g_lat = sb("g_lat", [P, D])
        b_lat = sb("b_lat", [P, D])
        winT = sb("winT", [P, 3 * D])
        woutT = sb("woutT", [P, D])
        score_hi = sb("score_hi", [P, H, D], F32R)
        score_lo = sb("score_lo", [P, H, D], F32R)
        value_w = sb("value_w", [P, H, D])
        win_raw = sb("win_raw", [P, 3, D])
        wout_raw = sb("wout_raw", [P, D])
        wq_raw = sb("wq_raw", [P, H * HD])
        wkv_raw = sb("wkv_raw", [P, 2 * H * HD])
        wo_raw = sb("wo_raw", [P, H // 2, D])
        wqT = sb("wqT", [P, H // 2, D])
        wkT = sb("wkT", [P, H // 2, D])
        wvT = sb("wvT", [P, H // 2, D])

        score_w = wkv_raw[:].rearrange("p (h d) -> p h d", d=D)

        x_raw = sb("x_raw", [P, 2, D])
        c_raw = sb("c_raw", [P, 2, D])
        st_in = sb("st_in", [P, 2, 2, 6])
        mv_in = sb("mv_in", [P, 2, 2, 2])
        ve_in = sb("ve_in", [P, 2, 2])
        rs_in = sb("rs_in", [P, 2, 2])
        x_hat = sb("x_hat", [P, 2, D])
        c_hat = sb("c_hat", [P, 2, D])
        xnT = sb("xnT", [P, 2, D])
        qkv = sb("qkv", [P, 2, 3 * D])
        sq_junk = sb("sq_junk", [P, 2, D])
        ss_qk = sb("ss_qk", [P, 2, 2])
        se_qk = sb("se_qk", [P, 2, 2])
        rs_qk = sb("rs_qk", [P, 2, 2])
        turned = sb("turned", [P, 2, 2, ROT])
        kv_prod = sb("kv_prod", [P, 2, D])
        k_pick = sb("k_pick", [P, 2, BT])
        yT = sb("yT", [P, 2, P])
        attn_o = sb("attn_o", [P, 2, D])
        z1 = sb("z1", [P, 2, D])
        x1s = sb("x1s", [P, 2, D])
        st_z1 = sb("st_z1", [P, 2, 6])
        mv_z1 = sb("mv_z1", [P, 2, 2])
        ve_z1 = sb("ve_z1", [P, 2, 1])
        rs_z1 = sb("rs_z1", [P, 2, 1])
        st_x1 = sb("st_x1", [P, 2, 6])
        mv_x1 = sb("mv_x1", [P, 2, 2])
        ve_x1 = sb("ve_x1", [P, 2, 1])
        rs_x1 = sb("rs_x1", [P, 2, 1])
        l_hat = sb("l_hat", [P, 2, D])
        l_scaled = sb("l_scaled", [P, 2, D])
        c_scaled = sb("c_scaled", [P, 2, D])
        l_rows = sb("l_rows", [P, 4, D])
        c_rows = sb("c_rows", [P, 4, D])
        kv_rows = sb("kv_rows", [P, 2, BT, D])
        kvT = sb("kvT", [P, 4, 4, S])
        l_upper = sb("l_upper", [P, 2, P])
        lT_hi = sb("lT_hi", [P, 2, 2, P], F32R)
        lT_lo = sb("lT_lo", [P, 2, 2, P], F32R)
        u_sb = sb("u_sb", [P, 2, 2 * BT, H, S])
        tT = sb("tT", [P, 2, H, P])
        z2 = sb("z2", [P, 2, D])
        st_z2 = sb("st_z2", [P, 2, 6])
        mv_z2 = sb("mv_z2", [P, 2, 2])
        ve_z2 = sb("ve_z2", [P, 2, 1])
        rs_z2 = sb("rs_z2", [P, 2, 1])
        neg_max = sb("neg_max", [P, 2, UP])
        probs = sb("probs", [P, 2, UP, P])
        sums = sb("sums", [P, 2, UP])
        inv_sum = sb("inv_sum", [P, 2, UP])
        probs_n = sb("probs_n", [P, 2, UP, P])
        pT = sb("pT", [P, 2, UP * P])
        x2s = sb("x2s", [P, 2, D])
        x2T = sb("x2T", [P, 2, P])
        wg_sb = sb("wg_sb", [P, E])
        bg_sb = sb("bg_sb", [P, E])
        tri = sb("tri", [P, P])
        tri_bf = sb("tri_bf", [P, P], BF16)
        ones = sb("ones", [P, P], BF16)
        ones_row = sb("ones_row", [1, E])
        eids = sb("eids", [P, E])
        rbase = sb("rbase", [P, E])
        rids = sb("rids", [P, NT, 2], I32)
        tids = sb("tids", [1, NF])
        logits = sb("logits", [P, 2, E])
        lmax = sb("lmax", [P, 2, 1])
        gexp = sb("gexp", [P, 2, E])
        gsum = sb("gsum", [P, 2, 1])
        ginv = sb("ginv", [P, 2, 1])
        gprob = sb("gprob", [P, 2, E])
        top = sb("top", [P, 2, 8])
        top_at = sb("top_at", [P, 2, 8], U32)
        top_atf = sb("top_atf", [P, 2, 2])
        den = sb("den", [P, 2, 1])
        den_g = sb("den_g", [P, 2, 1])
        den_i = sb("den_i", [P, 2, 1])
        picked = sb("picked", [P, 2, 2, E])
        mask = sb("mask", [P, 2, E], BF16)
        seen = sb("seen", [P, 2, E], BF16)
        pos_all = sb("pos_all", [P, 2, E])
        pos_sel = sb("pos_sel", [P, 2, 2, E])
        pos_f = sb("pos_f", [P, 2, 2])
        pos_i = sb("pos_i", [P, 2, 2], I32)
        routed = sb("routed", [P, 2, 2, ROW])
        pad_row = sb("pad_row", [P, ROW])
        rows = sb("rows", [P, NT, D])

        cnt_up = sb("cnt_up", [1, E])
        cnt_i = sb("cnt_i", [1, E], I32)
        nt_i = sb("nt_i", [1, E], I32)
        nt_f = sb("nt_f", [1, E])
        cum_nt = sb("cum_nt", [1, E])
        pad_f = sb("pad_f", [1, E])
        pad_i = sb("pad_i", [1, E], I32)
        past = sb("past", [1, NF, E])
        past_nt = sb("past_nt", [1, NF, E])
        ex_f = sb("ex_f", [1, NF])
        start_f = sb("start_f", [1, NF])
        valid_f = sb("valid_f", [1, NF])
        blk_f = sb("blk_f", [1, NF])
        blk_v = sb("blk_v", [1, NF])
        base_f = sb("base_f", [1, NF])
        exw_f = sb("exw_f", [1, NF])
        base_i = sb("base_i", [1, NF], I32)
        exw_i = sb("exw_i", [1, NF], I32)
        u_flat = u_sb[:].rearrange("p q n h s -> p (q n h s)")
        t_flat = tT[:].rearrange("p q h s -> p (q h s)")
        f_w = [t_flat[:, q * W_ROW:(q + 1) * W_ROW] for q in range(3)]
        f_w += [u_flat[:, q * W_ROW:(q + 1) * W_ROW] for q in range(W_RING - 3)]
        f_x = sb("f_x", [P, RING, TB, ROW])
        f_id = sb("f_id", [P, RING, TB])
        f_x_upper = wq_raw[:].rearrange("p (n t) -> p n t", t=T)[:, 0:2]
        f_w_upper = wkT[:].rearrange("p (q c) d -> p q (c d)", q=2)
        f_xT_hi, f_xT_lo = (w[:].rearrange("p q l s -> p q (l s)") for w in (lT_hi, lT_lo))
        f_w1_hi, f_w1_lo = (w[:].rearrange("p (q h) d -> p q (h d)", q=H // FC)[:, 0:2] for w in (score_hi, score_lo))
        f_h = wkv_raw[:].rearrange("p (q c t) -> p q c t", q=2, t=T)
        f_yb = wqT[:, 0:2 * TB].rearrange("p (q b) d -> p q b d", q=2)
        f_y = wvT[:].rearrange("p (q b) d -> p q b d", q=RING)
        e_y = t_flat.rearrange("p (q s c d) -> p q s c d", q=RING, s=2, c=ZT)
        e_parts = u_flat.rearrange("p (q c d) -> p q c d", c=ZT, d=D)
        e_z, e_sum, e_out = e_parts[:, 0:RING], e_parts[:, RING:RING + 2], e_parts[:, RING + 2:RING + 4]
        e_st = sb("e_st", [P, RING, ZT, 6])
        e_mv = sb("e_mv", [P, RING, ZT, 2])
        e_ve = sb("e_ve", [P, RING, ZT])
        e_rs = sb("e_rs", [P, RING, ZT])
        e_nm = sb("e_nm", [P, RING, ZT])
        eps_ln = sb("eps_ln", [P, ZT])
        eps_l2 = sb("eps_l2", [P, ZT])

        ps_s = [pb("ps_s0"), pb("ps_s1")]
        ps_pT = pb("ps_pT")
        ps_t = pb("ps_t")
        ps_u = pb("ps_u")
        ps_o = pb("ps_o")
        ps_a = pb("ps_a")
        ps_b = pb("ps_b")
        A_QKV = ps_a[:, 0:3 * D]
        A_XT = ps_a[:, 384:512]
        A_QT = ps_a[:, 0:P]
        A_AT = ps_a[:, P:P + BT]
        A_O = ps_a[:, 256:384]
        B_XT = ps_b[:, 0:P]
        B_RANK = ps_b[:, 128:128 + E]
        B_GATE = ps_b[:, 144:144 + E]
        F_XT = [ps_o[:, 0:T], ps_a[:, 0:T]]
        F_H = [ps_s, [ps_pT, ps_b]]
        F_Y = [ps_t[:, 0:TB * D], ps_u[:, 0:TB * D]]
        KVT = ps_u[:, 0:BT * P]

        s_const = sem("s_const")
        s_gains = sem("s_gains")
        s_ident = sem("s_ident")
        s_win = sem("s_win")
        s_wq = sem("s_wq")
        s_wkv = sem("s_wkv")
        s_wo = sem("s_wo")
        half_set = sem("half_set")
        win_kept = sem("win_kept")
        prep_ps = sem("prep_ps")
        prep_act = sem("prep_act")
        prep_dve = sem("prep_dve")
        x_in = [sem("x_in0"), sem("x_in1")]
        c_in = [sem("c_in0"), sem("c_in1")]
        names = """in_stats in_moments in_eps in_rstd x_hat_done c_hat_done xT_ps xnT_done qkv_ps qkv_done sq_done
        qk_eps qk_rstd rot_turned rot_cosed rot_done kvp_done pick_done at_ps yT_done wo_ps attn_done
        z1_done z1_stats z1_moments z1_eps z1_rstd x1_done x1_stats x1_moments x1_eps x1_rstd l_hat_done
        l_scaled_done c_scaled_done kv_done kv_kept kvT_ps kvT_done l_upper_done lT_done upper_done score_split u_ps u_done s_ps max_done exp_done inv_done p_done pT_ps pT_done
        t_ps t_done o_ps z2_done z2_stats z2_moments z2_eps z2_rstd x2_done
        x1_kept x2s_done x2T_ps x2T_done gate_ps logits_done lmax_done gexp_done ginv_done gprob_done top_done top_at_done den_done den_g_done den_i_done
        weight_done atf_done picked_done mask_done seen_done rows_kept rids_kept rank_ps pos_all_done pos_sel_done pos_f_done
        pos_done pad_ready cnt_ps tab tab_base tab_ready f_xT_ps f_x_upper_done f_xT_done f_w_upper_done f_w1_hi_done f_w1_lo_done f_h_ps f_h_done f_y_ps f_yb_done f_id_done f_y_done
        e_sum_done e_z_done e_stats e_moments e_eps e_rstd e_nm_done e_out_done""".split()
        (in_stats, in_moments, in_eps, in_rstd, x_hat_done, c_hat_done, xT_ps, xnT_done, qkv_ps, qkv_done, sq_done,
         qk_eps, qk_rstd, rot_turned, rot_cosed, rot_done, kvp_done, pick_done, at_ps, yT_done, wo_ps, attn_done,
         z1_done, z1_stats, z1_moments, z1_eps, z1_rstd, x1_done, x1_stats, x1_moments, x1_eps, x1_rstd, l_hat_done,
         l_scaled_done, c_scaled_done, kv_done, kv_kept, kvT_ps, kvT_done, l_upper_done, lT_done, upper_done, score_split, u_ps, u_done, s_ps, max_done, exp_done, inv_done,
         p_done, pT_ps, pT_done, t_ps, t_done, o_ps, z2_done, z2_stats, z2_moments, z2_eps, z2_rstd,
         x2_done, x1_kept, x2s_done, x2T_ps, x2T_done, gate_ps, logits_done, lmax_done, gexp_done, ginv_done, gprob_done,
         top_done, top_at_done, den_done, den_g_done, den_i_done, weight_done, atf_done, picked_done, mask_done, seen_done, rows_kept,
         rids_kept, rank_ps, pos_all_done, pos_sel_done, pos_f_done, pos_done, pad_ready, cnt_ps, tab, tab_base,
         tab_ready, f_xT_ps, f_x_upper_done, f_xT_done, f_w_upper_done, f_w1_hi_done, f_w1_lo_done, f_h_ps, f_h_done, f_y_ps, f_yb_done, f_id_done, f_y_done, e_sum_done, e_z_done, e_stats,
         e_moments, e_eps, e_rstd, e_nm_done, e_out_done) = [sem(n) for n in names]
        s_out = [sem("s_out0"), sem("s_out1")]
        x_routed = [sem("x_routed0"), sem("x_routed1")]
        pad_filled = sem("pad_filled")
        f_in = [sem(f"f_in{q}") for q in range(RING)]
        fw_in = [sem(f"fw_in{q}") for q in range(W_RING)]
        y_routed = [sem(f"y_routed{q}") for q in range(RING)]
        e_in = [sem(f"e_in{q}") for q in range(RING)]

        def count(n):
            return max(n, 0) if isinstance(n, int) else n

        def settle(eng):
            eng.nop(nofuse=True)

        FIRST, LAST = -5, NT + 4

        def periods(eng, period):
            lo = 6
            fours = (NT - 6 - lo) // 4
            hi = lo + 4 * fours
            for t in range(FIRST, lo):
                period(t, t % 4)
            with eng.Fori(0, fours) as i:
                for step in range(4):
                    period(i * 4 + (lo + step), (lo + step) % 4)
            for t in range(hi, LAST + 1):
                period(t, t % 4)

        def turns(eng, n, step, by, tail=0):
            for i in range(by):
                step(i, i)
            if n - tail > by:
                with eng.Fori(1, (n - tail) // by) as i:
                    for q in range(by):
                        step(i * by + q, q)
            for i in range(n - tail, n):
                step(i, i % by)

        def on(t, lag):
            return not isinstance(t, int) or 0 <= t + lag < NT

        def unit_on(t, k):
            return not isinstance(t, int) or 0 <= 4 * t + k < UNITS * NT

        def pair_on(t, p):
            return on(t, 2 - p)

        def one(t):
            return bass.ds(t, 1)

        banks = [ps_s[0], ps_s[1], ps_pT, ps_b, ps_t, ps_u, ps_o]
        def turned_jobs(raw, lo, dst):
            return [("t", [raw[:, lo + (4 * g + c) * P:lo + (4 * g + c + 1) * P] for c in range(4)],
                     dst[:, 4 * g:4 * g + 4].rearrange("p c d -> p (c d)")) for g in range(2)]

        def product_jobs(kind, dst):
            return [(kind, g, dst.rearrange("p (c r) d -> p c r d", r=2)[:, 4 * (g // 2):4 * (g // 2) + 4, g % 2])
                    for g in range(4)]

        jobs = [("in", [win_raw[:, c] for c in range(3)] + [wout_raw[:]], None)]
        jobs += turned_jobs(wq_raw, 0, wqT) + turned_jobs(wkv_raw, 0, wkT) + turned_jobs(wkv_raw, H * HD, wvT)
        TURNED = len(jobs)
        jobs += product_jobs("m", score_w) + product_jobs("v", value_w[:])
        BANKS = len(banks)

        def products(k):
            return range(TURNED + 2 * k, TURNED + 2 * k + 2)

        def prep_kept(at):
            return (prep_act, prep_dve)[at % 2], at // 2 + 1

        block = ctx.enter_context(nc.Block())

        N_CONST, N_GAINS = 10, 6

        @block.sync
        def _(sp):
            def load(j, q):
                sp.wait_ge(z1_done, count(j - 1))
                sp.wait_ge(c_hat_done, count(j - 1))
                sp.dma_start(x_raw[:, q:q + 1, :], x_t[one(j), :, :].rearrange("t p d -> p t d")).then_inc(x_in[q], 16)
                sp.dma_start(c_raw[S:P, q:q + 1, :],
                             ctx_t[one(j), 0, :, :].rearrange("t s d -> s t d")).then_inc(c_in[q], 16)
                sp.dma_start(c_raw[0:S, q:q + 1, :],
                             ctx_t[one(j), 1, :, :].rearrange("t s d -> s t d")).then_inc(c_in[q], 16)

            sp.dma_start(ident[:], eye).then_inc(s_ident, 16)
            sp.dma_start(wq_raw[:], w_q).then_inc(s_wq, 16)
            sp.dma_start(wkv_raw[:], w_kv).then_inc(s_wkv, 16)
            load(0, 0)
            sp.dma_start(wo_raw[:], w_o.rearrange("(c p) n -> p c n", p=P)).then_inc(s_wo, 16)
            sp.dma_start(tri[:], before).then_inc(s_const, 16)
            sp.dma_start(eids[:], expert_ids).then_inc(s_const, 16)
            sp.dma_start(rbase[:], region_base).then_inc(s_const, 16)
            sp.dma_start(rids[:], row_ids).then_inc(s_const, 16)
            sp.dma_start(tids[:], tile_ids).then_inc(s_const, 16)

            sp.wait_ge(pad_ready, 2)
            pad_rows = pad_row[:].rearrange("p (o d) -> p o d", o=1).to_broadcast([P, TB, ROW])
            sp.dma_start(x_rows[E * CAP:E * CAP + T, :].rearrange("(b p) d -> p b d", p=P), pad_rows).then_inc(pad_filled, 16)

            def period(t, c):
                p, up = c % 2, t + 2
                q = (p + 4) % 2
                if on(up, 4):
                    j = up + 4
                    m = (j - q) // 2 if isinstance(up, int) else None
                    load(j, q)

            periods(sp, period)

            sp.wait_ge(tab_ready, 1)
            for e in range(E // 2):
                at = sp.value_load(pad_i[0:1, e:e + 1], min_val=0, max_val=E * CAP - T)
                sp.dma_start(x_rows[bass.ds(at, T), :].rearrange("(b p) d -> p b d", p=P), pad_rows).then_inc(pad_filled, 16)

            AHEAD = 3

            def weights(i, q):
                e = sp.value_load(exw_i[0:1, bass.ds(i, 1)], min_val=0, max_val=E - 1)
                sp.wait_ge(f_y_ps, count(i - (W_RING - 1)))
                settle(sp)
                sp.wait_ge(f_yb_done, count(i - (W_RING - 1)))
                settle(sp)
                sp.dma_start(f_w[q].rearrange("p (o f) -> p o f", o=1),
                             expert_w[bass.ds(e, 1), :, :].rearrange("e p f -> p e f")).then_inc(fw_in[q], 16)

            def ffn(i, q):
                base = sp.value_load(base_i[0:1, bass.ds(i, 1)], min_val=0, max_val=E * CAP)
                sp.wait_ge(f_y_done, count(TB * i - TB * (RING - 1)))
                settle(sp)
                sp.wait_ge(f_id_done, count(i - (RING - 1)))
                settle(sp)
                sp.dma_start(f_x[:, q % RING], x_rows[bass.ds(base, T), :].rearrange("(b p) d -> p b d", p=P)).then_inc(f_in[q % RING], 16)
                if not isinstance(i, int) or i + AHEAD < NF:
                    weights(i + AHEAD, (q + AHEAD) % W_RING)

            sp.wait_ge(tab_ready, 2)
            for i in range(AHEAD):
                weights(i, i)
            for s in x_routed:
                sp.wait_ge(s, 16 * NT)
            sp.wait_ge(pad_filled, 16 * (E + 1))
            turns(sp, NF, ffn, W_RING, W_RING)
            for s in y_routed:
                sp.wait_ge(s, 16 * TB * (NF // RING))

            def last_in(g, q):
                sp.wait_ge(e_sum_done, count(g - (RING - 1)))
                for sl in range(2):
                    sp.dma_start(e_y[:, q, sl],
                                 y_rows[bass.ds(g * (ZT * P) + sl * N, ZT * P), :].rearrange("(c p) d -> p c d", p=P)
                                 ).then_inc(e_in[q], 16)

            turns(sp, NZ, last_in, RING)
            for q in range(2):
                sp.wait_ge(s_out[q], 16 * (NZ // 2))

        def half_count(t, p, lag, per):
            if isinstance(t, int):
                return per * ((t + lag) // 2 + 1)
            return (t + (lag - (p + lag) % 2 + 2)) * (per // 2)

        @block.gpsimd
        def _(pool):
            nc.gpsimd.memset(m_half[:], -0.5).then_inc(half_set, 1)
            nc.gpsimd.memset(eps_ln[:], EPS_LN).then_inc(half_set, 1)
            nc.gpsimd.memset(eps_l2[:], EPS_L2).then_inc(half_set, 1)
            for dst, src in ((g_ctx, ln1_g), (b_ctx, ln1_b), (g_lat, ln2_g), (b_lat, ln2_b)):
                pool.dma_start(dst[:], src.rearrange("(o d) -> o d", o=1).to_broadcast([P, D])).then_inc(s_gains, 16)
            pool.dma_start(wg_sb[:], w_g).then_inc(s_gains, 16)
            pool.dma_start(bg_sb[:], b_g.rearrange("(o d) -> o d", o=1).to_broadcast([P, E])).then_inc(s_gains, 16)

            def rstd(var, ve, rs, eps, moments, n_moments, eps_done, rstd_done, j):
                pool.wait_ge(moments, n_moments)
                nc.gpsimd.tensor_tensor(ve, var, eps[:, 0:var.shape[-1]], ALU.add).then_inc(eps_done, 1)
                pool.wait_ge(eps_done, j + 1)
                nc.gpsimd.tensor_tensor(rs, ve, m_half[:, 0:rs.shape[-1]], ALU.pow).then_inc(rstd_done, 1)

            def scale(t, k):
                n, sl = t * 4 + k, k % 2
                pool.wait_ge(inv_done, n + 1)
                pool.wait_ge(pT_ps, count(n - 1))
                nc.gpsimd.tensor_tensor(
                    probs_n[:, sl], probs[:, sl],
                    inv_sum[:, sl, :].rearrange("p (u o) -> p u o", o=1).to_broadcast([P, UP, P]),
                    ALU.mult).then_inc(p_done, 1)

            def route(j, q, sl):
                pool.wait_ge(rows_kept, j + 1)
                pool.wait_ge(rids_kept, j + 1)
                pool.wait_ge(weight_done, j + 1)
                pool.wait_ge(pos_done, j + 1)
                settle(pool)
                pool.indirect_dma_start(
                    out=x_rows, out_offset=bass.IndirectOffsetOnAxis(ap=pos_i[:, q, sl:sl + 1].bitcast(U32), axis=0),
                    in_=routed[:, q, sl], in_offset=None, bounds_check=E * CAP - 1,
                    oob_is_err=False).then_inc(x_routed[q], 16)

            def period(t, c):
                p, up = c % 2, t + 2
                p3, p2 = (p + 3) % 2, p
                for k in range(UNITS):
                    if k == 0 and on(t, -2):
                        rstd(mv_z2[:, p, 1:2], ve_z2[:, p], rs_z2[:, p], eps_ln, z2_moments, t - 1, z2_eps, z2_rstd, t - 2)
                    if on(t, 0):
                        scale(t, k)
                    if k == 0 and on(up, 3):
                        rstd(mv_in[:, p3, :, 1], ve_in[:, p3], rs_in[:, p3], eps_ln, in_moments, 2 * up + 8, in_eps, in_rstd, up + 3)
                    if k == 0 and on(up, 2):
                        rstd(mv_z1[:, p2, 1:2], ve_z1[:, p2], rs_z1[:, p2], eps_ln, z1_moments, up + 3, z1_eps, z1_rstd, up + 2)
                    if k == 1 and on(up, 2):
                        rstd(mv_x1[:, p2, 1:2], ve_x1[:, p2], rs_x1[:, p2], eps_ln, x1_moments, up + 3, x1_eps, x1_rstd, up + 2)
                    if k == 2 and on(up, 2):
                        pool.wait_ge(l_hat_done, up + 3)
                        nc.gpsimd.tensor_tensor(l_scaled[:, p2], l_hat[:, p2], g_lat[:], ALU.mult).then_inc(l_scaled_done, 1)
                        pool.wait_ge(c_hat_done, up + 3)
                        nc.gpsimd.tensor_tensor(c_scaled[:, p2], c_hat[:, p2], g_ctx[:], ALU.mult).then_inc(c_scaled_done, 1)
                        pool.wait_ge(kv_kept, count(4 * t + 4))
                        pool.wait_ge(l_scaled_done, up + 3)
                        nc.gpsimd.tensor_tensor(l_rows[:, c], l_scaled[:, p2], b_lat[:], ALU.add).then_inc(kv_done, 1)
                        pool.wait_ge(c_scaled_done, up + 3)
                        nc.gpsimd.tensor_tensor(c_rows[:, c], c_scaled[:, p2], b_ctx[:], ALU.add).then_inc(kv_done, 1)
                    if k == 2 and on(up, 3):
                        rstd(ss_qk[:, p3], se_qk[:, p3], rs_qk[:, p3], eps_l2, sq_done, 2 * up + 8, qk_eps, qk_rstd, up + 3)
                    if k == 3 and on(t, -4):
                        route(t - 4, p, 0)
                    if k == 1 and on(t, -5):
                        route(t - 5, 1 - p, 1)

            pool.wait_ge(half_set, 3)
            pool.wait_ge(s_const, 16 * N_CONST)
            pool.wait_ge(s_gains, 16 * N_GAINS)
            periods(pool, period)

            def ffn(i, q):
                pool.wait_ge(f_y_done, TB * (i + 1))
                settle(pool)
                pool.wait_ge(f_id_done, i + 1)
                for b in range(TB):
                    settle(pool)
                    pool.indirect_dma_start(
                        out=y_rows, out_offset=bass.IndirectOffsetOnAxis(ap=f_id[:, q % RING, b:b + 1].bitcast(U32), axis=0),
                        in_=f_y[:, q % RING, b], in_offset=None, bounds_check=2 * N - 1, oob_is_err=False).then_inc(y_routed[q % RING], 16)

            turns(pool, NF, ffn, W_RING)

            def last(g, q):
                if not isinstance(g, int) or g < NZ:
                    pool.wait_ge(e_in[q], (g + (RING - q)) * (32 // RING))
                    pool.wait_ge(e_z_done, count(g - 1))
                    nc.gpsimd.tensor_tensor(e_sum[:, q % 2], e_y[:, q, 0], e_y[:, q, 1], ALU.add).then_inc(e_sum_done, 1)
                if not isinstance(g, int) or g:
                    o = (q - 1) % RING
                    rstd(e_mv[:, o, :, 1], e_ve[:, o], e_rs[:, o], eps_ln, e_moments, ZT * g, e_eps, e_rstd, g - 1)

            turns(pool, NZ, last, RING)
            last(NZ, 0)

        @block.scalar
        def _(act):
            act.dma_start(win_raw[:], w_in.rearrange("(c p) d -> p c d", p=P)).then_inc(s_win, 16)
            act.dma_start(wout_raw[:], w_out).then_inc(s_win, 16)
            act.dma_start(gcol[:], ln_g.rearrange("(p o) -> p o", o=1)).then_inc(s_const, 16)
            act.dma_start(bcol[:], ln_b.rearrange("(p o) -> p o", o=1)).then_inc(s_const, 16)
            act.dma_start(cosb[:], rot_cos).then_inc(s_const, 16)
            act.dma_start(sinb[:], rot_sin).then_inc(s_const, 16)
            act.dma_start(member[:], batch_of).then_inc(s_const, 16)

            def keep_prepared(at):
                kind, _, dst = jobs[at]
                bank = banks[at % BANKS]
                act.wait_ge(prep_ps, at + 1)
                if kind == "in":
                    nc.scalar.activation(winT[:], bank[:, 0:3 * D], ACT.Copy).then_inc(win_kept, 1)
                    nc.scalar.activation(woutT[:], bank[:, 3 * D:4 * D], ACT.Copy).then_inc(prep_act, 1)
                elif kind == "t":
                    nc.scalar.activation(dst, bank[:], ACT.Copy).then_inc(prep_act, 1)
                else:
                    nc.scalar.activation(dst, bank[:].rearrange("p (c d) -> p c d", c=4), ACT.Copy,
                                         scale=QS_SCALE if kind == "m" else 1.0).then_inc(prep_act, 1)

            for at in range(0, TURNED, 2):
                keep_prepared(at)

            act.wait_ge(s_const, 16 * N_CONST)
            act.wait_ge(s_gains, 16 * N_GAINS)

            def exps(t, k):
                n, sl = t * 4 + k, k % 2
                act.wait_ge(max_done, n + 1)
                act.wait_ge(p_done, count(n - 1))
                for j in range(UP):
                    last = nc.scalar.activation(probs[:, sl, j], ps_s[sl][:, j * P:(j + 1) * P], ACT.Exp,
                                                bias=neg_max[:, sl, j:j + 1], accum_out=sums[:, sl, j:j + 1])
                last.then_inc(exp_done, 1)

            def keep_t(t, k, p):
                n = t * 4 + (k - 2)
                kk = (k - 2) % 4
                pp = p if k > 1 else (p + 1) % 2
                b, hf = kk // 2, kk % 2
                act.wait_ge(t_ps, n + 1)
                nc.scalar.activation(tT[:, pp, hf * HH:(hf + 1) * HH, b * S:(b + 1) * S],
                                     ps_t[:].rearrange("p (h q) -> p h q", q=S), ACT.Copy).then_inc(t_done, 1)

            def period(t, c):
                p, up = c % 2, t + 2
                p3, p2, p1 = (p + 3) % 2, p, (p + 1) % 2
                for k in range(UNITS):
                    if isinstance(t, int) and t == FIRST:
                        for at in products(k):
                            if at % 2 == 0:
                                keep_prepared(at)
                    if on(t, 0):
                        exps(t, k)
                    if k == 0 and unit_on(t, -2):
                        keep_t(t, 0, p)
                    if k == 0 and on(up, 2):
                        act.wait_ge(wo_ps, up + 3)
                        act.wait_ge(qk_rstd, up + 3)
                        nc.scalar.activation(attn_o[:, p2], A_O, ACT.Copy, scale=rs_qk[:, p2, 0:1]).then_inc(attn_done, 1)
                    if k == 2 and on(up, 3):
                        act.wait_ge(qkv_ps, up + 4)
                        nc.scalar.activation(qkv[:, p3], A_QKV, ACT.Copy).then_inc(qkv_done, 1)
                        for j in range(2):
                            nc.scalar.activation(sq_junk[:, j], A_QKV[:, j * D:(j + 1) * D], ACT.Square,
                                                 accum_out=ss_qk[:, p3, j:j + 1]).then_inc(sq_done, 1)
                    if pair_on(t, p):
                        h = 8 * p + 2 * k
                        act.wait_ge(u_ps, 4 * t + (9 + k))
                        nc.scalar.activation(u_sb[:, 1 - c // 2, :, h:h + 2, :].rearrange("p n h s -> p h n s"),
                                             ps_u[:].rearrange("p (h n s) -> p h n s", h=2, s=S), ACT.Copy).then_inc(u_done, 1)
                    if k == 1 and on(t, -3):
                        act.wait_ge(lmax_done, t - 2)
                        nc.scalar.activation(gexp[:, p3], logits[:, p3], ACT.Exp, bias=lmax[:, p3, 0:1],
                                             accum_out=gsum[:, p3, 0:1]).then_inc(gexp_done, 1)
                    if k == 3 and on(t, -2):
                        act.wait_ge(x2T_ps, t - 1)
                        nc.scalar.activation(x2T[:, p], B_XT, ACT.Copy).then_inc(x2T_done, 1)
                    if k and unit_on(t, k - 2):
                        keep_t(t, k, p)
                    if k == 1 and on(up, 3):
                        act.wait_ge(xT_ps, up + 4)
                        nc.scalar.activation(xnT[:, p3], A_XT, ACT.Identity, scale=gcol[:, 0:1],
                                             bias=bcol[:, 0:1]).then_inc(xnT_done, 1)
                    if k == 3 and on(up, 2):
                        act.wait_ge(kvT_ps, up + 3)
                        nc.scalar.activation(kvT[:, c, 1:3], KVT[:, 0:P].rearrange("p (b s) -> p b s", b=BT), ACT.Copy).then_inc(kvT_done, 1)
                        nc.scalar.activation(kvT[:, c, 0:4:3], KVT[:, P:2 * P].rearrange("p (b s) -> p b s", b=BT), ACT.Copy).then_inc(kvT_done, 1)

            periods(act, period)

            act.wait_ge(tab_ready, 1)
            act.wait_ge(pad_ready, 5)
            for e in range(E // 2, E):
                at = act.value_load(pad_i[0:1, e:e + 1], min_val=0, max_val=E * CAP - T)
                act.dma_start(x_rows[bass.ds(at, T), :].rearrange("(b p) d -> p b d", p=P),
                              pad_row[:].rearrange("p (o d) -> p o d", o=1).to_broadcast([P, TB, ROW])).then_inc(pad_filled, 16)

            def upper_weights(i, q):
                act.wait_ge(f_w_upper_done, i + 1)
                nc.scalar.activation(f_w1_hi[:, q % 2], f_w_upper[:, q % 2], ACT.Copy).then_inc(f_w1_hi_done, 1)

            def ffn(i, q):
                act.wait_ge(fw_in[q], (i + (W_RING - q)) * (16 // W_RING))
                for c in range(FC):
                    act.wait_ge(f_h_ps, i * (FC // 2) + (c // 2 + 1))
                    if c == 0:
                        act.wait_ge(f_y_ps, count(i - 1))
                    nc.scalar.activation(f_h[:, q % 2, c], F_H[q % 2][c // 2][:, (c % 2) * T:(c % 2 + 1) * T], ACT.Gelu,
                                         bias=f_w[q][:, B1_AT + c:B1_AT + c + 1]).then_inc(f_h_done, 1)
                    if c == 1 and (not isinstance(i, int) or i + 1 < NF):
                        upper_weights(i + 1, (q + 1) % W_RING)

            upper_weights(0, 0)
            turns(act, NF, ffn, W_RING, W_RING)

            def last(g, q):
                act.wait_ge(e_nm_done, g + 1)
                act.wait_ge(s_out[q % 2], (g - q % 2) * 8)
                for c in range(ZT):
                    nc.scalar.activation(e_out[:, q % 2, c], e_z[:, q, c], ACT.Identity, scale=e_rs[:, q, c:c + 1],
                                         bias=e_nm[:, q, c:c + 1]).then_inc(e_out_done, 1)
                act.wait_ge(e_out_done, ZT * g + ZT)
                settle(act)
                act.dma_start(out_z[bass.ds(g * ZT, ZT), :, :].rearrange("t p d -> p t d"),
                              e_out[:, q % 2]).then_inc(s_out[q % 2], 16)

            turns(act, NZ, last, RING)

        @block.vector
        def _(dve):
            nc.vector.memset(pad_row[:, 0:D + 1], 0.0).then_inc(pad_ready, 1)
            nc.vector.memset(pad_row[:, D + 1:D + 2].bitcast(I32), 2 * N).then_inc(pad_ready, 1)
            nc.vector.memset(ones[:], 1.0).then_inc(pad_ready, 1)
            nc.vector.memset(ones_row[:], 1.0).then_inc(pad_ready, 1)
            nc.vector.memset(seen[:, 0], 0.0).then_inc(seen_done, 1)
            def keep_prepared(at):
                kind, _, dst = jobs[at]
                bank = banks[at % BANKS]
                dve.wait_ge(prep_ps, at + 1)
                if kind == "t":
                    nc.vector.tensor_copy(dst, bank[:]).then_inc(prep_dve, 1)
                else:
                    nc.vector.tensor_scalar(dst, bank[:].rearrange("p (c d) -> p c d", c=4),
                                            QS_SCALE if kind == "m" else 1.0, None, ALU.mult).then_inc(prep_dve, 1)

            for at in range(1, TURNED, 2):
                keep_prepared(at)

            dve.wait_ge(s_const, 16 * N_CONST)
            dve.wait_ge(s_gains, 16 * N_GAINS)
            nc.vector.tensor_copy(tri_bf[:], tri[:]).then_inc(pad_ready, 1)

            def split_scores():
                dve.wait_ge(prep_act, (len(jobs) + 1) // 2)
                dve.wait_ge(prep_dve, len(jobs) // 2)
                upper = t_flat.rearrange("p (n d) -> p n d", d=D)[:, 0:H]
                nc.vector.tensor_scalar(upper.bitcast(I32), score_w.bitcast(I32), HI_BITS, None,
                                        ALU.bitwise_and).then_inc(upper_done, 1)
                dve.wait_ge(upper_done, 1)
                nc.vector.tensor_copy(score_hi[:], upper).then_inc(score_split, 1)
                nc.vector.tensor_tensor(score_lo[:], score_w, upper, ALU.subtract).then_inc(score_split, 1)

            def period(t, c):
                p, up = c % 2, t + 2
                p3, p2, p1 = (p + 3) % 2, p, (p + 1) % 2

                def row_max(k):
                    n, sl = t * 4 + k, k % 2
                    dve.wait_ge(s_ps, n + 1)
                    dve.wait_ge(exp_done, count(n - 1))
                    nc.vector.tensor_reduce(neg_max[:, sl], ps_s[sl][:].rearrange("p (u k) -> p u k", k=P),
                                            axis=AX.X, op=ALU.max, negate=True).then_inc(max_done, 1)

                def inverse_sum(k):
                    n, sl = t * 4 + k, k % 2
                    dve.wait_ge(exp_done, n + 1)
                    nc.vector.reciprocal(inv_sum[:, sl], sums[:, sl]).then_inc(inv_done, 1)

                def keep_pT(k):
                    m, ss = t * 4 + (k - 1), (k - 1) % 2
                    dve.wait_ge(pT_ps, m + 1)
                    dve.wait_ge(t_ps, count(m - 1))
                    nc.vector.tensor_copy(pT[:, ss], ps_pT[:]).then_inc(pT_done, 1)

                def in_sums():
                    dve.wait_ge(x_in[p3], half_count(up, p, 3, 16))
                    settle(dve)
                    nc.vector.bn_stats(st_in[:, p3, 0], x_raw[:, p3]).then_inc(in_stats, 1)
                    dve.wait_ge(c_in[p3], half_count(up, p, 3, 32))
                    settle(dve)
                    nc.vector.bn_stats(st_in[:, p3, 1], c_raw[:, p3]).then_inc(in_stats, 1)

                def in_mean(j):
                    dve.wait_ge(in_stats, 2 * up + (7 + j))
                    settle(dve)
                    nc.vector.bn_aggr(mv_in[:, p3, j], st_in[:, p3, j]).then_inc(in_moments, 1)

                def in_hats():
                    dve.wait_ge(in_rstd, up + 4)
                    nc.vector.tensor_scalar(x_hat[:, p3], x_raw[:, p3], mv_in[:, p3, 0, 0:1], rs_in[:, p3, 0:1],
                                            ALU.subtract, ALU.mult).then_inc(x_hat_done, 1)
                    nc.vector.tensor_scalar(c_hat[:, p3], c_raw[:, p3], mv_in[:, p3, 1, 0:1], rs_in[:, p3, 1:2],
                                            ALU.subtract, ALU.mult).then_inc(c_hat_done, 1)

                qk = qkv[:, p3, 0:2 * D].rearrange("p (w d) -> p w d", w=2)[:, :, 0:ROT]

                def rot_turn():
                    pairs = qk.rearrange("p w (i two) -> p w i two", two=2)
                    trn = turned[:, p3].rearrange("p w (i two) -> p w i two", two=2)
                    sn = sinb[:].rearrange("p (o i two) -> p o i two", o=1, two=2)
                    dve.wait_ge(qkv_done, up + 4)
                    for j in range(2):
                        nc.vector.tensor_tensor(trn[:, :, :, j], pairs[:, :, :, 1 - j],
                                                sn[:, :, :, j].to_broadcast([P, 2, ROT // 2]), ALU.mult).then_inc(rot_turned, 1)

                def rot_cos_part():
                    dve.wait_ge(rot_turned, 2 * up + 8)
                    nc.vector.tensor_tensor(qk, qk, cosb[:].rearrange("p (o d) -> p o d", o=1).to_broadcast([P, 2, ROT]),
                                            ALU.mult).then_inc(rot_cosed, 1)

                def rot_add():
                    dve.wait_ge(rot_cosed, up + 4)
                    nc.vector.tensor_tensor(qk, qk, turned[:, p3], ALU.add).then_inc(rot_done, 1)

                def pick_keys():
                    dve.wait_ge(qk_rstd, up + 4)
                    nc.vector.tensor_scalar(k_pick[:, p3], member[:], rs_qk[:, p3, 1:2], None, ALU.mult).then_inc(pick_done, 1)

                def kv_product():
                    dve.wait_ge(rot_done, up + 4)
                    nc.vector.tensor_tensor(kv_prod[:, p3], qkv[:, p3, D:2 * D], qkv[:, p3, 2 * D:3 * D],
                                            ALU.mult).then_inc(kvp_done, 1)

                def scale_queries():
                    dve.wait_ge(at_ps, up + 4)
                    for b in range(BT):
                        nc.vector.tensor_scalar(yT[:, p3, b * S:(b + 1) * S], A_QT[:, b * S:(b + 1) * S],
                                                A_AT[:, b:b + 1], None, ALU.mult).then_inc(yT_done, 1)

                def z1_sum():
                    dve.wait_ge(attn_done, up + 3)
                    nc.vector.scalar_tensor_tensor(z1[:, p2], x_raw[:, p2], 2.0, attn_o[:, p2], ALU.mult, ALU.add).then_inc(z1_done, 1)

                def z1_sums():
                    dve.wait_ge(z1_done, up + 3)
                    settle(dve)
                    nc.vector.bn_stats(st_z1[:, p2], z1[:, p2]).then_inc(z1_stats, 1)

                def z1_mean():
                    dve.wait_ge(z1_stats, up + 3)
                    settle(dve)
                    nc.vector.bn_aggr(mv_z1[:, p2], st_z1[:, p2]).then_inc(z1_moments, 1)

                def x1_norm():
                    dve.wait_ge(z1_rstd, up + 3)
                    nc.vector.tensor_scalar(x1s[:, p2], z1[:, p2], mv_z1[:, p2, 0:1], rs_z1[:, p2, 0:1],
                                            ALU.subtract, ALU.mult).then_inc(x1_done, 1)
                    nc.vector.tensor_scalar(rows[:, one(up + 2), :], z1[:, p2:p2 + 1], mv_z1[:, p2, 0:1], rs_z1[:, p2, 0:1],
                                            ALU.subtract, ALU.mult).then_inc(x1_kept, 1)

                def x1_sums():
                    dve.wait_ge(x1_done, up + 3)
                    settle(dve)
                    nc.vector.bn_stats(st_x1[:, p2], x1s[:, p2]).then_inc(x1_stats, 1)

                def x1_mean():
                    dve.wait_ge(x1_stats, up + 3)
                    settle(dve)
                    nc.vector.bn_aggr(mv_x1[:, p2], st_x1[:, p2]).then_inc(x1_moments, 1)

                def latent_norm():
                    dve.wait_ge(x1_rstd, up + 3)
                    nc.vector.tensor_scalar(l_hat[:, p2], x1s[:, p2], mv_x1[:, p2, 0:1], rs_x1[:, p2, 0:1],
                                            ALU.subtract, ALU.mult).then_inc(l_hat_done, 1)

                def keep_rows():
                    dve.wait_ge(kv_done, 2 * t + 4)
                    dve.wait_ge(t_ps, count(4 * t))
                    for b in range(BT):
                        own, other = slice(b * S, (b + 1) * S), slice((1 - b) * S, (2 - b) * S)
                        nc.vector.tensor_copy(kv_rows[own, p1, b], l_rows[own, (c + 1) % 4]).then_inc(kv_kept, 1)
                        nc.vector.tensor_copy(kv_rows[other, p1, b], c_rows[other, (c + 1) % 4]).then_inc(kv_kept, 1)

                def split_latents():
                    c3 = (c + 3) % 4
                    pair, l = c3 // 2, c3 % 2
                    whole = kvT[:, c3, 1:3].rearrange("p b s -> p (b s)")
                    dve.wait_ge(kvT_done, 2 * t + 8)
                    nc.vector.tensor_scalar(l_upper[:, l].bitcast(I32), whole.bitcast(I32), HI_BITS, None,
                                            ALU.bitwise_and).then_inc(l_upper_done, 1)
                    dve.wait_ge(l_upper_done, t + 4)
                    nc.vector.tensor_copy(lT_hi[:, pair, l], l_upper[:, l]).then_inc(lT_done, 1)
                    nc.vector.tensor_tensor(lT_lo[:, pair, l], whole, l_upper[:, l], ALU.subtract).then_inc(lT_done, 1)

                def z2_sum():
                    dve.wait_ge(o_ps, t - 1)
                    dve.wait_ge(x1_kept, t - 1)
                    nc.vector.tensor_tensor(z2[:, p:p + 1], ps_o[:, 0:D].rearrange("p (o d) -> p o d", o=1),
                                            rows[:, one(t - 2), :], ALU.add).then_inc(z2_done, 1)

                def z2_sums():
                    dve.wait_ge(z2_done, t - 1)
                    settle(dve)
                    nc.vector.bn_stats(st_z2[:, p], z2[:, p]).then_inc(z2_stats, 1)

                def z2_mean():
                    dve.wait_ge(z2_stats, t - 1)
                    settle(dve)
                    nc.vector.bn_aggr(mv_z2[:, p], st_z2[:, p]).then_inc(z2_moments, 1)

                def x2_norm():
                    dve.wait_ge(z2_rstd, t - 1)
                    dve.wait_ge(x2T_ps, count(t - 3))
                    nc.vector.tensor_scalar(x2s[:, p], z2[:, p], mv_z2[:, p, 0:1], rs_z2[:, p, 0:1],
                                            ALU.subtract, ALU.mult).then_inc(x2s_done, 1)
                    nc.vector.tensor_scalar(rows[:, one(t - 2), :], z2[:, p:p + 1], mv_z2[:, p, 0:1], rs_z2[:, p, 0:1],
                                            ALU.subtract, ALU.mult).then_inc(x2_done, 1)

                def gate_logits():
                    dve.wait_ge(gate_ps, t - 2)
                    nc.vector.tensor_tensor(logits[:, p3], B_GATE, bg_sb[:], ALU.add).then_inc(logits_done, 1)

                def gate_max():
                    dve.wait_ge(logits_done, t - 2)
                    nc.vector.tensor_reduce(lmax[:, p3], logits[:, p3], axis=AX.X, op=ALU.max, negate=True).then_inc(lmax_done, 1)

                def gate_inverse():
                    dve.wait_ge(gexp_done, t - 2)
                    nc.vector.reciprocal(ginv[:, p3], gsum[:, p3]).then_inc(ginv_done, 1)

                def gate_probs():
                    dve.wait_ge(ginv_done, t - 2)
                    nc.vector.tensor_scalar(gprob[:, p3], gexp[:, p3], ginv[:, p3, 0:1], None, ALU.mult).then_inc(gprob_done, 1)

                def gate_top():
                    dve.wait_ge(gprob_done, t - 2)
                    settle(dve)
                    nc.vector.max(top[:, p3], gprob[:, p3]).then_inc(top_done, 1)

                def gate_top_at():
                    dve.wait_ge(top_done, t - 2)
                    settle(dve)
                    nc.vector.max_index(top_at[:, p3], top[:, p3], gprob[:, p3]).then_inc(top_at_done, 1)
                    nc.vector.tensor_tensor(den[:, p3], top[:, p3, 0:1], top[:, p3, 1:2], ALU.add).then_inc(den_done, 1)

                def gate_ids():
                    dve.wait_ge(top_at_done, t - 2)
                    nc.vector.tensor_copy(top_atf[:, p3], top_at[:, p3, 0:2]).then_inc(atf_done, 1)
                    dve.wait_ge(den_done, t - 2)
                    nc.vector.scalar_tensor_tensor(den_g[:, p3], den[:, p3], 0.0, den[:, p3], ALU.is_equal,
                                                   ALU.add).then_inc(den_g_done, 1)

                def gate_picked():
                    dve.wait_ge(atf_done, t - 2)
                    nc.vector.tensor_tensor(picked[:, p3], eids[:].rearrange("p (o e) -> p o e", o=1).to_broadcast([P, 2, E]),
                                            top_atf[:, p3].rearrange("p (s o) -> p s o", o=1).to_broadcast([P, 2, E]),
                                            ALU.is_equal).then_inc(picked_done, 1)
                    dve.wait_ge(den_g_done, t - 2)
                    nc.vector.reciprocal(den_i[:, p3], den_g[:, p3]).then_inc(den_i_done, 1)

                def gate_mask():
                    dve.wait_ge(picked_done, t - 2)
                    nc.vector.tensor_tensor(mask[:, p3], picked[:, p3, 0], picked[:, p3, 1], ALU.add).then_inc(mask_done, 1)

                def seen_add():
                    dve.wait_ge(mask_done, t - 3)
                    dve.wait_ge(rank_ps, t - 4)
                    nc.vector.tensor_tensor(seen[:, 1 - p], seen[:, p], mask[:, p], ALU.add).then_inc(seen_done, 1)

                def route_rows():
                    dve.wait_ge(x_routed[p], (t - (p + 4)) * 16)
                    dve.wait_ge(den_i_done, t - 3)
                    nc.vector.tensor_scalar(routed[:, p, :, D], top[:, p, 0:2], den_i[:, p, 0:1], None,
                                            ALU.mult).then_inc(weight_done, 1)
                    dve.wait_ge(x2_done, t - 3)
                    settle(dve)
                    nc.vector.tensor_copy(routed[:, p, :, 0:D],
                                          rows[:, one(t - 4), :].to_broadcast([P, 2, D])).then_inc(rows_kept, 1)
                    nc.vector.tensor_copy(routed[:, p, :, D + 1:D + 2].bitcast(I32).rearrange("p s o -> p o s"),
                                          rids[:, one(t - 4), :]).then_inc(rids_kept, 1)

                def place_all():
                    dve.wait_ge(rank_ps, t - 3)
                    nc.vector.tensor_tensor(pos_all[:, p], B_RANK, rbase[:], ALU.add).then_inc(pos_all_done, 1)

                def place_picked():
                    dve.wait_ge(pos_all_done, t - 3)
                    nc.vector.tensor_tensor(pos_sel[:, p], picked[:, p], pos_all[:, p:p + 1].to_broadcast([P, 2, E]),
                                            ALU.mult).then_inc(pos_sel_done, 1)

                def place_sum():
                    dve.wait_ge(pos_sel_done, t - 3)
                    nc.vector.tensor_reduce(pos_f[:, p], pos_sel[:, p], axis=AX.X, op=ALU.add).then_inc(pos_f_done, 1)

                def place_int():
                    dve.wait_ge(pos_f_done, t - 3)
                    nc.vector.tensor_copy(pos_i[:, p], pos_f[:, p]).then_inc(pos_done, 1)

                if on(t, 3):
                    split_latents()
                if isinstance(t, int) and t == FIRST:
                    keep_prepared(products(0)[TURNED % 2 == 0])
                if on(t, 0):
                    row_max(0)
                if on(t, -2):
                    z2_sum()
                if on(up, 3):
                    in_sums()
                if on(t, -2):
                    z2_sums()
                if on(up, 3):
                    in_mean(0)
                    in_mean(1)
                if on(t, -2):
                    z2_mean()
                if on(t, 0):
                    inverse_sum(0)
                if unit_on(t, -1):
                    keep_pT(0)
                if on(t, -4):
                    route_rows()
                if on(up, 2):
                    z1_sum()
                if on(t, -4):
                    seen_add()
                if on(up, 2):
                    z1_sums()
                if on(up, 2):
                    z1_mean()
                if isinstance(t, int) and t == FIRST:
                    keep_prepared(products(1)[TURNED % 2 == 0])
                if on(t, 0):
                    row_max(1)
                if on(t, -3):
                    gate_logits()
                if on(t, -2):
                    x2_norm()
                if on(t, -3):
                    gate_max()
                if on(up, 3):
                    in_hats()
                if on(t, 0):
                    inverse_sum(1)
                if unit_on(t, 0):
                    keep_pT(1)
                if on(up, 2):
                    x1_norm()
                    x1_sums()
                    x1_mean()
                if isinstance(t, int) and t == FIRST:
                    keep_prepared(products(2)[TURNED % 2 == 0])
                if isinstance(t, int) and t == FIRST + 1:
                    split_scores()
                if on(t, 0):
                    row_max(2)
                if on(t, -3):
                    gate_inverse()
                if on(t, 1):
                    keep_rows()
                if on(t, -3):
                    gate_probs()
                if on(t, 0):
                    inverse_sum(2)
                if unit_on(t, 1):
                    keep_pT(2)
                if on(up, 2):
                    latent_norm()
                if on(t, -4):
                    place_all()
                if on(t, -3):
                    gate_top()
                if isinstance(t, int) and t == FIRST:
                    keep_prepared(products(3)[TURNED % 2 == 0])
                if on(t, 0):
                    row_max(3)
                if on(t, -3):
                    gate_top_at()
                if on(up, 3):
                    rot_turn()
                if on(t, -3):
                    gate_ids()
                if on(up, 3):
                    rot_cos_part()
                if on(t, -3):
                    gate_picked()
                if on(up, 3):
                    rot_add()
                if on(t, 0):
                    inverse_sum(3)
                if unit_on(t, 2):
                    keep_pT(3)
                if on(up, 3):
                    pick_keys()
                    kv_product()
                if on(t, -4):
                    place_picked()
                if on(t, -4):
                    place_sum()
                if on(t, -3):
                    gate_mask()
                if on(t, -4):
                    place_int()
                if on(up, 3):
                    scale_queries()

            periods(dve, period)

            steps = [0]

            def then(ins):
                steps[0] += 1
                ins.then_inc(tab, 1)
                dve.wait_ge(tab, steps[0])

            dve.wait_ge(cnt_ps, 1)
            dve.wait_ge(pad_ready, 5)
            then(nc.vector.tensor_scalar(cnt_up[:], B_RANK[0:1], float(T - 1), None, ALU.add))
            nc.vector.tensor_tensor(pad_f[:], B_RANK[0:1], rbase[0:1], ALU.add).then_inc(tab_base, 1)
            then(nc.vector.tensor_copy(cnt_i[:], cnt_up[:]))
            dve.wait_ge(tab_base, 1)
            nc.vector.tensor_copy(pad_i[:], pad_f[:]).then_inc(tab_ready, 1)
            then(nc.vector.tensor_scalar(nt_i[:], cnt_i[:], T.bit_length() - 1, None, ALU.arith_shift_right))
            then(nc.vector.tensor_copy(nt_f[:], nt_i[:]))
            then(nc.vector.tensor_tensor_scan(cum_nt[:], ones_row[:], nt_f[:], 0.0, ALU.mult, ALU.add))
            over_tiles = lambda ap: ap.rearrange("p (o e) -> p o e", o=1).to_broadcast([1, NF, E])
            then(nc.vector.tensor_tensor(past[:], over_tiles(cum_nt[:]),
                                         tids[:].rearrange("p (i o) -> p i o", o=1).to_broadcast([1, NF, E]), ALU.is_le))
            then(nc.vector.tensor_tensor(past_nt[:], past[:], over_tiles(nt_f[:]), ALU.mult))
            then(nc.vector.tensor_reduce(ex_f[:], past[:], axis=AX.X, op=ALU.add))
            then(nc.vector.tensor_reduce(start_f[:], past_nt[:], axis=AX.X, op=ALU.add))
            then(nc.vector.tensor_scalar(valid_f[:], ex_f[:], E - 0.5, float(T), ALU.is_lt, ALU.mult))
            then(nc.vector.tensor_tensor(blk_f[:], tids[:], start_f[:], ALU.subtract))
            then(nc.vector.tensor_tensor(blk_v[:], blk_f[:], valid_f[:], ALU.mult))
            then(nc.vector.scalar_tensor_tensor(base_f[:], ex_f[:], float(CAP), blk_v[:], ALU.mult, ALU.add))
            then(nc.vector.tensor_scalar(exw_f[:], ex_f[:], float(E - 1), None, ALU.min))
            then(nc.vector.tensor_copy(base_i[:], base_f[:]))
            nc.vector.tensor_copy(exw_i[:], exw_f[:]).then_inc(tab_ready, 1)

            def rowsT(i, q):
                dve.wait_ge(f_xT_ps, i + 1)
                dve.wait_ge(f_h_ps, count(i * (FC // 2) - FC // 2))
                nc.vector.tensor_scalar(f_x_upper[:, q % 2].bitcast(I32), F_XT[q % 2].bitcast(I32), HI_BITS, None,
                                        ALU.bitwise_and).then_inc(f_x_upper_done, 1)
                dve.wait_ge(f_x_upper_done, i + 1)
                nc.vector.tensor_copy(f_xT_hi[:, q % 2], f_x_upper[:, q % 2]).then_inc(f_xT_done, 1)
                nc.vector.tensor_tensor(f_xT_lo[:, q % 2], F_XT[q % 2], f_x_upper[:, q % 2], ALU.subtract).then_inc(f_xT_done, 1)

            def split_weights(i, q):
                dve.wait_ge(fw_in[q], (i + (W_RING - q)) * (16 // W_RING))
                dve.wait_ge(f_w1_hi_done, count(i - 1))
                dve.wait_ge(f_h_ps, count(i * (FC // 2) - FC // 2))
                nc.vector.tensor_scalar(f_w_upper[:, q % 2].bitcast(I32), f_w[q][:, 0:F].bitcast(I32), HI_BITS, None,
                                        ALU.bitwise_and).then_inc(f_w_upper_done, 1)
                dve.wait_ge(f_w_upper_done, i + 1)
                nc.vector.tensor_tensor(f_w1_lo[:, q % 2], f_w[q][:, 0:F], f_w_upper[:, q % 2], ALU.subtract).then_inc(f_w1_lo_done, 1)

            def result(i, q):
                dve.wait_ge(f_y_ps, i + 1)
                dve.wait_ge(f_y_done, count(TB * i - TB))
                nc.vector.tensor_tensor(f_yb[:, q % 2], F_Y[q % 2].rearrange("p (b d) -> p b d", d=D),
                                        f_w[q][:, B2_AT:B2_AT + D].rearrange("p (o d) -> p o d", o=1).to_broadcast([P, TB, D]),
                                        ALU.add).then_inc(f_yb_done, 1)
                dve.wait_ge(y_routed[q % RING], (i - q % RING) * (16 * TB // RING))
                nc.vector.tensor_copy(f_id[:, q % RING], f_x[:, q % RING, :, D + 1]).then_inc(f_id_done, 1)
                dve.wait_ge(f_yb_done, i + 1)
                for b in range(TB):
                    nc.vector.tensor_scalar(f_y[:, q % RING, b], f_yb[:, q % 2, b], f_x[:, q % RING, b, D:D + 1], None,
                                            ALU.mult).then_inc(f_y_done, 1)

            def ffn(i, q):
                if not isinstance(i, int) or i + 1 < NF:
                    split_weights(i + 1, (q + 1) % W_RING)
                    rowsT(i + 1, (q + 1) % W_RING)
                if not isinstance(i, int) or i:
                    result(i - 1, (q - 1) % W_RING)

            split_weights(0, 0)
            rowsT(0, 0)
            turns(dve, NF, ffn, W_RING, W_RING)
            result(NF - 1, W_RING - 1)

            def last(g, q):
                if not isinstance(g, int) or g < NZ:
                    dve.wait_ge(e_sum_done, g + 1)
                    dve.wait_ge(e_out_done, count(ZT * g - ZT * (RING - 1)))
                    nc.vector.tensor_tensor(e_z[:, q], e_sum[:, q % 2], rows[:, bass.ds(g * ZT, ZT), :], ALU.add).then_inc(e_z_done, 1)
                    dve.wait_ge(e_z_done, g + 1)
                    for c in range(ZT):
                        nc.vector.bn_stats(e_st[:, q, c], e_z[:, q, c]).then_inc(e_stats, 1)
                    for c in range(ZT):
                        dve.wait_ge(e_stats, g * ZT + (c + 1))
                        settle(dve)
                        nc.vector.bn_aggr(e_mv[:, q, c], e_st[:, q, c]).then_inc(e_moments, 1)
                if not isinstance(g, int) or g:
                    o = (q - 1) % RING
                    dve.wait_ge(e_rstd, g)
                    nc.vector.scalar_tensor_tensor(e_nm[:, o], e_mv[:, o, :, 0], -1.0, e_rs[:, o], ALU.mult, ALU.mult).then_inc(e_nm_done, 1)

            turns(dve, NZ, last, RING)
            last(NZ, 0)

        @block.tensor
        def _(pe):
            pe.wait_ge(s_ident, 16)
            pe.wait_ge(s_win, 32)
            def prepare(at):
                kind, what, _ = jobs[at]
                bank = banks[at % BANKS]
                if at == 1:
                    pe.wait_ge(s_wq, 16)
                if at == 3:
                    pe.wait_ge(s_wkv, 16)
                if at == TURNED:
                    pe.wait_ge(prep_act, (TURNED + 1) // 2)
                    pe.wait_ge(prep_dve, TURNED // 2)
                    pe.wait_ge(s_wo, 16)
                if at >= BANKS:
                    kept, n = prep_kept(at - BANKS)
                    pe.wait_ge(kept, n)
                    pe.wait_ge(win_kept, 1)
                for c in range(4):
                    o = bank[:, c * P:(c + 1) * P]
                    if kind in ("in", "t"):
                        last = nc.tensor.transpose(o, what[c], ident[:])
                        continue
                    h = 8 * (what // 2) + 2 * c + what % 2
                    e = slice((h % 2) * HD, (h % 2 + 1) * HD)
                    if kind == "m":
                        last = nc.tensor.matmul(o, wqT[e, h // 2], wkT[e, h // 2], start=True, stop=True)
                    else:
                        last = nc.tensor.matmul(o, wvT[e, h // 2], wo_raw[e, h // 2], start=True, stop=True)
                last.then_inc(prep_ps, 1)

            for at in range(TURNED):
                prepare(at)
            pe.wait_ge(pad_ready, 5)
            pe.wait_ge(s_const, 16 * N_CONST)
            pe.wait_ge(s_gains, 16 * N_GAINS)

            def score(t, k, c):
                p = c % 2
                n, sl, b, hf = t * 4 + k, k % 2, k // 2, k % 2
                if k == 0:
                    pe.wait_ge(u_done, 4 * t + (8 - 4 * p))
                    pe.wait_ge(kvT_done, 2 * t + 2)
                pe.wait_ge(exp_done, count(n - 1))
                for j in range(UP):
                    h = hf * HH + 2 * j
                    last = nc.tensor.matmul(ps_s[sl][:, j * P:(j + 1) * P], u_sb[:, c // 2, BT * p + b, h:h + 2].rearrange("p h s -> p (h s)"),
                                            kvT[:, c, 1 - b:4 - b:2], start=True, stop=True)
                last.then_inc(s_ps, 1)

            def out_part(t, k, p):
                if k == 1:
                    pe.wait_ge(t_done, 4 * t - 1)
                    pe.wait_ge(z2_done, t - 1)
                if k == 2:
                    pe.wait_ge(t_done, 4 * t)
                lo, hi = ((0, 8), (8, 12), (12, 16))[k - 1]
                for h in range(lo, hi):
                    last = nc.tensor.matmul(ps_o[:, 0:D], tT[:, (p + 1) % 2, h], value_w[:, h],
                                            start=(h == 0), stop=(h == H - 1))
                if k == 3:
                    last.then_inc(o_ps, 1)

            def turn_probs(t, k):
                m, ss = t * 4 + (k - 1), (k - 1) % 2
                pe.wait_ge(p_done, m + 1)
                pe.wait_ge(pT_done, m)
                for j in range(UP):
                    last = nc.tensor.transpose(ps_pT[:, j * P:(j + 1) * P], probs_n[:, ss, j], ident[:])
                last.then_inc(pT_ps, 1)

            def weigh(t, k, p):
                m, ss = t * 4 + (k - 2), (k - 2) % 2
                b = (k - 2) % 4 // 2
                pp = p if k > 1 else (p + 1) % 2
                pe.wait_ge(pT_done, m + 1)
                pe.wait_ge(t_done, m)
                nc.tensor.matmul(ps_t[:], kv_rows[:, pp, b], pT[:, ss], start=True, stop=True).then_inc(t_ps, 1)

            def latents_part(t, k, c):
                p, pair = c % 2, 1 - c // 2
                if k == 0:
                    pe.wait_ge(lT_done, 2 * min(t + 4, NT) if isinstance(t, int) else 2 * t + 8)
                    pe.wait_ge(kvT_done, 2 * min(t + 4, NT) if isinstance(t, int) else 2 * t + 8)
                    pe.wait_ge(score_split, 2)
                pe.wait_ge(u_done, 4 * t + (8 + k))
                l_hi = lT_hi[:, pair].rearrange("p l s -> p (l s)")
                l_lo = lT_lo[:, pair].rearrange("p l s -> p (l s)")
                for j in range(2):
                    h = 8 * p + 2 * k + j
                    u = ps_u[:, j * 2 * P:(j + 1) * 2 * P]
                    nc.tensor.matmul(u, score_hi[:, h], l_hi, start=True, stop=False)
                    nc.tensor.matmul(u, score_hi[:, h], l_lo, start=False, stop=False)
                    last = nc.tensor.matmul(u, score_lo[:, h], l_hi, start=False, stop=True)
                last.then_inc(u_ps, 1)

            def period(t, c):
                p, up = c % 2, t + 2
                p3, p2, p1 = (p + 3) % 2, p, (p + 1) % 2
                if isinstance(t, int) and t == FIRST + 1:
                    pe.wait_ge(prep_act, (len(jobs) + 1) // 2)
                    pe.wait_ge(prep_dve, len(jobs) // 2)
                for k in range(UNITS):
                    if isinstance(t, int) and t == FIRST:
                        for at in products(k):
                            prepare(at)
                    if on(t, 0):
                        score(t, k, c)
                    if k == 0:
                        if unit_on(t, -2):
                            weigh(t, 0, p)
                        if pair_on(t, p):
                            latents_part(t, 0, c)
                    if k == 2 and pair_on(t, p):
                        latents_part(t, 2, c)
                    if k and on(t, -1):
                        out_part(t, k, p)
                    if unit_on(t, k - 1):
                        turn_probs(t, k)
                    if k == 0 and on(up, 2):
                        pe.wait_ge(yT_done, 2 * up + 6)
                        nc.tensor.matmul(A_O, yT[:, p2], woutT[:], start=True, stop=True).then_inc(wo_ps, 1)
                    if k == 0 and on(t, -3):
                        pe.wait_ge(x2T_done, t - 2)
                        nc.tensor.matmul(B_GATE, x2T[:, p3], wg_sb[:], start=True, stop=True).then_inc(gate_ps, 1)
                    if k == 2 and on(t, -4):
                        pe.wait_ge(mask_done, t - 3)
                        pe.wait_ge(seen_done, t - 3)
                        pe.wait_ge(logits_done, min(t - 2, NT) if isinstance(t, int) else t - 2)
                        nc.tensor.matmul(B_RANK, ones[:], seen[:, p], start=True, stop=False)
                        nc.tensor.matmul(B_RANK, tri_bf[:], mask[:, p], start=False, stop=True).then_inc(rank_ps, 1)
                    if k == 3 and on(t, -2):
                        pe.wait_ge(x2s_done, t - 1)
                        pe.wait_ge(pos_all_done, count(t - 3))
                        nc.tensor.transpose(B_XT, x2s[:, p], ident[:]).then_inc(x2T_ps, 1)
                    if k == 2 and on(up, 3):
                        pe.wait_ge(xnT_done, up + 4)
                        nc.tensor.matmul(A_QKV, xnT[:, p3], winT[:], start=True, stop=True).then_inc(qkv_ps, 1)
                    if k:
                        if k != 2 and pair_on(t, p):
                            latents_part(t, k, c)
                        if unit_on(t, k - 2):
                            weigh(t, k, p)
                    if k == 1 and on(up, 3):
                        pe.wait_ge(x_hat_done, up + 4)
                        pe.wait_ge(attn_done, up + 3)
                        nc.tensor.transpose(A_XT, x_hat[:, p3], ident[:]).then_inc(xT_ps, 1)
                    if k == 3 and on(up, 2):
                        pe.wait_ge(kv_done, 2 * up + 6)
                        pe.wait_ge(u_done, count(4 * t + 12))
                        nc.tensor.transpose(KVT[:, 0:P], l_rows[:, c], ident[:])
                        last = nc.tensor.transpose(KVT[:, P:2 * P], c_rows[:, c], ident[:])
                        last.then_inc(kvT_ps, 1)
                    if k == 3 and on(up, 3):
                        pe.wait_ge(kvp_done, up + 4)
                        pe.wait_ge(pick_done, up + 4)
                        nc.tensor.transpose(A_QT, qkv[:, p3, 0:D], ident[:])
                        nc.tensor.matmul(A_AT, kv_prod[:, p3], k_pick[:, p3], start=True, stop=True).then_inc(at_ps, 1)

            periods(pe, period)

            pe.wait_ge(pos_all_done, NT)
            pe.wait_ge(seen_done, NT + 1)
            nc.tensor.matmul(B_RANK, ones[:], seen[:, NT % 2], start=True, stop=True).then_inc(cnt_ps, 1)
            pe.wait_ge(tab, 1)

            def rowsT(i, q):
                pe.wait_ge(f_in[q % RING], (i + (RING - q % RING)) * (16 // RING))
                pe.wait_ge(f_xT_done, count(2 * i - 2))
                for b in range(TB):
                    last = nc.tensor.transpose(F_XT[q % 2][:, b * P:(b + 1) * P], f_x[:, q % RING, b, 0:D], ident[:])
                last.then_inc(f_xT_ps, 1)

            def hidden(i, q):
                pe.wait_ge(fw_in[q], (i + (W_RING - q)) * (16 // W_RING))
                pe.wait_ge(f_xT_done, 2 * i + 2)
                pe.wait_ge(f_w1_hi_done, i + 1)
                pe.wait_ge(f_w1_lo_done, i + 1)
                pe.wait_ge(f_h_done, count(i * FC - FC))
                for c in range(FC):
                    h = F_H[q % 2][c // 2][:, (c % 2) * T:(c % 2 + 1) * T]
                    part = slice(c * P, (c + 1) * P)
                    nc.tensor.matmul(h, f_w1_hi[:, q % 2, part], f_xT_hi[:, q % 2], start=True, stop=False)
                    nc.tensor.matmul(h, f_w1_hi[:, q % 2, part], f_xT_lo[:, q % 2], start=False, stop=False)
                    done = nc.tensor.matmul(h, f_w1_lo[:, q % 2, part], f_xT_hi[:, q % 2], start=False, stop=True)
                    if c % 2:
                        done.then_inc(f_h_ps, 1)

            def result(i, q):
                pe.wait_ge(f_h_done, i * FC + FC)
                pe.wait_ge(f_yb_done, count(i - 1))
                for b in range(TB):
                    for c in range(FC):
                        last = nc.tensor.matmul(F_Y[q % 2][:, b * D:(b + 1) * D], f_h[:, q % 2, c, b * P:(b + 1) * P],
                                                f_w[q][:, W2_AT + c * D:W2_AT + (c + 1) * D], start=(c == 0), stop=(c == FC - 1))
                last.then_inc(f_y_ps, 1)

            def ffn(i, q):
                hidden(i, q)
                if not isinstance(i, int) or i + 1 < NF:
                    rowsT(i + 1, (q + 1) % W_RING)
                if not isinstance(i, int) or i:
                    result(i - 1, (q - 1) % W_RING)

            rowsT(0, 0)
            turns(pe, NF, ffn, W_RING, W_RING)
            result(NF - 1, W_RING - 1)


_ARGS = {
    "x": "x", "ctx_in": "ctx_1024", "w_in": "L0_attn_W_in", "w_out": "L0_attn_W_out", "ln_g": "L0_attn_ln_g",
    "ln_b": "L0_attn_ln_b", "ln1_g": "L0_xattn_ln1_g", "ln1_b": "L0_xattn_ln1_b", "ln2_g": "L0_xattn_ln2_g",
    "ln2_b": "L0_xattn_ln2_b", "w_q": "L0_xattn_Wq", "w_kv": "L0_xattn_Wkv", "w_o": "L0_xattn_Wo",
    "w_g": "L0_ffn_Wg", "b_g": "L0_ffn_bg",
}


def shape_constants(batches, length, width, experts):
    import numpy as np

    f32 = np.float32
    tokens, p = batches * length, 128
    rot = width // 2
    inv_freq = f32(1.0) / f32(10000.0) ** (np.arange(0, rot, 2, dtype=f32) / f32(rot))
    angle = np.repeat(np.arange(length, dtype=f32)[:, None] * inv_freq[None, :], 2, axis=-1)
    sign = np.tile(np.array([-1.0, 1.0], f32), rot // 2)
    lane = np.arange(p)
    cap = tokens + FFN_ROWS
    return {
        "rot_cos": np.tile(np.cos(angle), (p // length, 1)),
        "rot_sin": np.tile(np.sin(angle) * sign, (p // length, 1)),
        "batch_of": np.repeat(np.eye(p // length, dtype=f32), length, 0),
        "eye": np.eye(p, dtype=f32),
        "before": (lane[:, None] < lane[None, :]).astype(f32),
        "expert_ids": np.tile(np.arange(experts, dtype=f32), (p, 1)),
        "region_base": np.tile(np.arange(experts, dtype=f32) * f32(cap), (p, 1)),
        "row_ids": (lane[:, None, None] + p * np.arange(tokens // p)[None, :, None]
                    + tokens * np.arange(2)[None, None, :]).astype(np.int32),
        "tile_ids": np.arange(ffn_tiles(tokens, experts), dtype=f32)[None],
    }


def expert_rows(w1, b1, w2, b2):
    import numpy as np

    e, d, f = w1.shape
    return np.concatenate([
        w1,
        w2.reshape(e, f // d, d, d).transpose(0, 2, 1, 3).reshape(e, d, f),
        b1.reshape(e, f // d, d).transpose(0, 2, 1),
        np.broadcast_to(b2[:, None, :], (e, d, d)),
    ], axis=2)


def kernel(**inputs):
    import numpy as np
    import concourse.bacc as bacc
    from concourse.bass_utils import run_bass_kernel_spmd

    nc = bacc.Bacc("TRN2", target_bir_lowering=False, num_devices=1)
    arrays, args = {}, {}

    def give(name, a):
        a = np.ascontiguousarray(a)
        arrays[f"in_{name}"] = a
        args[name] = nc.dram_tensor(f"in_{name}", a.shape, mybir.dt.from_np(a.dtype), kind="ExternalInput").ap()

    for name, key in _ARGS.items():
        give(name, inputs[key])
    give("expert_w", expert_rows(*(np.asarray(inputs[f"L0_ffn_{n}"]) for n in ("W1", "b1", "W2", "b2"))))
    batches, length, width = arrays["in_x"].shape
    experts = arrays["in_expert_w"].shape[0]
    for name, a in shape_constants(batches, length, width, experts).items():
        give(name, a)
    tokens = batches * length
    f32 = mybir.dt.float32
    args["x_rows"] = nc.dram_tensor("x_rows", [experts * (tokens + FFN_ROWS) + FFN_ROWS, width + 2], f32, kind="Internal").ap()
    args["y_rows"] = nc.dram_tensor("y_rows", [2 * tokens, width], f32, kind="Internal").ap()
    args["out"] = nc.dram_tensor("out", [batches, length, width], f32, kind="ExternalOutput").ap()
    decoder_layer(nc, **args)
    return run_bass_kernel_spmd(nc, [arrays], core_ids=[0]).results[0]["out"]
```
